# Optimizing a Trainium2 kernel written in Bass

```python
import numpy as np
import jax
import jax.numpy as jnp

def _softmax(x, axis=-1):
    return jax.nn.softmax(x, axis=axis)

def _gelu(x):
    return jax.nn.gelu(x, approximate=True)

def _silu(x):
    return jax.nn.silu(x)

def _sigmoid(x):
    return jax.nn.sigmoid(x)

def _layernorm(x, axis=-1, eps=1e-05):
    m = jnp.mean(x, axis=axis, keepdims=True)
    v = jnp.var(x, axis=axis, keepdims=True)
    return (x - m) / jnp.sqrt(v + eps)

def _scatter_add(tgt, idx, src, axis=0):
    return tgt.at[idx].add(src)

def _segment_sum(src, seg, n):
    return jax.ops.segment_sum(src, seg, n)
kernel_name = 'mk_hybrid_d1_jaxref_r4_bd9baf'

def setup_inputs(seed: int=0):
    np.random.seed(seed)
    _w = jnp.asarray

    def _L0_attn_a_setup():
        import jax, jax.numpy as jnp
        import numpy as np
        NUM_HEADS = 16
        D_MODEL = 256
        HEAD_DIM = D_MODEL // NUM_HEADS
        EPS = 1e-06

        def _feature_map(x):
            return jax.nn.elu(x) + 1.0
        key = jax.random.key(seed)
        ks = jax.random.split(key, 9)
        B, S, D = (4, 2048, D_MODEL)
        scale = 1.0 / np.sqrt(D)
        inputs_q = jax.random.normal(ks[0], (B, S, D), dtype=jnp.float32)
        Wq = jax.random.normal(ks[1], (D, D), dtype=jnp.float32) * scale
        Wk = jax.random.normal(ks[2], (D, D), dtype=jnp.float32) * scale
        Wv = jax.random.normal(ks[3], (D, D), dtype=jnp.float32) * scale
        Wo = jax.random.normal(ks[4], (D, D), dtype=jnp.float32) * scale
        bq = jnp.zeros((D,), jnp.float32)
        bk = jnp.zeros((D,), jnp.float32)
        bv = jnp.zeros((D,), jnp.float32)
        bo = jnp.zeros((D,), jnp.float32)
        return {'inputs_q': inputs_q, 'Wq': Wq, 'bq': bq, 'Wk': Wk, 'bk': bk, 'Wv': Wv, 'bv': bv, 'Wo': Wo, 'bo': bo}
    _L0_attn_a_in = _L0_attn_a_setup()

    def _L0_attn_b_setup():
        import jax, jax.numpy as jnp
        import numpy as np
        B, CTX, DIMS, HEAD = (8, 1024, 256, 16)
        HD = DIMS // HEAD
        EPS = 1e-05
        THRESH = 0.01
        FACTOR = 0.1
        MAX_IT = 3

        def _ln(x, w):
            m = jnp.mean(x, axis=-1, keepdims=True)
            v = jnp.mean((x - m) ** 2, axis=-1, keepdims=True)
            return (x - m) * jax.lax.rsqrt(v + EPS) * w
        key = jax.random.key(seed)
        ks = jax.random.split(key, 9)
        w = lambda k, shp: jax.random.normal(k, shp, jnp.float32) * 0.02
        return {'x': jax.random.normal(ks[0], (B, CTX, DIMS), jnp.float32), 'qw': w(ks[1], (DIMS, DIMS)), 'qb': jnp.zeros((DIMS,), jnp.float32), 'kw': w(ks[2], (DIMS, DIMS)), 'vw': w(ks[3], (DIMS, DIMS)), 'vb': jnp.zeros((DIMS,), jnp.float32), 'ow': w(ks[4], (DIMS, DIMS)), 'ob': jnp.zeros((DIMS,), jnp.float32), 'lna_w': jnp.ones((DIMS,), jnp.float32), 'lnb_w': jnp.ones((DIMS,), jnp.float32), 'lnc_w': jnp.ones((HD,), jnp.float32), 'lnd_w': jnp.ones((HD,), jnp.float32), 'lqw': w(ks[5], (HD, HD)), 'lqb': jnp.zeros((HD,), jnp.float32), 'lkw': w(ks[6], (HD, HD)), 'lkb': jnp.zeros((HD,), jnp.float32), 'lvw': w(ks[7], (HD, HD)), 'lvb': jnp.zeros((HD,), jnp.float32)}
    _L0_attn_b_in = _L0_attn_b_setup()

    def _L0_ffn_setup():
        import jax, jax.numpy as jnp
        import numpy as np
        D_MODEL = 256
        EXPERT_DIM = 128
        N_EXPERTS = 8
        TOP_K = 2

        def _sq_relu(h):
            return jnp.square(jax.nn.relu(h))
        key = jax.random.key(seed)
        ks = jax.random.split(key, 6)
        s = 0.02
        x = jax.random.normal(ks[0], (2, 512, D_MODEL), dtype=jnp.float32)
        Ws1 = jax.random.normal(ks[1], (D_MODEL, EXPERT_DIM), dtype=jnp.float32) * s
        Ws2 = jax.random.normal(ks[2], (EXPERT_DIM, D_MODEL), dtype=jnp.float32) * s
        W1 = jax.random.normal(ks[3], (N_EXPERTS, D_MODEL, EXPERT_DIM), dtype=jnp.float32) * s
        W2 = jax.random.normal(ks[4], (N_EXPERTS, EXPERT_DIM, D_MODEL), dtype=jnp.float32) * s
        Wr = jax.random.normal(ks[5], (D_MODEL, N_EXPERTS), dtype=jnp.float32) * s
        return {'x': x, 'Ws1': Ws1, 'Ws2': Ws2, 'W1': W1, 'W2': W2, 'Wr': Wr}
    _L0_ffn_in = _L0_ffn_setup()
    _d = {'L0_attn_a_inputs_q': _L0_attn_a_in['inputs_q'], 'L0_attn_a_Wq': _L0_attn_a_in['Wq'], 'L0_attn_a_bq': _L0_attn_a_in['bq'], 'L0_attn_a_Wk': _L0_attn_a_in['Wk'], 'L0_attn_a_bk': _L0_attn_a_in['bk'], 'L0_attn_a_Wv': _L0_attn_a_in['Wv'], 'L0_attn_a_bv': _L0_attn_a_in['bv'], 'L0_attn_a_Wo': _L0_attn_a_in['Wo'], 'L0_attn_a_bo': _L0_attn_a_in['bo'], 'L0_attn_b_qw': _L0_attn_b_in['qw'], 'L0_attn_b_qb': _L0_attn_b_in['qb'], 'L0_attn_b_kw': _L0_attn_b_in['kw'], 'L0_attn_b_vw': _L0_attn_b_in['vw'], 'L0_attn_b_vb': _L0_attn_b_in['vb'], 'L0_attn_b_ow': _L0_attn_b_in['ow'], 'L0_attn_b_ob': _L0_attn_b_in['ob'], 'L0_attn_b_lna_w': _L0_attn_b_in['lna_w'], 'L0_attn_b_lnb_w': _L0_attn_b_in['lnb_w'], 'L0_attn_b_lnc_w': _L0_attn_b_in['lnc_w'], 'L0_attn_b_lnd_w': _L0_attn_b_in['lnd_w'], 'L0_attn_b_lqw': _L0_attn_b_in['lqw'], 'L0_attn_b_lqb': _L0_attn_b_in['lqb'], 'L0_attn_b_lkw': _L0_attn_b_in['lkw'], 'L0_attn_b_lkb': _L0_attn_b_in['lkb'], 'L0_attn_b_lvw': _L0_attn_b_in['lvw'], 'L0_attn_b_lvb': _L0_attn_b_in['lvb'], 'L0_ffn_Ws1': _L0_ffn_in['Ws1'], 'L0_ffn_Ws2': _L0_ffn_in['Ws2'], 'L0_ffn_W1': _L0_ffn_in['W1'], 'L0_ffn_W2': _L0_ffn_in['W2'], 'L0_ffn_Wr': _L0_ffn_in['Wr']}
    _x0 = _d['L0_attn_a_inputs_q']
    _d['L0_attn_a_inputs_q'] = jax.random.normal(jax.random.fold_in(jax.random.key(seed), 1), (4, 2048, 256), dtype=_x0.dtype)
    del _x0
    return _d

def reference(L0_attn_a_inputs_q, L0_attn_a_Wq, L0_attn_a_bq, L0_attn_a_Wk, L0_attn_a_bk, L0_attn_a_Wv, L0_attn_a_bv, L0_attn_a_Wo, L0_attn_a_bo, L0_attn_b_qw, L0_attn_b_qb, L0_attn_b_kw, L0_attn_b_vw, L0_attn_b_vb, L0_attn_b_ow, L0_attn_b_ob, L0_attn_b_lna_w, L0_attn_b_lnb_w, L0_attn_b_lnc_w, L0_attn_b_lnd_w, L0_attn_b_lqw, L0_attn_b_lqb, L0_attn_b_lkw, L0_attn_b_lkb, L0_attn_b_lvw, L0_attn_b_lvb, L0_ffn_Ws1, L0_ffn_Ws2, L0_ffn_W1, L0_ffn_W2, L0_ffn_Wr):

    def _L0_attn_a_ref(inputs_q, Wq, bq, Wk, bk, Wv, bv, Wo, bo):
        import jax, jax.numpy as jnp
        import numpy as np
        NUM_HEADS = 16
        D_MODEL = 256
        HEAD_DIM = D_MODEL // NUM_HEADS
        EPS = 1e-06

        def _feature_map(x):
            return jax.nn.elu(x) + 1.0
        B, S, D = inputs_q.shape
        H, Dh = (NUM_HEADS, HEAD_DIM)
        q = (inputs_q @ Wq + bq).reshape(B, S, H, Dh)
        k = (inputs_q @ Wk + bk).reshape(B, S, H, Dh)
        v = (inputs_q @ Wv + bv).reshape(B, S, H, Dh)
        q = _feature_map(q)
        k = _feature_map(k)
        kv = jnp.einsum('bkhd,bkhm->bhdm', k, v)
        out = jnp.einsum('bqhd,bhdm->bqhm', q, kv)
        normalizer = jnp.einsum('bqhd,bkhd->bqh', q, k)
        normalizer = jnp.maximum(normalizer, EPS)
        out = out / normalizer[..., None]
        out = out.reshape(B, S, D)
        return out @ Wo + bo

    def _L0_attn_b_ref(x, qw, qb, kw, vw, vb, ow, ob, lna_w, lnb_w, lnc_w, lnd_w, lqw, lqb, lkw, lkb, lvw, lvb):
        import jax, jax.numpy as jnp
        import numpy as np
        B, CTX, DIMS, HEAD = (8, 1024, 256, 16)
        HD = DIMS // HEAD
        EPS = 1e-05
        THRESH = 0.01
        FACTOR = 0.1
        MAX_IT = 3

        def _ln(x, w):
            m = jnp.mean(x, axis=-1, keepdims=True)
            v = jnp.mean((x - m) ** 2, axis=-1, keepdims=True)
            return (x - m) * jax.lax.rsqrt(v + EPS) * w
        b, ctx, dims = x.shape
        q = _ln(x, lna_w) @ qw.T + qb
        xb = _ln(x, lnb_w)
        k = xb @ kw.T
        v = xb @ vw.T + vb
        split = lambda t: t.reshape(b, ctx, HEAD, HD).transpose(0, 2, 1, 3)
        query, key_t, value = (split(q), split(k), split(v))
        eff = min(ctx, HEAD)
        kn = _ln(key_t[:, :, :eff, :] @ lkw.T + lkb, lnd_w)
        vi = value[:, :, :eff, :] @ lvw.T + lvb
        scale = 1.0 / np.sqrt(HD)

        def step(qcur):
            qn = _ln(qcur[:, :, :eff, :] @ lqw.T + lqb, lnc_w)
            logits = jnp.einsum('bhqd,bhkd->bhqk', qn, kn) * scale
            attn = jax.nn.softmax(logits, axis=-1) @ vi
            return jnp.zeros_like(qcur).at[:, :, :eff, :].set(attn)
        prev = jnp.zeros_like(query)
        attn_out = jnp.zeros_like(query)
        qcur = query
        done = jnp.asarray(False)
        for it in range(MAX_IT):
            iter_out = step(qcur)
            diff = jnp.mean(jnp.abs(iter_out - prev))
            brk = (diff < THRESH + FACTOR * diff) & jnp.asarray(it > 0) & ~done
            attn_out = jnp.where(done, attn_out, iter_out)
            prev = jnp.where(done, prev, iter_out)
            qcur = jnp.where(done | brk, qcur, qcur + iter_out)
            done = done | brk
        out = attn_out.transpose(0, 2, 1, 3).reshape(b, ctx, dims)
        return out @ ow.T + ob

    def _L0_ffn_ref(x, Ws1, Ws2, W1, W2, Wr):
        import jax, jax.numpy as jnp
        import numpy as np
        D_MODEL = 256
        EXPERT_DIM = 128
        N_EXPERTS = 8
        TOP_K = 2

        def _sq_relu(h):
            return jnp.square(jax.nn.relu(h))
        shape = x.shape
        xf = x.reshape(-1, D_MODEL)
        out_shared = _sq_relu(xf @ Ws1) @ Ws2
        logits = xf @ Wr
        top_vals, top_idx = jax.lax.top_k(logits, TOP_K)
        rw = jax.nn.softmax(top_vals.astype(jnp.float32), axis=-1).astype(x.dtype)
        onehot = jax.nn.one_hot(top_idx, N_EXPERTS, dtype=x.dtype)
        prob = jnp.einsum('tk,tke->te', rw, onehot)
        prob = jnp.trunc(prob)
        h = _sq_relu(jnp.einsum('td,edf->tef', xf, W1))
        y = jnp.einsum('tef,efd->ted', h, W2)
        out_routed = jnp.einsum('ted,te->td', y, prob)
        return (out_shared + out_routed).reshape(shape)
    x = L0_attn_a_inputs_q
    x = x + _L0_attn_a_ref(_layernorm(x, axis=-1), L0_attn_a_Wq, L0_attn_a_bq, L0_attn_a_Wk, L0_attn_a_bk, L0_attn_a_Wv, L0_attn_a_bv, L0_attn_a_Wo, L0_attn_a_bo)
    x = x + _L0_ffn_ref(_layernorm(x, axis=-1), L0_ffn_Ws1, L0_ffn_Ws2, L0_ffn_W1, L0_ffn_W2, L0_ffn_Wr)
    x = x + _L0_attn_b_ref(_layernorm(x, axis=-1), L0_attn_b_qw, L0_attn_b_qb, L0_attn_b_kw, L0_attn_b_vw, L0_attn_b_vb, L0_attn_b_ow, L0_attn_b_ob, L0_attn_b_lna_w, L0_attn_b_lnb_w, L0_attn_b_lnc_w, L0_attn_b_lnd_w, L0_attn_b_lqw, L0_attn_b_lqb, L0_attn_b_lkw, L0_attn_b_lkb, L0_attn_b_lvw, L0_attn_b_lvb)
    x = x + _L0_ffn_ref(_layernorm(x, axis=-1), L0_ffn_Ws1, L0_ffn_Ws2, L0_ffn_W1, L0_ffn_W2, L0_ffn_Wr)
    return x

_drawn_inputs = setup_inputs


def setup_inputs(seed=0):
    import zlib

    import numpy as np

    out = dict(_drawn_inputs(seed))
    spreads = {'L0_attn_a_bq': (0.0, 0.8),
     'L0_attn_a_bk': (0.0, 0.8),
     'L0_attn_a_bv': (0.0, 0.1),
     'L0_attn_a_bo': (0.0, 0.1),
     'L0_attn_b_qb': (0.0, 0.8),
     'L0_attn_b_vb': (0.0, 0.8),
     'L0_attn_b_ob': (0.0, 0.1),
     'L0_attn_b_lna_w': (1.0, 0.6),
     'L0_attn_b_lnb_w': (1.0, 0.6),
     'L0_attn_b_lnc_w': (1.0, 0.6),
     'L0_attn_b_lnd_w': (1.0, 0.6),
     'L0_attn_b_lqb': (0.0, 0.8),
     'L0_attn_b_lkb': (0.0, 0.8),
     'L0_attn_b_lvb': (0.0, 0.8)}
    factors = {'L0_attn_a_Wq': 8.0,
     'L0_attn_a_Wk': 4.072,
     'L0_attn_b_qw': 8.0,
     'L0_attn_b_kw': 8.0,
     'L0_attn_b_vw': 8.0,
     'L0_attn_b_ow': 8.0,
     'L0_attn_b_lqw': 8.0,
     'L0_attn_b_lkw': 8.0,
     'L0_attn_b_lvw': 8.0}
    for name, (base, spread) in spreads.items():
        noise = np.random.default_rng([zlib.crc32(name.encode()), seed]).standard_normal(out[name].shape)
        drawn = base * np.exp(spread * noise) if base else spread * noise
        out[name] = jnp.asarray(drawn.astype(out[name].dtype))
    for name, factor in factors.items():
        out[name] = (out[name] * factor).astype(out[name].dtype)
    return out
```

```python
from contextlib import ExitStack

import concourse.bass as bass
from concourse import mybir

F32 = mybir.dt.float32
F32R = mybir.dt.float32r
BF16 = mybir.dt.bfloat16
I32 = mybir.dt.int32
ALU = mybir.AluOpType
ACT = mybir.ActivationFunctionType
AX = mybir.AxisListType.X

P = 128
B, S, D = 4, 2048, 256
C = D // P
H, HD = 16, 16
HC = H // C
T = 4
GT = T * P
G = S // GT
NG = B * G
F = 128
NE = 8
KVW = P + HC
LN_EPS = 1e-5
NORM_EPS = 1e-6
SPT = 16
SP = B * SPT
ITERS = 3
THRESH, FACTOR = 0.01, 0.1
WR_NORM2_BOUND = (16.0 / (2.0 * D ** 0.5)) ** 2


def ge(eng, sem, value):
    if isinstance(value, int) and value <= 0:
        return
    eng.wait_ge(sem, value)


def hybrid_kernel(nc, x_in, Wq, bq, Wk, bk, Wv, bv, Wo, bo, qw, qb, kw, vw, vb, ow, ob,
                  lna_w, lnb_w, lnc_w, lnd_w, lqw, lqb, lkw, lkb, lvw, lvb,
                  Ws1, Ws2, W1, W2, Wr, out):
    x_dram = x_in.rearrange("b (g t p) d -> (b g) p t d", t=T, p=P)
    out_dram = out.rearrange("b (g t p) d -> (b g) p t d", t=T, p=P)

    def rows(w):
        return w.rearrange("(c p) n -> p c n", p=P)

    def row(v):
        return v.rearrange("(o n) -> o n", o=1)

    with ExitStack() as ctx:
        def sb(name, shape, dt=F32):
            return ctx.enter_context(nc.sbuf_tensor(name, shape, dt))

        def ps(name):
            return ctx.enter_context(nc.psum_tensor(name, [P, 2, 512], F32))

        def sem(name):
            return ctx.enter_context(nc.semaphore(name))

        x_all = sb("x_all", [P, NG * T, D])
        q_all = sb("q_all", [P, NG * C, GT])
        kv_all = sb("kv_all", [P, B * C, KVW])
        ident = sb("ident", [P, P])
        head_mask = sb("head_mask", [P, HC])
        ones_row = sb("ones_row", [P, GT], BF16)
        bias3 = sb("bias3", [P, 2 * D], BF16)
        bv_rows, bo_rows, ob_rows = [sb(n, [P, D]) for n in ("bv_rows", "bo_rows", "ob_rows")]
        wv = sb("wv", [P, C, D])
        wo = sb("wo", [P, C, D])
        ws1 = sb("ws1", [P, C, F])
        ws2 = sb("ws2", [P, D])
        wr = sb("wr", [P, C, NE])
        wq_hi, wq_lo = sb("wq_hi", [P, C, D], F32R), sb("wq_lo", [P, C, D], F32R)
        wk_hi, wk_lo = sb("wk_hi", [P, C, D], F32R), sb("wk_lo", [P, C, D], F32R)
        routed_flag = sb("routed_flag", [1, 1], I32)
        wr_tmp = sb("wr_tmp", [P, C * NE])
        wr_max = sb("wr_max", [1, 4])
        ones_f = sb("ones_f", [P, P])
        kv_tmp = sb("kv_tmp", [P, C, P])
        minus_half = sb("minus_half", [P, H])
        minus_one = sb("minus_one", [P, 1])
        ln_bn = sb("ln_bn", [P, 2, T, 6])
        ln_mv = sb("ln_mv", [P, 2, T, 2])
        ln_rstd = sb("ln_rstd", [P, 2, T])
        ln_shift = sb("ln_shift", [P, 2, T])
        norm_sb = sb("norm_sb", [P, T * C, HC])
        norm_inv = sb("norm_inv", [P, T * C, HC])
        g_sb = sb("g_sb", [P, C, D + 1])
        g_t = sb("g_t", [P, C, D])
        probs = sb("probs", [P, NE, T])
        r_lg = sb("r_lg", [P, T, NE])
        r_top = sb("r_top", [P, T, 8])
        r_gap = sb("r_gap", [P, 4, T])

        SCR = 10 * 1024
        scratch = sb("scratch", [P, SCR])
        used = [0]

        def part(n):
            a = scratch[:, used[0]:used[0] + n]
            used[0] += n
            assert used[0] <= SCR
            return a

        xn = [part(T * (D + 1)).rearrange("p (t d) -> p t d", t=T) for _ in range(2)]
        k_tok = part(T * D).rearrange("p (t d) -> p t d", t=T)
        exp_kq = part(T * D)
        exp_k = exp_kq.rearrange("p (t d) -> p t d", t=T)
        exp_q = exp_kq.rearrange("p (c n) -> p c n", c=C)
        wq_raw = part(C * D).rearrange("p (c n) -> p c n", c=C)
        wk_raw = part(C * D).rearrange("p (c n) -> p c n", c=C)
        bias_rows = part(2 * D)
        bpart = part(2 * D).bitcast(BF16).rearrange("p (k n) -> p k n", k=2)
        used[0] = 0
        q_cur = [part(C * GT).rearrange("p (c n) -> p c n", c=C) for _ in range(2)]
        o_tok = part(T * D).rearrange("p (k n) -> p k n", k=T * C)
        o_t = part(C * GT).rearrange("p (c n) -> p c n", c=C)
        y2 = part(T * D).rearrange("p (t d) -> p t d", t=T)
        y3 = part(T * D).rearrange("p (t d) -> p t d", t=T)
        x2t = part(C * GT).rearrange("p (c n) -> p c n", c=C)
        x3t = part(C * GT).rearrange("p (c n) -> p c n", c=C)
        h2, h3 = part(GT), part(GT)
        x_out = part(T * D).rearrange("p (t d) -> p t d", t=T)
        xt_hi, xt_lo = sb("xt_hi", [P, C, GT], F32R), sb("xt_lo", [P, C, GT], F32R)

        PT, PA, PB, PG = ps("PT"), ps("PA"), ps("PB"), ps("PG")

        w1e, w2e = g_t[:, 0, :].rearrange("p (c f) -> p c f", c=C), g_t[:, 1, :]

        qf = q_all[:, :, :].rearrange("p k n -> p (k n)")
        sused = [0]

        def spart(n, p=P):
            a = qf[0:p, sused[0]:sused[0] + n]
            sused[0] += n
            assert sused[0] <= NG * C * GT
            return a

        raw4 = [spart(C * D).rearrange("p (c n) -> p c n", c=C) for _ in range(4)]
        w4t = [spart(C * D).rearrange("p (c n) -> p c n", c=C) for _ in range(4)]
        l_rows = [spart(HD) for _ in range(3)]
        l_blk = [spart(P) for _ in range(3)]
        l_bdt = [spart(P) for _ in range(3)]
        qb_col, vb_col = spart(C), spart(C)
        ob_b, lna_b, lnb_b = [spart(D, SP) for _ in range(3)]
        lqb_b, lkb_b, lvb_b, lnc_b, lnd_b = [spart(HD, SP) for _ in range(5)]
        xs, zs, zz, za, zb = [spart(D, SP) for _ in range(5)]
        s_bn, s_mv, s_rs = spart(6, SP), spart(2, SP), spart(4, SP)
        za_t, zb_t, qcur_t, k_t, v_t, kn_t, qn_t = [spart(C * SP).rearrange("p (c n) -> p c n", c=C) for _ in range(7)]
        vi = spart(D, SP)
        lin, cen, sq16, kn, qn = [spart(D, SP) for _ in range(5)]
        st16 = [spart(H, SP) for _ in range(4)]
        kn_mask = [spart(HC * SP) for _ in range(C)]
        neg_mask = spart(SP, SP)
        batch_mask = spart(SP, SP)
        lg = spart(H * SP, SP)
        pr = spart(H * SP, SP)
        pr_t = spart(H * SP, SP)
        mx16, sum16, inv16 = [spart(H, SP) for _ in range(3)]
        outs = [spart(D, SP) for _ in range(ITERS)]
        att, dif, tmpd = [spart(D, SP) for _ in range(3)]
        dsum = spart(8, P)
        att_t = spart(C * SP).rearrange("p (c n) -> p c n", c=C)
        ys = spart(D, SP)
        xs_t = spart(C * SP).rearrange("p (c n) -> p c n", c=C)
        h_s = spart(SP)
        x_s_out = spart(D, SP)

        w_loaded = sem("w_loaded")
        w2_loaded = sem("w2_loaded")
        wr_loaded = sem("wr_loaded")
        bias_loaded = sem("bias_loaded")
        consts = sem("consts")
        pool_setup = sem("pool_setup")
        setup_dve = sem("setup_dve")
        w_split = sem("w_split")
        bias_ready = sem("bias_ready")
        wr_sq, wr_sum, flag_ready = sem("wr_sq"), sem("wr_sum"), sem("flag_ready")
        x_loaded = [sem(f"x_loaded{g}") for g in range(G)]
        bn1, stat1, pow1, rstd1, norm1 = [sem(n) for n in ("bn1", "stat1", "pow1", "rstd1", "norm1")]
        bn2, stat2, pow2, rstd2, norm2 = [sem(n) for n in ("bn2", "stat2", "pow2", "rstd2", "norm2")]
        bn3, stat3, pow3, rstd3, norm3 = [sem(n) for n in ("bn3", "stat3", "pow3", "rstd3", "norm3")]
        t1_mm, t1_hi, t1_lo = sem("t1_mm"), sem("t1_hi"), sem("t1_lo")
        k_mm, k_exp, k_done = sem("k_mm"), sem("k_exp"), sem("k_done")
        q_mm, q_exp, q_done = sem("q_mm"), sem("q_exp"), sem("q_done")
        g_mm, g_copied, gt_mm, gt_copied, kv_mm, kv_step, kv_done = [
            sem(n) for n in ("g_mm", "g_copied", "gt_mm", "gt_copied", "kv_mm", "kv_step", "kv_done")]
        q_copied, o_mm, o_max, o_inv, o_done = [sem(n) for n in ("q_copied", "o_mm", "o_max", "o_inv", "o_done")]
        ot_mm, ot_done, w_mm, w_added = [sem(n) for n in ("ot_mm", "ot_done", "w_mm", "w_added")]
        t2_mm, t2_done, f1_mm, f1_relu, f1_sq, f2_mm, f2_added = [
            sem(n) for n in ("t2_mm", "t2_done", "f1_mm", "f1_relu", "f1_sq", "f2_mm", "f2_added")]
        t3_mm, t3_done, f3_mm, f3_relu, f3_sq, f4_mm, f4_added = [
            sem(n) for n in ("t3_mm", "t3_done", "f3_mm", "f3_relu", "f3_sq", "f4_mm", "f4_added")]
        stored = sem("stored")
        bo_added, ob_added = sem("bo_added"), sem("ob_added")
        r_logits, r_step, r_gap_ready, r_exp, r_turn, r_w, r_hid, r_relu, r_sq, r_y = [
            sem(n) for n in ("r_logits", "r_step", "r_gap_ready", "r_exp", "r_turn", "r_w", "r_hid", "r_relu", "r_sq", "r_y")]
        c_link = sem("c_link")
        c_pool = sem("c_pool")
        (c_wts, c_vecs, c_xs, c_out, c_wt, c_wt_sb, c_blk, c_lt, c_lt_sb, c_stat, c_rstd, c_z, c_zt, c_zt_sb,
         c_qkv, c_qkv_sb, c_klin, c_kn, c_knt, c_kmask, c_qlin, c_var, c_rstd16, c_qn, c_qnt, c_qnt_sb, c_logit,
         c_lg, c_pr, c_prt, c_prt_sb, c_pv, c_outs, c_outt, c_qcur, c_dsum, c_diff, c_att, c_att_t, c_att_t_sb,
         c_proj, c_hid, c_relu, c_sq, c_ffn, c_final) = [sem(f"c_{n}") for n in (
             "wts", "vecs", "xs", "out", "wt", "wt_sb", "blk", "lt", "lt_sb", "stat", "rstd", "z", "zt", "zt_sb",
             "qkv", "qkv_sb", "klin", "kn", "knt", "kmask", "qlin", "var", "rstd16", "qn", "qnt", "qnt_sb", "logit",
             "lg", "pr", "prt", "prt_sb", "pv", "outs", "outt", "qcur", "dsum", "diff", "att", "att_t", "att_t_sb",
             "proj", "hid", "relu", "sq", "ffn", "final")]

        waits_passed = {"sp": sem("sp_waits_passed"), "act": sem("act_waits_passed"),
                        "dve": sem("dve_waits_passed"), "pool": sem("pool_waits_passed")}

        def ge_apart(eng, name, sem_, value):
            ge(eng, sem_, value)
            if not isinstance(value, int):
                eng.sem_inc(waits_passed[name], 1)

        block = ctx.enter_context(nc.Block())

        def four(pair):
            return pair[:, :, :].rearrange("p b (t d) -> p (b t) d", d=D)

        def x_group(n):
            return x_all[:, bass.ds(n * T, T), :]

        def x_tile(n, t):
            return x_all[:, bass.ds(n * T + t, 1), :]

        def lagged(g, b, back):
            k = b - back
            gj, bj = g + k // B, k % B
            return gj * B + bj, bj * G + gj, bj

        def runs(j):
            return not isinstance(j, int) or 0 <= j < NG

        def routed_ordinal(g, b, second):
            i = g * B + b
            if not isinstance(i, int):
                return i * 2 - 4 + second
            f4, f2 = min(max(i - 3, 0), NG), min(max(i - 1, 0), NG)
            return f4 + f2 + (1 if second and 0 <= i - 3 < NG else 0)

        def per_head(ap, k, p=P):
            return ap.rearrange("p (a h o) -> p a h o", a=k, o=1).to_broadcast([p, k, HC, HD])

        @block.sync
        def _(sp):
            sp.dma_start(x_all[:, 0:T, :], x_dram[0]).then_inc(x_loaded[0], 16)
            for dst, w in ((wq_raw, Wq), (wk_raw, Wk)):
                sp.dma_start(dst, rows(w)).then_inc(w_loaded, 16)
            for i, v in enumerate((bq, bk)):
                sp.dma_start(bias_rows[0:3, i * D:(i + 1) * D], row(v).to_broadcast([3, D])).then_inc(bias_loaded, 16)
            sp.dma_start(wr[:, :, :], rows(Wr)).then_inc(wr_loaded, 16)
            for g in range(1, G):
                sp.dma_start(x_all[:, g * T:(g + 1) * T, :], x_dram[g]).then_inc(x_loaded[g], 16)
            for dst, w in ((wv[:, :, :], rows(Wv)), (wo[:, :, :], rows(Wo)),
                           (ws1[:, :, :], rows(Ws1)), (ws2[:, :], Ws2), (bv_rows[:, :], row(bv).to_broadcast([P, D])),
                           (bo_rows[:, :], row(bo).to_broadcast([P, D])), (ob_rows[:, :], row(ob).to_broadcast([P, D]))):
                sp.dma_start(dst, w).then_inc(w2_loaded, 16)
            with sp.Fori(1, B) as b:
                for g in range(G):
                    n = b * G + g
                    sp.wait_ge(stat1, T * (n - G + 1))
                    sp.dma_start(x_group(n), x_dram[bass.ds(n, 1)].rearrange("o p t d -> p (o t) d")).then_inc(x_loaded[g], 16)
            sp.wait_ge(flag_ready, 1)
            routed = sp.value_load(routed_flag[0:1, 0:1], min_val=0, max_val=1)

            def load_experts(k):
                with sp.If(routed > 0):
                    with sp.Fori(0, NE) as e:
                        sp.wait_ge(r_turn, k * (NE + 1) + e + 1)
                        sp.dma_start(w1e[:, :, :], W1[bass.ds(e, 1)].rearrange("o (c p) f -> p (o c) f", p=P)).then_inc(r_w, 16)
                        sp.dma_start(w2e[:, :], W2[bass.ds(e, 1)].rearrange("o f d -> f (o d)")).then_inc(r_w, 16)
                    ge_apart(sp, "sp", r_turn, (k + 1) * (NE + 1))

            def step(g, b):
                u, n, bu = lagged(g, b, 3)
                if runs(u):
                    load_experts(routed_ordinal(g, b, 0))
                    sp.wait_ge(f4_added, u + 1)
                    sp.dma_start(out_dram[bass.ds(n, 1)].rearrange("o p t d -> p (o t) d"),
                                 x_out).then_inc(stored, 16)
                if runs(lagged(g, b, 1)[0]):
                    load_experts(routed_ordinal(g, b, 1))

            for b in range(B):
                step(0, b)
            with sp.Fori(1, G) as g:
                for b in range(B):
                    step(g, b)
            for b in range(3):
                step(G, b)

            sp.wait_ge(q_copied, NG)
            for dst, w in zip(raw4, (qw, kw, vw, ow)):
                sp.dma_start(dst, rows(w)).then_inc(c_wts, 16)
            for dst, w in zip(l_rows, (lqw, lkw, lvw)):
                for h in range(HC):
                    sp.dma_start(dst[h * HD:(h + 1) * HD, :], w).then_inc(c_wts, 16)
            with nc.allow_non_contiguous_dma(reason="two short bias vectors, features on partitions"):
                for dst, v in ((qb_col, qb), (vb_col, vb)):
                    sp.dma_start(dst, v.rearrange("(c p) -> p c", p=P)).then_inc(c_vecs, 16)
            for dst, v in ((ob_b, ob), (lna_b, lna_w), (lnb_b, lnb_w)):
                sp.dma_start(dst, row(v).to_broadcast([SP, D])).then_inc(c_vecs, 16)
            for dst, v in ((lqb_b, lqb), (lkb_b, lkb), (lvb_b, lvb), (lnc_b, lnc_w), (lnd_b, lnd_w)):
                sp.dma_start(dst, row(v).to_broadcast([SP, HD])).then_inc(c_vecs, 16)
            sp.wait_ge(f2_added, NG)
            for b in range(B):
                sp.dma_start(xs[b * SPT:(b + 1) * SPT, :], x_all[0:SPT, b * G * T, :]).then_inc(c_xs, 16)
            load_experts(2 * NG)
            sp.wait_ge(stored, 16 * NG)
            sp.wait_ge(c_final, 1)
            for b in range(B):
                sp.dma_start(out[b, 0:SPT, :], x_s_out[b * SPT:(b + 1) * SPT, :]).then_inc(c_out, 16)
            sp.wait_ge(c_out, 16 * B)

        @block.gpsimd
        def _(pool):
            def mask(ap, pattern, lower, upper):
                for base, mult, pat in (lower, upper):
                    pool.wait_ge(pool_setup, mask.n)
                    nc.gpsimd.affine_select(out=ap, in_=ap, compare_op=ALU.is_ge, fill=0.0, base=base,
                                            pattern=[[pat, pattern]], channel_multiplier=mult).then_inc(pool_setup, 1)
                    mask.n += 1
            mask.n = 3
            nc.gpsimd.memset(ident[:, :], 1.0).then_inc(pool_setup, 1)
            nc.gpsimd.memset(head_mask[:, :], 1.0).then_inc(pool_setup, 1)
            nc.gpsimd.memset(minus_half[:, :], -0.5).then_inc(pool_setup, 1)
            mask(ident[:, :], P, (0, 1, -1), (0, -1, 1))
            mask(head_mask[:, :], HC, (0, 1, -HD), (HD - 1, -1, HD))
            nc.gpsimd.memset(ones_f[:, :], 1.0).then_inc(consts, 1)
            nc.gpsimd.memset(ones_row[:, :], 1.0).then_inc(consts, 1)
            for i in range(2):
                nc.gpsimd.memset(xn[i][:, :, D:D + 1], 1.0).then_inc(consts, 1)
            pool.wait_ge(pool_setup, mask.n)
            nc.gpsimd.tensor_copy(norm_inv[:, 0, 0:1], ident[:, 0:1]).then_inc(consts, 1)

            def rstd(slot, j, stat, powed, done, normed):
                mean, var = ln_mv[:, slot, :, 0], ln_mv[:, slot, :, 1]
                pool.wait_ge(stat, T * (j + 1))
                ge_apart(pool, "pool", normed, T * j)
                nc.gpsimd.tensor_scalar(ln_rstd[:, slot, :], var, LN_EPS, None, ALU.add).then_inc(powed, 1)
                pool.wait_ge(powed, 3 * j + 1)
                nc.gpsimd.tensor_tensor(ln_rstd[:, slot, :], ln_rstd[:, slot, :], minus_half[:, 0:T], ALU.pow).then_inc(powed, 1)
                pool.wait_ge(powed, 3 * j + 2)
                nc.gpsimd.tensor_tensor(ln_shift[:, slot, :], mean, ln_rstd[:, slot, :], ALU.mult).then_inc(powed, 1)
                ge_apart(pool, "pool", powed, 3 * j + 3)
                nc.gpsimd.tensor_scalar(ln_shift[:, slot, :], ln_shift[:, slot, :], -1.0, None, ALU.mult).then_inc(done, 1)

            def ln1(n):
                rstd(0, n, stat1, pow1, rstd1, norm1)

            def add_row(n, rows_, done):
                nc.gpsimd.tensor_tensor(x_group(n), x_group(n), rows_[:, :].rearrange("p (o d) -> p o d", o=1).to_broadcast([P, T, D]),
                                        ALU.add).then_inc(done, 1)

            def add_bo(n):
                ge_apart(pool, "pool", norm1, T * (n + 1))
                add_row(n, bo_rows, bo_added)

            ln1(0)
            pool.wait_ge(w2_loaded, 16 * 7)
            with pool.Fori(1, NG) as n:
                ln1(n)
                add_bo(n - 1)
            add_bo(NG - 1)

            pool.wait_ge(g_mm, NG)
            pool.wait_ge(q_done, NG)
            pool.wait_ge(norm1, T * NG)

            def copy_q(g, b, ahead):
                i, n, bi = lagged(g, b, -ahead)
                if runs(i):
                    ge(pool, o_mm, i - 1)
                    nc.gpsimd.tensor_copy(q_cur[bi % 2], q_all[:, bass.ds(n * C, C), :]).then_inc(q_copied, 1)

            def step(g, b):
                r, nr, _ = lagged(g, b, 1)
                if runs(r):
                    ge_apart(pool, "pool", norm2, T * (r + 1))
                    add_row(nr, ob_rows, ob_added)
                u = lagged(g, b, 2)[0]
                if runs(u):
                    rstd(1, u, stat3, pow3, rstd3, norm3)
                copy_q(g, b, 1)
                i = g * B + b
                if runs(i):
                    rstd(0, i, stat2, pow2, rstd2, norm2)

            copy_q(0, 0, 0)
            for b in range(B):
                step(0, b)
            with pool.Fori(1, G - 1) as g:
                for b in range(B):
                    step(g, b)
            for b in range(B):
                step(G - 1, b)
            for b in range(2):
                step(G, b)

            links = [0]

            def link(ins):
                ins.then_inc(c_pool, 1)
                links[0] += 1
                pool.wait_ge(c_pool, links[0])

            def chain_rstd(k):
                pool.wait_ge(c_stat, k + 1)
                link(nc.gpsimd.tensor_scalar(s_rs[:, 0:1], s_mv[:, 1:2], LN_EPS, None, ALU.add))
                nc.gpsimd.tensor_tensor(s_rs[:, 1:2], s_rs[:, 0:1], minus_half[0:SP, 0:1], ALU.pow).then_inc(c_rstd, 1)

            def chain_rstd16(k):
                pool.wait_ge(c_var, k + 1)
                link(nc.gpsimd.tensor_scalar(st16[2], st16[2], 1.0 / HD, LN_EPS, ALU.mult, ALU.add))
                nc.gpsimd.tensor_tensor(st16[3], st16[2], minus_half[0:SP, :], ALU.pow).then_inc(c_rstd16, 1)

            chain_rstd(0)
            chain_rstd(1)
            for k in range(1 + ITERS):
                chain_rstd16(k)
            chain_rstd(2)

        @block.scalar
        def _(act):
            def normalise(dst, n, slot, j, ready, done):
                ge_apart(act, "act", ready, j + 1)
                for t in range(T):
                    nc.scalar.activation(dst[:, t:t + 1, 0:D], x_tile(n, t), ACT.Identity, scale=ln_rstd[:, slot, t:t + 1],
                                         bias=ln_shift[:, slot, t:t + 1]).then_inc(done, 1)

            def ln1(n, g):
                ge_apart(act, "act", g_mm, n - 1)
                normalise(xn[g % 2], n, 0, n, rstd1, norm1)

            def t1(n, g):
                act.wait_ge(t1_mm, n + 1)
                ge(act, q_mm, n)
                nc.scalar.activation(xt_hi[:, :, :], PT[:, :, :], ACT.Copy).then_inc(t1_hi, 1)

            act.wait_ge(w_loaded, 32)
            for hi, raw in ((wq_hi, wq_raw), (wk_hi, wk_raw)):
                nc.scalar.activation(hi[:, :, :], raw, ACT.Copy).then_inc(w_split, 1)
            ln1(0, 0)
            t1(0, 0)

            def pass1(b, last):
                for g in range(G):
                    n = b * G + g
                    if not (last and g == G - 1):
                        ln1(n + 1, g + 1)
                    act.wait_ge(k_mm, n + 1)
                    ge(act, q_done, n)
                    nc.scalar.activation(exp_k, four(PB), ACT.Exp, bias=minus_one[:, 0:1]).then_inc(k_exp, 1)
                    if g == 0 and not (isinstance(b, int) and b == 0):
                        transposed_g(b - 1)
                    act.wait_ge(q_mm, n + 1)
                    act.wait_ge(k_done, n + 1)
                    nc.scalar.activation(exp_q, PA[:, :, :], ACT.Exp, bias=minus_one[:, 0:1]).then_inc(q_exp, 1)
                    if not (last and g == G - 1):
                        t1(n + 1, g + 1)

            def transposed_g(b):
                act.wait_ge(gt_mm, b + 1)
                ge(act, kv_mm, b)
                nc.scalar.activation(g_t[:, :, :], PG[:, :, 0:D], ACT.Copy).then_inc(gt_copied, 1)

            act.wait_ge(setup_dve, 1)
            pass1(0, False)
            with act.Fori(1, B - 1) as b:
                pass1(b, False)
            pass1(B - 1, True)
            transposed_g(B - 1)

            act.wait_ge(flag_ready, 1)
            routed = act.value_load(routed_flag[0:1, 0:1], min_val=0, max_val=1)

            act.wait_ge(g_mm, NG)
            act.wait_ge(q_done, NG)

            def run_experts(k, n_tok, relu):
                with act.If(routed > 0):
                    act.wait_ge(r_gap_ready, k + 1)
                    nc.scalar.activation(r_gap[:, 1, :], r_gap[:, 0, :], ACT.Exp).then_inc(r_exp, 1)
                    with act.Fori(0, NE) as e:
                        act.wait_ge(r_hid, k * NE + e + 1)
                        nc.scalar.activation(relu, PT[:, 1, 0:n_tok], ACT.Relu).then_inc(r_relu, 1)

            def step(g, b):
                i = g * B + b
                u3 = lagged(g, b, 3)[0]
                if runs(u3):
                    run_experts(routed_ordinal(g, b, 0), GT, h3)
                r = lagged(g, b, 1)[0]
                if runs(r):
                    act.wait_ge(t2_mm, r + 1)
                    ge(act, f1_mm, r)
                    for c in range(C):
                        nc.scalar.activation(x2t[:, c, :], PT[:, c, :], ACT.Copy).then_inc(t2_done, 1)
                if runs(i):
                    act.wait_ge(ot_mm, i + 1)
                    ge(act, w_mm, i)
                    nc.scalar.activation(o_t, PG[:, :, :], ACT.Copy).then_inc(ot_done, 1)
                u, nu, _ = lagged(g, b, 2)
                if runs(r):
                    act.wait_ge(f1_mm, r + 1)
                    ge(act, f2_mm, r)
                    nc.scalar.activation(h2, PA[:, 0, :], ACT.Relu).then_inc(f1_relu, 1)
                if runs(u):
                    ge(act, t3_mm, u)
                    normalise(y3, nu, 1, u, rstd3, norm3)
                    act.wait_ge(t3_mm, u + 1)
                    ge(act, f3_mm, u)
                    nc.scalar.activation(x3t, PT[:, :, :], ACT.Copy).then_inc(t3_done, 1)
                if runs(r):
                    run_experts(routed_ordinal(g, b, 1), GT, h2)
                if runs(u):
                    act.wait_ge(f3_mm, u + 1)
                    ge(act, f4_mm, u)
                    nc.scalar.activation(h3, PA[:, 1, :], ACT.Relu).then_inc(f3_relu, 1)
                if runs(i):
                    ge(act, t2_mm, i)
                    normalise(y2, lagged(g, b, 0)[1], 0, i, rstd2, norm2)

            for b in range(B):
                step(0, b)
            with act.Fori(1, G) as g:
                for b in range(B):
                    step(g, b)
            for b in range(3):
                step(G, b)

            for i, pair in enumerate((PA, PB, PT, PG)):
                act.wait_ge(c_wt, i + 1)
                nc.scalar.activation(w4t[i], pair[:, :, 0:D], ACT.Copy).then_inc(c_wt_sb, 1)
            for it in range(ITERS):
                act.wait_ge(c_qnt, it + 1)
                nc.scalar.activation(qn_t, PT[:, 1, 0:C * SP].rearrange("p (c n) -> p c n", c=C), ACT.Copy).then_inc(c_qnt_sb, 1)
                act.wait_ge(c_lg, it + 1)
                nc.scalar.activation(pr, lg, ACT.Exp).then_inc(c_pr, 1)
                act.wait_ge(c_prt, it + 1)
                nc.scalar.activation(pr_t.rearrange("p (b n) -> p b n", b=2), PG[0:SP, :, :], ACT.Copy).then_inc(c_prt_sb, 1)
            act.wait_ge(c_hid, 1)
            nc.scalar.activation(h_s, PA[:, 1, 0:SP], ACT.Relu).then_inc(c_relu, 1)
            run_experts(2 * NG, SP, h_s)

        @block.vector
        def _(dve):
            links = [0]

            def link(ins):
                ins.then_inc(c_link, 1)
                links[0] += 1
                dve.wait_ge(c_link, links[0])

            def stats(n, slot, j, bn, stat, used):
                ge_apart(dve, "dve", used, j)
                for t in range(T):
                    nc.vector.bn_stats(ln_bn[:, slot, t:t + 1, :], x_tile(n, t)).then_inc(bn, 1)
                for t in range(T):
                    ge_apart(dve, "dve", bn, T * j + t + 1)
                    nc.vector.bn_aggr(ln_mv[:, slot, t:t + 1, :], ln_bn[:, slot, t:t + 1, :]).then_inc(stat, 1)

            def ln1(n, g, b):
                dve.wait_ge(x_loaded[g % G], 16 * (b + g // G + 1))
                stats(n, 0, n, bn1, stat1, rstd1)

            def t1(n, g):
                dve.wait_ge(t1_hi, n + 1)
                ge(dve, q_mm, n)
                nc.vector.tensor_tensor(xt_lo[:, :, :], PT[:, :, :], xt_hi[:, :, :].bitcast(F32),
                                        ALU.subtract).then_inc(t1_lo, 1)

            nc.vector.memset(minus_one[:, :], -1.0).then_inc(setup_dve, 1)
            nc.vector.memset(bias3[:, :], 0.0).then_inc(setup_dve, 1)
            ln1(0, 0, 0)
            for i, (lo, hi, raw) in enumerate(((wq_lo, wq_hi, wq_raw), (wk_lo, wk_hi, wk_raw))):
                dve.wait_ge(w_split, i + 1)
                nc.vector.tensor_tensor(lo[:, :, :], raw, hi[:, :, :].bitcast(F32), ALU.subtract).then_inc(setup_dve, 1)
            dve.wait_ge(bias_loaded, 32)
            dve.wait_ge(consts, 5)
            link(nc.vector.tensor_scalar(bias_rows[0:3, 0:2 * D], bias_rows[0:3, 0:2 * D], 1.0, None, ALU.add))
            link(nc.vector.tensor_copy(bpart[0:3, 0, :], bias_rows[0:3, :]))
            link(nc.vector.tensor_tensor(bias_rows[0:3, :], bias_rows[0:3, :], bpart[0:3, 0, :], ALU.subtract))
            link(nc.vector.tensor_copy(bpart[0:3, 1, :], bias_rows[0:3, :]))
            link(nc.vector.tensor_tensor(bias_rows[0:3, :], bias_rows[0:3, :], bpart[0:3, 1, :], ALU.subtract))
            link(nc.vector.tensor_scalar(bias_rows[0:3, :], bias_rows[0:3, :], ident[0:3, 2:3], None, ALU.mult))
            link(nc.vector.scalar_tensor_tensor(bias_rows[0:3, :], bpart[0:3, 1, :], ident[0:3, 1:2], bias_rows[0:3, :], ALU.mult, ALU.add))
            nc.vector.scalar_tensor_tensor(bias3[0:3, :], bpart[0:3, 0, :], ident[0:3, 0:1], bias_rows[0:3, :],
                                           ALU.mult, ALU.add).then_inc(bias_ready, 1)
            dve.wait_ge(wr_loaded, 16)
            nc.vector.tensor_tensor(wr_tmp[:, :], wr[:, :, :].rearrange("p c e -> p (c e)"),
                                    wr[:, :, :].rearrange("p c e -> p (c e)"), ALU.mult).then_inc(wr_sq, 1)
            ln1(1, 1, 0)
            t1(0, 0)
            dve.wait_ge(wr_sum, 1)
            link(nc.vector.reduce_max(wr_max[0:1, 0:1], PG[0:1, 0, 0:NE], AX))
            link(nc.vector.tensor_scalar(wr_max[0:1, 1:2], wr_max[0:1, 0:1], WR_NORM2_BOUND, None, ALU.is_lt))
            nc.vector.tensor_scalar(routed_flag[0:1, 0:1], wr_max[0:1, 1:2], -1.0, 1.0, ALU.mult, ALU.add).then_inc(flag_ready, 1)

            def pass1(b, last):
                for g in range(G):
                    n = b * G + g
                    later_batch = not (isinstance(b, int) and b == 0)
                    if g == 0 and later_batch:
                        copy_g(b - 1)
                    dve.wait_ge(k_exp, n + 1)
                    ge(dve, g_mm, n)
                    nc.vector.scalar_tensor_tensor(k_tok, exp_k, 1.0, four(PB), ALU.min, ALU.max).then_inc(k_done, 1)
                    if not (last and g >= G - 2):
                        ln1(n + 2, g + 2, b)
                    if g == 0 and later_batch:
                        batch_kv(b - 1)
                    dve.wait_ge(q_exp, n + 1)
                    nc.vector.scalar_tensor_tensor(q_all[:, bass.ds(n * C, C), :], exp_q, 1.0, PA[:, :, :],
                                                   ALU.min, ALU.max).then_inc(q_done, 1)
                    if not (last and g == G - 1):
                        t1(n + 1, g + 1)

            def copy_g(b):
                dve.wait_ge(g_mm, (b + 1) * G)
                ge(dve, kv_done, 2 * C * b)
                ge(dve, gt_mm, b)
                nc.vector.tensor_copy(g_sb[:, :, :], PG[:, :, 0:D + 1]).then_inc(g_copied, 1)

            def batch_kv(b):
                dve.wait_ge(kv_mm, b + 1)
                for c in range(C):
                    nc.vector.scalar_tensor_tensor(kv_tmp[:, c, :], bv_rows[:, c * P:(c + 1) * P], g_sb[:, c, D:D + 1],
                                                   PG[:, c, D:D + P], ALU.mult, ALU.add).then_inc(kv_step, 1)
                for c in range(C):
                    dve.wait_ge(kv_step, C * b + c + 1)
                    dst = kv_all[:, bass.ds(b * C + c, 1), :]
                    nc.vector.tensor_tensor(dst[:, :, 0:P].rearrange("p o (h e) -> p (o h) e", e=HD),
                                            kv_tmp[:, c, :].rearrange("p (h e) -> p h e", e=HD),
                                            head_mask[:, :].rearrange("p (h o) -> p h o", o=1).to_broadcast([P, HC, HD]),
                                            ALU.mult).then_inc(kv_done, 1)
                    nc.vector.tensor_scalar(dst[:, :, P:KVW].rearrange("p o h -> p (o h)"), head_mask[:, :],
                                            g_sb[:, c, D:D + 1], None, ALU.mult).then_inc(kv_done, 1)

            pass1(0, False)
            with dve.Fori(1, B - 1) as b:
                pass1(b, False)
            pass1(B - 1, True)
            copy_g(B - 1)
            batch_kv(B - 1)

            dve.wait_ge(flag_ready, 1)
            routed = dve.value_load(routed_flag[0:1, 0:1], min_val=0, max_val=1)

            def run_experts(k, p, tiles, x_of, y, h):
                with dve.If(routed > 0):
                    dve.wait_ge(r_logits, k + 1)
                    nc.vector.tensor_copy(r_lg[0:p, 0:tiles, :], PT[0:p, 0, 0:tiles * NE].rearrange("p (t e) -> p t e", e=NE)).then_inc(r_step, 1)
                    ge_apart(dve, "dve", r_step, 4 * k + 1)
                    for t in range(tiles):
                        last = nc.vector.max(r_top[0:p, t, :], r_lg[0:p, t, :])
                    last.then_inc(r_step, 1)
                    dve.wait_ge(r_step, 4 * k + 2)
                    nc.vector.tensor_tensor(r_gap[0:p, 0, 0:tiles], r_top[0:p, 0:tiles, 1], r_top[0:p, 0:tiles, 0],
                                            ALU.subtract).then_inc(r_gap_ready, 1)
                    dve.wait_ge(r_exp, k + 1)
                    nc.vector.tensor_scalar(r_gap[0:p, 2, 0:tiles], r_gap[0:p, 1, 0:tiles], 1.0, None, ALU.add).then_inc(r_step, 1)
                    dve.wait_ge(r_step, 4 * k + 3)
                    nc.vector.tensor_scalar(r_gap[0:p, 3, 0:tiles], r_gap[0:p, 2, 0:tiles], 1.0, None, ALU.is_le).then_inc(r_step, 1)
                    dve.wait_ge(r_step, 4 * k + 4)
                    for t in range(tiles):
                        last = nc.vector.tensor_scalar(probs[0:p, :, t], r_lg[0:p, t, :], r_top[0:p, t, 0:1],
                                                       r_gap[0:p, 3, t:t + 1], ALU.is_ge, ALU.mult)
                    last.then_inc(r_turn, 1)
                    with dve.Fori(0, NE) as e:
                        dve.wait_ge(r_relu, k * NE + e + 1)
                        nc.vector.tensor_tensor(h, h, h, ALU.mult).then_inc(r_sq, 1)
                        dve.wait_ge(r_y, k * NE + e + 1)
                        dve.wait_ge(r_turn, k * (NE + 1) + e + 1)
                        for t in range(tiles):
                            x = x_of(t)
                            last = nc.vector.scalar_tensor_tensor(x, y[0:p, t:t + 1, :], probs[0:p, bass.ds(e, 1), t], x,
                                                                  ALU.mult, ALU.add)
                        last.then_inc(r_turn, 1)
                    ge_apart(dve, "dve", r_turn, (k + 1) * (NE + 1))

            dve.wait_ge(norm1, T * NG)
            dve.wait_ge(g_mm, NG)

            def step(g, b):
                i, n, _ = lagged(g, b, 0)
                r, nr, _ = lagged(g, b, 1)
                u, nu, _ = lagged(g, b, 2)
                v, nv, bv_ = lagged(g, b, 3)
                if runs(i):
                    regions = ((6, 2, PT[:, 0, 0:2 * KVW]), (0, 3, PA[:, 0, 0:3 * KVW]), (3, 3, PA[:, 1, 0:3 * KVW]))
                    dve.wait_ge(o_mm, i + 1)
                    for k0, nb, reg in regions:
                        last = nc.vector.tensor_scalar(norm_sb[:, k0:k0 + nb, :], reg.rearrange("p (k w) -> p k w", w=KVW)[:, :, P:KVW],
                                                       NORM_EPS, None, ALU.max)
                    last.then_inc(o_max, 1)
                    dve.wait_ge(o_max, i + 1)
                    nc.vector.reciprocal(norm_inv[:, :, :], norm_sb[:, :, :]).then_inc(o_inv, 1)
                    dve.wait_ge(o_inv, i + 1)
                    ge(dve, ot_mm, i)
                    for k0, nb, reg in regions:
                        nc.vector.tensor_tensor(o_tok[:, k0:k0 + nb, :].rearrange("p k (h e) -> p k h e", e=HD),
                                                reg.rearrange("p (k w) -> p k w", w=KVW)[:, :, 0:P].rearrange("p k (h e) -> p k h e", e=HD),
                                                norm_inv[:, k0:k0 + nb, :].unsqueeze(3).to_broadcast([P, nb, HC, HD]),
                                                ALU.mult).then_inc(o_done, 1)
                if runs(u):
                    stats(nu, 1, u, bn3, stat3, rstd3)
                if runs(v):
                    dve.wait_ge(f4_mm, v + 1)
                    ge(dve, stored, 16 * v)
                    nc.vector.tensor_tensor(x_out, four(PB), x_group(nv), ALU.add).then_inc(f4_added, 1)
                    ge_apart(dve, "dve", f4_added, v + 1)
                    run_experts(routed_ordinal(g, b, 0), P, T, lambda t: x_out[:, t:t + 1, :], four(PB), h3)
                if runs(r):
                    dve.wait_ge(f1_relu, r + 1)
                    nc.vector.tensor_tensor(h2, h2, h2, ALU.mult).then_inc(f1_sq, 1)
                if runs(i):
                    dve.wait_ge(w_mm, i + 1)
                    dve.wait_ge(bo_added, NG)
                    nc.vector.tensor_tensor(x_group(n), four(PB), x_group(n), ALU.add).then_inc(w_added, 1)
                    dve.wait_ge(w_added, i + 1)
                    stats(n, 0, i, bn2, stat2, rstd2)
                if runs(r):
                    dve.wait_ge(f2_mm, r + 1)
                    dve.wait_ge(ob_added, r + 1)
                    nc.vector.tensor_tensor(x_group(nr), four(PG), x_group(nr), ALU.add).then_inc(f2_added, 1)
                    ge_apart(dve, "dve", f2_added, r + 1)
                    run_experts(routed_ordinal(g, b, 1), P, T, lambda t: x_tile(nr, t), four(PG), h2)
                if runs(u):
                    dve.wait_ge(f3_relu, u + 1)
                    nc.vector.tensor_tensor(h3, h3, h3, ALU.mult).then_inc(f3_sq, 1)

            for b in range(B):
                step(0, b)
            with dve.Fori(1, G) as g:
                for b in range(B):
                    step(g, b)
            for b in range(3):
                step(G, b)

            def heads(ap):
                return ap.rearrange("p (h e) -> p h e", e=HD)

            def over_heads(ap):
                return ap.rearrange("p (o e) -> p o e", o=1).to_broadcast([SP, H, HD])

            def over_feats(ap):
                return ap.rearrange("p (h o) -> p h o", o=1).to_broadcast([SP, H, HD])

            def over_keys(ap):
                return ap.rearrange("p (h o) -> p h o", o=1).to_broadcast([SP, H, SP])

            def layernorm(dst, src, k):
                link(nc.vector.bn_stats(s_bn, src))
                nc.vector.bn_aggr(s_mv, s_bn).then_inc(c_stat, 1)
                dve.wait_ge(c_stat, k + 1)
                dve.wait_ge(c_rstd, k + 1)
                link(nc.vector.tensor_scalar(dst, src, s_mv[:, 0:1], s_rs[:, 1:2], ALU.subtract, ALU.mult))

            def layernorm16(dst, w, k):
                link(nc.vector.reduce_sum(st16[0], heads(lin), AX))
                link(nc.vector.tensor_scalar(st16[1], st16[0], 1.0 / HD, None, ALU.mult))
                link(nc.vector.tensor_tensor(heads(cen), heads(lin), over_feats(st16[1]), ALU.subtract))
                link(nc.vector.tensor_tensor(sq16, cen, cen, ALU.mult))
                nc.vector.reduce_sum(st16[2], heads(sq16), AX).then_inc(c_var, 1)
                dve.wait_ge(c_rstd16, k + 1)
                link(nc.vector.tensor_tensor(heads(cen), heads(cen), over_feats(st16[3]), ALU.mult))
                return nc.vector.tensor_tensor(heads(dst), heads(cen), over_heads(w), ALU.mult)

            dve.wait_ge(c_wts, 16 * (4 + 3 * HC))
            dve.wait_ge(c_vecs, 16 * 10)
            for rows16, blk in zip(l_rows, l_blk):
                nc.vector.tensor_tensor(blk.rearrange("p (h e) -> p h e", e=HD),
                                        rows16.rearrange("p (o e) -> p o e", o=1).to_broadcast([P, HC, HD]),
                                        head_mask[:, :].rearrange("p (h o) -> p h o", o=1).to_broadcast([P, HC, HD]),
                                        ALU.mult).then_inc(c_blk, 1)
            link(nc.vector.tensor_scalar(neg_mask.rearrange("p (b s) -> p b s", s=SPT),
                                         head_mask[0:SP, 0:B].rearrange("p (b o) -> p b o", o=1).to_broadcast([SP, B, SPT]),
                                         1.0, 1e30, ALU.subtract, ALU.mult))
            dve.wait_ge(c_xs, 16 * B)
            link(nc.vector.tensor_tensor(xs, xs, ob_b, ALU.subtract))
            layernorm(zs, xs, 0)
            layernorm(zz, zs, 1)
            nc.vector.tensor_tensor(za, zz, lna_b, ALU.mult).then_inc(c_z, 1)
            nc.vector.tensor_tensor(zb, zz, lnb_b, ALU.mult).then_inc(c_z, 1)
            dve.wait_ge(c_lt, 1)
            for i in range(3):
                nc.vector.tensor_copy(l_bdt[i], PA[:, 0, i * P:(i + 1) * P]).then_inc(c_lt_sb, 1)
            dve.wait_ge(c_zt, 1)
            nc.vector.tensor_copy(za_t, PT[:, 0, 0:C * SP].rearrange("p (c n) -> p c n", c=C)).then_inc(c_zt_sb, 1)
            nc.vector.tensor_copy(zb_t, PT[:, 0, C * SP:2 * C * SP].rearrange("p (c n) -> p c n", c=C)).then_inc(c_zt_sb, 1)
            dve.wait_ge(c_qkv, 1)
            for c in range(C):
                nc.vector.tensor_scalar(qcur_t[:, c, :], PA[:, 0, c * SP:(c + 1) * SP], qb_col[:, c:c + 1], None, ALU.add).then_inc(c_qkv_sb, 1)
                nc.vector.tensor_copy(k_t[:, c, :], PA[:, 0, (C + c) * SP:(C + c + 1) * SP]).then_inc(c_qkv_sb, 1)
                nc.vector.tensor_scalar(v_t[:, c, :], PA[:, 0, (2 * C + c) * SP:(2 * C + c + 1) * SP], vb_col[:, c:c + 1],
                                        None, ALU.add).then_inc(c_qkv_sb, 1)
            dve.wait_ge(c_klin, 1)
            link(nc.vector.tensor_tensor(heads(vi), heads(PB[0:SP, 1, 0:D]), over_heads(lvb_b), ALU.add))
            link(nc.vector.tensor_tensor(heads(lin), heads(PB[0:SP, 0, 0:D]), over_heads(lkb_b), ALU.add))
            layernorm16(kn, lnd_b, 0).then_inc(c_kn, 1)
            dve.wait_ge(c_knt, 1)
            for c in range(C):
                nc.vector.tensor_tensor(kn_mask[c].rearrange("p (h s) -> p h s", s=SP),
                                        PT[:, 0, c * SP:(c + 1) * SP].rearrange("p (o s) -> p o s", o=1).to_broadcast([P, HC, SP]),
                                        head_mask[:, :].rearrange("p (h o) -> p h o", o=1).to_broadcast([P, HC, SP]),
                                        ALU.mult).then_inc(c_kmask, 1)
            for it in range(ITERS):
                dve.wait_ge(c_qlin, it + 1)
                link(nc.vector.tensor_tensor(heads(lin), heads(PB[0:SP, 0, 0:D]), over_heads(lqb_b), ALU.add))
                layernorm16(qn, lnc_b, it + 1).then_inc(c_qn, 1)
                dve.wait_ge(c_logit, it + 1)
                lgh = lg.rearrange("p (h s) -> p h s", s=SP)
                prh = pr.rearrange("p (h s) -> p h s", s=SP)
                link(nc.vector.scalar_tensor_tensor(lgh, PA[0:SP, :, :].rearrange("p b (h s) -> p (b h) s", s=SP), HD ** -0.5,
                                                    neg_mask.rearrange("p (o s) -> p o s", o=1).to_broadcast([SP, H, SP]),
                                                    ALU.mult, ALU.add))
                link(nc.vector.reduce_max(mx16, lgh, AX))
                nc.vector.tensor_tensor(lgh, lgh, over_keys(mx16), ALU.subtract).then_inc(c_lg, 1)
                dve.wait_ge(c_pr, it + 1)
                link(nc.vector.reduce_sum(sum16, prh, AX))
                link(nc.vector.reciprocal(inv16, sum16))
                dve.wait_ge(c_pv, it + 1)
                nc.vector.tensor_tensor(heads(outs[it]), heads(PT[0:SP, 0, 0:D]), over_feats(inv16), ALU.mult).then_inc(c_outs, 1)
                dve.wait_ge(c_outs, it + 1)
                if it < ITERS - 1:
                    dve.wait_ge(c_outt, it + 1)
                    nc.vector.tensor_tensor(qcur_t, PB[:, 1, 0:C * SP].rearrange("p (c n) -> p c n", c=C), qcur_t, ALU.add).then_inc(c_qcur, 1)
                if it == 1:
                    link(nc.vector.tensor_tensor(dif, outs[1], outs[0], ALU.subtract))
                    nc.vector.tensor_reduce(dsum[0:SP, 0:1], dif, AX, ALU.add, apply_absolute_value=True).then_inc(c_dsum, 1)
            dve.wait_ge(c_diff, 1)
            link(nc.vector.tensor_scalar(dsum[0:SP, 1:2], PG[0:SP, 0, 0:1], 1.0 / (B * S * D), None, ALU.mult))
            link(nc.vector.tensor_scalar(dsum[0:SP, 2:3], dsum[0:SP, 1:2], FACTOR, THRESH, ALU.mult, ALU.add))
            link(nc.vector.tensor_tensor(dsum[0:SP, 3:4], dsum[0:SP, 1:2], dsum[0:SP, 2:3], ALU.is_lt))
            link(nc.vector.tensor_scalar(dsum[0:SP, 4:5], dsum[0:SP, 3:4], -1.0, 1.0, ALU.mult, ALU.add))
            link(nc.vector.tensor_scalar(tmpd, outs[1], dsum[0:SP, 3:4], None, ALU.mult))
            nc.vector.scalar_tensor_tensor(att, outs[2], dsum[0:SP, 4:5], tmpd, ALU.mult, ALU.add).then_inc(c_att, 1)
            dve.wait_ge(c_att_t, 1)
            nc.vector.tensor_copy(att_t, PT[:, 1, 0:C * SP].rearrange("p (c n) -> p c n", c=C)).then_inc(c_att_t_sb, 1)
            dve.wait_ge(c_proj, 1)
            link(nc.vector.tensor_tensor(tmpd, PB[0:SP, 0, 0:D], ob_b, ALU.add))
            link(nc.vector.tensor_tensor(xs, xs, tmpd, ALU.add))
            layernorm(ys, xs, 2)
            nc.vector.tensor_copy(zs, ys).then_inc(c_z, 1)
            dve.wait_ge(c_zt, 2)
            nc.vector.tensor_copy(xs_t, PT[:, 0, 0:C * SP].rearrange("p (c n) -> p c n", c=C)).then_inc(c_zt_sb, 1)
            dve.wait_ge(c_relu, 1)
            nc.vector.tensor_tensor(h_s, h_s, h_s, ALU.mult).then_inc(c_sq, 1)
            dve.wait_ge(c_ffn, 1)
            link(nc.vector.tensor_tensor(x_s_out, PB[0:SP, 1, 0:D], xs, ALU.add))
            run_experts(2 * NG, SP, 1, lambda t: x_s_out.rearrange("p (t d) -> p t d", t=1), four(PB)[:, 2:3, :], h_s)
            nc.vector.tensor_copy(dsum[0:SP, 7:8], x_s_out[:, 0:1]).then_inc(c_final, 1)

        @block.tensor
        def _(pe):
            mm = nc.tensor.matmul

            def t1(n, g):
                pe.wait_ge(norm1, T * (n + 1))
                ge(pe, t1_lo, n)
                for c in range(C):
                    for t in range(T):
                        last = nc.tensor.transpose(PT[:, c, t * P:(t + 1) * P], xn[g % 2][:, t, c * P:(c + 1) * P], ident[:, :])
                last.then_inc(t1_mm, 1)

            def column_norms():
                pe.wait_ge(wr_sq, 1)
                for c in range(C):
                    last = mm(PG[0:P, 0, 0:NE], ones_f[:, :], wr_tmp[:, c * NE:(c + 1) * NE], start=(c == 0), stop=(c == C - 1))
                last.then_inc(wr_sum, 1)

            pe.wait_ge(consts, 5)
            t1(0, 0)
            column_norms()
            pe.wait_ge(setup_dve, 4)
            pe.wait_ge(bias_ready, 1)

            def k_product(n, g):
                pe.wait_ge(t1_lo, n + 1)
                ge(pe, k_done, n)
                for t in range(T):
                    dst = four(PB)[:, t, :]
                    mm(dst, ones_row[:, 0:P], bias3[:, D:2 * D], start=True, stop=False)
                    for c in range(C):
                        hi, lo = (x[:, c, t * P:(t + 1) * P] for x in (xt_hi, xt_lo))
                        mm(dst, hi, wk_hi[:, c, :], start=False, stop=False)
                        mm(dst, hi, wk_lo[:, c, :], start=False, stop=False)
                        last = mm(dst, lo, wk_hi[:, c, :], start=False, stop=(c == C - 1))
                last.then_inc(k_mm, 1)

            def q_product(n, g):
                ge(pe, q_done, n)
                for o in range(C):
                    dst, cols = PA[:, o, :], slice(o * P, (o + 1) * P)
                    mm(dst, bias3[:, cols], ones_row[:, :], start=True, stop=False)
                    for c in range(C):
                        hi, lo = xt_hi[:, c, :], xt_lo[:, c, :]
                        mm(dst, wq_hi[:, c, cols], hi, start=False, stop=False)
                        mm(dst, wq_hi[:, c, cols], lo, start=False, stop=False)
                        last = mm(dst, wq_lo[:, c, cols], hi, start=False, stop=(c == C - 1))
                last.then_inc(q_mm, 1)

            def g_product(n, g):
                pe.wait_ge(k_done, n + 1)
                for t in range(T):
                    for c in range(C):
                        last = mm(PG[:, c, 0:D + 1], k_tok[:, t, c * P:(c + 1) * P], xn[g % 2][:, t, :],
                                  start=(g == 0 and t == 0), stop=(g == G - 1 and t == T - 1))
                last.then_inc(g_mm, 1)

            def g_transposes(b):
                pe.wait_ge(g_copied, b + 1)
                for i in range(C):
                    for c in range(C):
                        last = nc.tensor.transpose(PG[:, i, c * P:(c + 1) * P], g_sb[:, c, i * P:(i + 1) * P], ident[:, :])
                last.then_inc(gt_mm, 1)

            def kv_product(b):
                pe.wait_ge(gt_copied, b + 1)
                for c in range(C):
                    for i in range(C):
                        last = mm(PG[:, c, D:D + P], g_t[:, i, c * P:(c + 1) * P], wv[:, i, c * P:(c + 1) * P],
                                  start=(i == 0), stop=(i == C - 1))
                last.then_inc(kv_mm, 1)

            def pass1(b, last):
                for g in range(G):
                    n = b * G + g
                    later_batch = g == 0 and not (isinstance(b, int) and b == 0)
                    k_product(n, g)
                    if later_batch:
                        g_transposes(b - 1)
                    q_product(n, g)
                    if later_batch:
                        kv_product(b - 1)
                    if not (last and g == G - 1):
                        t1(n + 1, g + 1)
                    if g == 0 and later_batch:
                        pe.wait_ge(kv_done, 2 * C * b)
                    elif g == 0:
                        pe.wait_ge(flag_ready, 1)
                    g_product(n, g)

            pass1(0, False)
            with pe.Fori(1, B - 1) as b:
                pass1(b, False)
            pass1(B - 1, True)
            g_transposes(B - 1)
            kv_product(B - 1)

            pe.wait_ge(flag_ready, 1)
            routed = pe.value_load(routed_flag[0:1, 0:1], min_val=0, max_val=1)

            def run_experts(k, p, tiles, xt, y, h, free):
                with pe.If(routed > 0):
                    for s, v in free:
                        ge(pe, s, v)
                    for t in range(tiles):
                        for c in range(C):
                            last = mm(PT[0:p, 0, t * NE:(t + 1) * NE], xt[:, c, t * P:t * P + p], wr[:, c, :],
                                      start=(c == 0), stop=(c == C - 1))
                    last.then_inc(r_logits, 1)
                    with pe.Fori(0, NE) as e:
                        pe.wait_ge(r_w, 32 * (k * NE + e + 1))
                        for c in range(C):
                            last = mm(PT[:, 1, 0:tiles * p], w1e[:, c, :], xt[:, c, :], start=(c == 0), stop=(c == C - 1))
                        last.then_inc(r_hid, 1)
                        pe.wait_ge(r_sq, k * NE + e + 1)
                        for t in range(tiles):
                            last = mm(y[0:p, t, :], h[:, t * P:t * P + p], w2e[:, :], start=True, stop=True)
                        last.then_inc(r_y, 1)
                    pe.wait_ge(r_turn, (k + 1) * (NE + 1))

            pe.wait_ge(kv_done, 2 * C * B)
            pe.wait_ge(q_done, NG)
            pe.wait_ge(k_done, NG)

            def transposes(dst, src, done):
                for c in range(C):
                    for t in range(T):
                        last = nc.tensor.transpose(dst[:, c, t * P:(t + 1) * P], src[:, t, c * P:(c + 1) * P], ident[:, :])
                last.then_inc(done, 1)

            def hidden(dst, xt, done, copied, before, each):
                for c in range(C):
                    if c == 0 or each:
                        pe.wait_ge(copied, before + c + 1)
                    last = mm(dst, ws1[:, c, :], xt[:, c, :], start=(c == 0), stop=(c == C - 1))
                last.then_inc(done, 1)

            def down(pair, h, done):
                for t in range(T):
                    last = mm(four(pair)[:, t, :], h[:, t * P:(t + 1) * P], ws2[:, :], start=True, stop=True)
                last.then_inc(done, 1)

            def step(g, b):
                i, r, u, v = (lagged(g, b, back)[0] for back in range(4))
                if runs(i):
                    pe.wait_ge(q_copied, i + 1)
                    ge(pe, f1_relu, i - 1)
                    ge(pe, t3_done, i - 2)
                    for k in (0, 1, 2, 6, 7, 3, 4, 5):
                        t, c = k // C, k % C
                        if k == 3:
                            ge(pe, f3_relu, i - 2)
                        dst = PA[:, k // 3, (k % 3) * KVW:(k % 3 + 1) * KVW] if k < 6 else PT[:, 0, (k - 6) * KVW:(k - 5) * KVW]
                        last = mm(dst, q_cur[b % 2][:, c, t * P:(t + 1) * P], kv_all[:, b * C + c, :], start=True, stop=True)
                    last.then_inc(o_mm, 1)
                if runs(v):
                    pe.wait_ge(f3_sq, v + 1)
                    ge(pe, w_added, min(i, NG) if isinstance(i, int) else i)
                    down(PB, h3, f4_mm)
                    run_experts(routed_ordinal(g, b, 0), P, T, x3t, four(PB), h3,
                                [(f4_added, v + 1), (t3_done, v + 1)] + ([(o_done, 3 * (i + 1))] if runs(i) else []))
                if runs(r):
                    pe.wait_ge(norm2, T * (r + 1))
                    ge(pe, t3_done, i - 2)
                    if runs(i):
                        pe.wait_ge(o_done, 3 * i + 1)
                    transposes(PT, y2, t2_mm)
                if runs(i):
                    pe.wait_ge(o_done, 3 * (i + 1))
                    ge(pe, f2_added, i - 1)
                    for c in range(C):
                        for t in range(T):
                            last = nc.tensor.transpose(PG[:, c, t * P:(t + 1) * P], o_tok[:, t * C + c, :], ident[:, :])
                    last.then_inc(ot_mm, 1)
                if runs(r):
                    hidden(PA[:, 0, :], x2t, f1_mm, t2_done, C * r, 1)
                if runs(i):
                    pe.wait_ge(ot_done, i + 1)
                    ge(pe, f4_added, i - 2)
                    for t in range(T):
                        dst = four(PB)[:, t, :]
                        for c in range(C):
                            last = mm(dst, o_t[:, c, t * P:(t + 1) * P], wo[:, c, :], start=(c == 0), stop=(c == C - 1))
                    last.then_inc(w_mm, 1)
                if runs(u):
                    pe.wait_ge(norm3, T * (u + 1))
                    if runs(r):
                        pe.wait_ge(t2_done, C * (r + 1))
                    transposes(PT, y3, t3_mm)
                if runs(r):
                    pe.wait_ge(f1_sq, r + 1)
                    if runs(i):
                        pe.wait_ge(ot_done, i + 1)
                    ge(pe, f2_added, r)
                    down(PG, h2, f2_mm)
                    run_experts(routed_ordinal(g, b, 1), P, T, x2t, four(PG), h2,
                                [(f2_added, r + 1)] + ([(t3_done, u + 1)] if runs(u) else [(t2_done, C * (r + 1))]))
                if runs(u):
                    hidden(PA[:, 1, :], x3t, f3_mm, t3_done, u, 0)

            for b in range(B):
                step(0, b)
            with pe.Fori(1, G) as g:
                for b in range(B):
                    step(g, b)
            for b in range(3):
                step(G, b)

            def special_transposes(dst, src):
                for c in range(C):
                    last = nc.tensor.transpose(dst[:, c * SP:(c + 1) * SP], src[:, c * P:(c + 1) * P], ident[0:SP, 0:SP])
                return last

            pe.wait_ge(c_wts, 16 * (4 + 3 * HC))
            pe.wait_ge(f4_added, NG)
            for w, pair in enumerate((PA, PB, PT, PG)):
                for i in range(C):
                    for o in range(C):
                        last = nc.tensor.transpose(pair[:, i, o * P:(o + 1) * P], raw4[w][:, o, i * P:(i + 1) * P], ident[:, :])
                last.then_inc(c_wt, 1)
            pe.wait_ge(c_wt_sb, 4)
            pe.wait_ge(c_blk, 3)
            for i in range(3):
                last = nc.tensor.transpose(PA[:, 0, i * P:(i + 1) * P], l_blk[i], ident[:, :])
            last.then_inc(c_lt, 1)
            pe.wait_ge(c_z, 2)
            special_transposes(PT[:, 0, 0:C * SP], za)
            special_transposes(PT[:, 0, C * SP:2 * C * SP], zb).then_inc(c_zt, 1)
            pe.wait_ge(c_zt_sb, 2)
            pe.wait_ge(c_lt_sb, 3)
            for w, zt in enumerate((za_t, zb_t, zb_t)):
                for o in range(C):
                    for i in range(C):
                        last = mm(PA[:, 0, (w * C + o) * SP:(w * C + o + 1) * SP], w4t[w][:, i, o * P:(o + 1) * P], zt[:, i, :],
                                  start=(i == 0), stop=(i == C - 1))
            last.then_inc(c_qkv, 1)
            pe.wait_ge(c_qkv_sb, 3 * C)
            for bank, src, bd in ((0, k_t, l_bdt[1]), (1, v_t, l_bdt[2])):
                for c in range(C):
                    last = mm(PB[0:SP, bank, c * P:(c + 1) * P], src[:, c, :], bd, start=True, stop=True)
            last.then_inc(c_klin, 1)
            pe.wait_ge(c_kn, 1)
            special_transposes(PT[:, 0, 0:C * SP], kn).then_inc(c_knt, 1)
            for it in range(ITERS):
                if it == 0:
                    pe.wait_ge(c_kmask, C)
                else:
                    pe.wait_ge(c_qcur, it)
                for c in range(C):
                    last = mm(PB[0:SP, 0, c * P:(c + 1) * P], qcur_t[:, c, :], l_bdt[0], start=True, stop=True)
                last.then_inc(c_qlin, 1)
                if it == ITERS - 1:
                    pe.wait_ge(c_dsum, 1)
                    mm(PG[0:SP, 0, 0:1], ones_f[0:SP, 0:SP], dsum[0:SP, 0:1], start=True, stop=True).then_inc(c_diff, 1)
                pe.wait_ge(c_qn, it + 1)
                special_transposes(PT[:, 1, 0:C * SP], qn).then_inc(c_qnt, 1)
                pe.wait_ge(c_qnt_sb, it + 1)
                for c in range(C):
                    last = mm(PA[0:SP, c, :], qn_t[:, c, :], kn_mask[c], start=True, stop=True)
                last.then_inc(c_logit, 1)
                pe.wait_ge(c_pr, it + 1)
                for h in range(H):
                    last = nc.tensor.transpose(PG[0:SP, h // HC, (h % HC) * SP:(h % HC + 1) * SP], pr[:, h * SP:(h + 1) * SP],
                                               ident[0:SP, 0:SP])
                last.then_inc(c_prt, 1)
                pe.wait_ge(c_prt_sb, it + 1)
                for h in range(H):
                    last = mm(PT[0:SP, 0, h * HD:(h + 1) * HD], pr_t[:, h * SP:(h + 1) * SP], vi[:, h * HD:(h + 1) * HD],
                              start=True, stop=True)
                last.then_inc(c_pv, 1)
                pe.wait_ge(c_outs, it + 1)
                if it < ITERS - 1:
                    special_transposes(PB[:, 1, 0:C * SP], outs[it]).then_inc(c_outt, 1)
            pe.wait_ge(c_att, 1)
            special_transposes(PT[:, 1, 0:C * SP], att).then_inc(c_att_t, 1)
            pe.wait_ge(c_att_t_sb, 1)
            for i in range(C):
                last = mm(PB[0:SP, 0, 0:D], att_t[:, i, :], w4t[3][:, i, :], start=(i == 0), stop=(i == C - 1))
            last.then_inc(c_proj, 1)
            pe.wait_ge(c_z, 3)
            special_transposes(PT[:, 0, 0:C * SP], zs).then_inc(c_zt, 1)
            pe.wait_ge(c_zt_sb, 3)
            for c in range(C):
                last = mm(PA[:, 1, 0:SP], ws1[:, c, :], xs_t[:, c, :], start=(c == 0), stop=(c == C - 1))
            last.then_inc(c_hid, 1)
            pe.wait_ge(c_sq, 1)
            mm(PB[0:SP, 1, 0:D], h_s, ws2[:, :], start=True, stop=True).then_inc(c_ffn, 1)
            run_experts(2 * NG, SP, 1, xs_t, four(PB)[:, 2:3, :], h_s, [])


_NAMES = ["inputs_q", "Wq", "bq", "Wk", "bk", "Wv", "bv", "Wo", "bo"]
_NAMES_B = ["qw", "qb", "kw", "vw", "vb", "ow", "ob", "lna_w", "lnb_w", "lnc_w", "lnd_w", "lqw", "lqb", "lkw", "lkb", "lvw", "lvb"]
_NAMES_F = ["Ws1", "Ws2", "W1", "W2", "Wr"]
_INS = [f"L0_attn_a_{n}" for n in _NAMES] + [f"L0_attn_b_{n}" for n in _NAMES_B] + [f"L0_ffn_{n}" for n in _NAMES_F]


def kernel(**inputs):
    import numpy as _np
    import concourse.bacc as _bacc
    from concourse import mybir as _mybir
    from concourse.bass_utils import run_bass_kernel_spmd as _run

    nc = _bacc.Bacc("TRN2", target_bir_lowering=False, num_devices=1)
    arrays, args = {}, []
    for name in _INS:
        a = _np.ascontiguousarray(inputs[name])
        arrays[f"in_{name}_dram"] = a
        args.append(nc.dram_tensor(f"in_{name}_dram", a.shape, _mybir.dt.from_np(a.dtype), kind="ExternalInput").ap())
    args.append(nc.dram_tensor("out_0_dram", (B, S, D), _mybir.dt.float32, kind="ExternalOutput").ap())
    hybrid_kernel(nc, *args)
    r = _run(nc, [arrays], core_ids=[0])
    return r.results[0]["out_0_dram"]
```

```python
from contextlib import ExitStack

import concourse.bass as bass
from concourse import mybir

F32 = mybir.dt.float32
F32R = mybir.dt.float32r
BF16 = mybir.dt.bfloat16
I32 = mybir.dt.int32
ALU = mybir.AluOpType
ACT = mybir.ActivationFunctionType
AX = mybir.AxisListType.X

P = 128
B, S, D = 4, 2048, 256
C = D // P
H, HD = 16, 16
HC = H // C
T = 4
GT = T * P
G = S // GT
NG = B * G
F = 128
NE = 8
KVW = P + HC
LN_EPS = 1e-5
NORM_EPS = 1e-6
SPT = 16
SP = B * SPT
ITERS = 3
THRESH, FACTOR = 0.01, 0.1
WR_NORM2_BOUND = (16.0 / (2.0 * D ** 0.5)) ** 2


def ge(eng, sem, value):
    if isinstance(value, int) and value <= 0:
        return
    eng.wait_ge(sem, value)


def hybrid_kernel(nc, x_in, Wq, bq, Wk, bk, Wv, bv, Wo, bo, qw, qb, kw, vw, vb, ow, ob,
                  lna_w, lnb_w, lnc_w, lnd_w, lqw, lqb, lkw, lkb, lvw, lvb,
                  Ws1, Ws2, W1, W2, Wr, out):
    x_dram = x_in.rearrange("b (g t p) d -> (b g) p t d", t=T, p=P)
    out_dram = out.rearrange("b (g t p) d -> (b g) p t d", t=T, p=P)

    def rows(w):
        return w.rearrange("(c p) n -> p c n", p=P)

    def row(v):
        return v.rearrange("(o n) -> o n", o=1)

    with ExitStack() as ctx:
        def sb(name, shape, dt=F32):
            return ctx.enter_context(nc.sbuf_tensor(name, shape, dt))

        def ps(name):
            return ctx.enter_context(nc.psum_tensor(name, [P, 2, 512], F32))

        def sem(name):
            return ctx.enter_context(nc.semaphore(name))

        x_all = sb("x_all", [P, NG * T, D])
        q_all = sb("q_all", [P, NG * C, GT])
        kv_all = sb("kv_all", [P, B * C, KVW])
        ident = sb("ident", [P, P])
        head_mask = sb("head_mask", [P, HC])
        ones_row = sb("ones_row", [P, GT], BF16)
        bias3 = sb("bias3", [P, 2 * D], BF16)
        bv_rows, bo_rows, ob_rows = [sb(n, [P, D]) for n in ("bv_rows", "bo_rows", "ob_rows")]
        wv = sb("wv", [P, C, D])
        wo = sb("wo", [P, C, D])
        ws1 = sb("ws1", [P, C, F])
        ws2 = sb("ws2", [P, D])
        wr = sb("wr", [P, C, NE])
        routed_flag = sb("routed_flag", [1, 1], I32)
        wr_tmp = sb("wr_tmp", [P, C * NE])
        wr_max = sb("wr_max", [1, 4])
        ones_f = sb("ones_f", [P, P])
        kv_tmp = sb("kv_tmp", [P, C, P])
        minus_half = sb("minus_half", [P, H])
        minus_one = sb("minus_one", [P, 1])
        ln_bn = sb("ln_bn", [P, 2, T, 6])
        ln_mv = sb("ln_mv", [P, 2, T, 2])
        ln_rstd = sb("ln_rstd", [P, 2, T])
        ln_shift = sb("ln_shift", [P, 2, T])
        norm_sb = sb("norm_sb", [P, T * C, HC])
        norm_inv = sb("norm_inv", [P, T * C, HC])
        g_sb = sb("g_sb", [P, C, D + 1])
        g_t = sb("g_t", [P, C, D])
        probs = sb("probs", [P, NE, T])
        r_lg = sb("r_lg", [P, T, NE])
        r_top = sb("r_top", [P, T, 8])
        r_gap = sb("r_gap", [P, 4, T])

        SCR = 10 * 1024
        scratch = sb("scratch", [P, SCR])
        used = [0]

        def part(n):
            a = scratch[:, used[0]:used[0] + n]
            used[0] += n
            assert used[0] <= SCR
            return a

        xn = [part(T * (D + 1)).rearrange("p (t d) -> p t d", t=T) for _ in range(2)]
        k_tok = part(T * D).rearrange("p (t d) -> p t d", t=T)
        exp_kq = part(T * D)
        exp_k = exp_kq.rearrange("p (t d) -> p t d", t=T)
        exp_q = exp_kq.rearrange("p (c n) -> p c n", c=C)
        wq_raw = part(C * D).rearrange("p (c n) -> p c n", c=C)
        wk_raw = part(C * D).rearrange("p (c n) -> p c n", c=C)
        bias_rows = part(2 * D)
        bpart = part(2 * D).bitcast(BF16).rearrange("p (k n) -> p k n", k=2)
        used[0] = 0
        q_cur = [part(C * GT).rearrange("p (c n) -> p c n", c=C) for _ in range(2)]
        o_tok = part(T * D).rearrange("p (k n) -> p k n", k=T * C)
        o_t = part(C * GT).rearrange("p (c n) -> p c n", c=C)
        y2 = part(T * D).rearrange("p (t d) -> p t d", t=T)
        y3 = part(T * D).rearrange("p (t d) -> p t d", t=T)
        x2t = part(C * GT).rearrange("p (c n) -> p c n", c=C)
        x3t = part(C * GT).rearrange("p (c n) -> p c n", c=C)
        h2, h3 = part(GT), part(GT)
        x_out = part(T * D).rearrange("p (t d) -> p t d", t=T)

        with ExitStack() as pass1_memory:
            def sb1(name, shape):
                return pass1_memory.enter_context(nc.sbuf_tensor(name, shape, F32R))

            wq_hi, wq_lo = sb1("wq_hi", [P, C, D]), sb1("wq_lo", [P, C, D])
            wk_hi, wk_lo = sb1("wk_hi", [P, C, D]), sb1("wk_lo", [P, C, D])
            xt_hi, xt_lo = sb1("xt_hi", [P, C, GT]), sb1("xt_lo", [P, C, GT])
        b_weights = sb("b_weights", [P, 2, 4, C * D])

        PT, PA, PB, PG = ps("PT"), ps("PA"), ps("PB"), ps("PG")

        w1e, w2e = g_t[:, 0, :].rearrange("p (c f) -> p c f", c=C), g_t[:, 1, :]

        raw4 = [b_weights[:, 0, i, :].rearrange("p (c n) -> p c n", c=C) for i in range(4)]
        w4t = [b_weights[:, 1, i, :].rearrange("p (c n) -> p c n", c=C) for i in range(4)]

        def carve(piece):
            at = [0]

            def take(n, p=P):
                a = piece[0:p, at[0]:at[0] + n]
                at[0] += n
                assert at[0] <= piece.shape[1]
                return a
            return take

        def chunked(ap):
            return ap.rearrange("p (c n) -> p c n", c=C)

        used_q = [carve(q_all[:, b * G * C:(b * G + 1) * C, :].rearrange("p k n -> p (k n)")) for b in range(B)]
        l_rows = [used_q[0](HD) for _ in range(3)]
        l_blk = [used_q[0](P) for _ in range(3)]
        l_bdt_all = used_q[0](3 * P)
        l_bdt = [l_bdt_all[:, i * P:(i + 1) * P] for i in range(3)]
        qb_col, vb_col = used_q[0](C), used_q[0](C)
        lqb_b, lkb_b, lvb_b, lnc_b, lnd_b = [used_q[0](HD, SP) for _ in range(5)]
        s_bn, s_mv, s_rs = used_q[0](6, SP), used_q[0](2, SP), used_q[0](4, SP)
        xs, zs, zz, za = [used_q[1](D, SP) for _ in range(4)]
        zb, ob_b, lna_b, lnb_b = [used_q[2](D, SP) for _ in range(4)]
        za_t, zb_t, qcur_t, k_t, v_t, qn_t, att_t, xs_t = [chunked(used_q[3](C * SP)) for _ in range(8)]
        after_raw = carve(b_weights[:, 0, :, :].rearrange("p i n -> p (i n)"))
        vi, lin, cen, sq16, kn, qn = [after_raw(D, SP) for _ in range(6)]
        neg_mask = after_raw(SP, SP)
        st16 = [after_raw(H, SP) for _ in range(4)]
        mx16, sum16, inv16 = [after_raw(H, SP) for _ in range(3)]
        dsum = after_raw(8)
        out_cur = after_raw(D, SP)
        later_q = [q_all[:, (b * G + 1) * C:(b * G + 2) * C, :].rearrange("p k n -> p (k n)") for b in range(B)]
        kn_mask = [later_q[0][:, c * HC * SP:(c + 1) * HC * SP] for c in range(C)]
        lg, pr, pr_t = [piece[0:SP, :] for piece in later_q[1:]]
        last_q = [carve(q_all[:, (b * G + 2) * C:(b * G + 3) * C, :].rearrange("p k n -> p (k n)")) for b in range(2)]
        out_prev, dif, att = [last_q[0](D, SP) for _ in range(3)]
        tmpd, x_s_out = [last_q[1](D, SP) for _ in range(2)]
        h_s = last_q[1](SP)

        w_loaded = sem("w_loaded")
        w2_loaded = sem("w2_loaded")
        wr_loaded = sem("wr_loaded")
        bias_loaded = sem("bias_loaded")
        consts = sem("consts")
        pool_setup = sem("pool_setup")
        setup_dve = sem("setup_dve")
        w_split = sem("w_split")
        bias_ready = sem("bias_ready")
        wr_sq, wr_sum, flag_ready = sem("wr_sq"), sem("wr_sum"), sem("flag_ready")
        x_loaded = [sem(f"x_loaded{g}") for g in range(G)]
        bn1, stat1, pow1, rstd1, norm1 = [sem(n) for n in ("bn1", "stat1", "pow1", "rstd1", "norm1")]
        bn2, stat2, pow2, rstd2, norm2 = [sem(n) for n in ("bn2", "stat2", "pow2", "rstd2", "norm2")]
        bn3, stat3, pow3, rstd3, norm3 = [sem(n) for n in ("bn3", "stat3", "pow3", "rstd3", "norm3")]
        t1_mm, t1_hi, t1_lo = sem("t1_mm"), sem("t1_hi"), sem("t1_lo")
        k_mm, k_exp, k_done = sem("k_mm"), sem("k_exp"), sem("k_done")
        q_mm, q_exp, q_done = sem("q_mm"), sem("q_exp"), sem("q_done")
        g_mm, g_copied, gt_mm, gt_copied, kv_mm, kv_step, kv_done = [
            sem(n) for n in ("g_mm", "g_copied", "gt_mm", "gt_copied", "kv_mm", "kv_step", "kv_done")]
        q_copied, o_mm, o_max, o_inv, o_done = [sem(n) for n in ("q_copied", "o_mm", "o_max", "o_inv", "o_done")]
        ot_mm, ot_done, w_mm, w_added = [sem(n) for n in ("ot_mm", "ot_done", "w_mm", "w_added")]
        t2_mm, t2_done, f1_mm, f1_relu, f1_sq, f2_mm, f2_added = [
            sem(n) for n in ("t2_mm", "t2_done", "f1_mm", "f1_relu", "f1_sq", "f2_mm", "f2_added")]
        t3_mm, t3_done, f3_mm, f3_relu, f3_sq, f4_mm, f4_added = [
            sem(n) for n in ("t3_mm", "t3_done", "f3_mm", "f3_relu", "f3_sq", "f4_mm", "f4_added")]
        stored = sem("stored")
        bo_added, ob_added = sem("bo_added"), sem("ob_added")
        r_logits, r_step, r_gap_ready, r_exp, r_turn, r_w, r_hid, r_relu, r_sq, r_y = [
            sem(n) for n in ("r_logits", "r_step", "r_gap_ready", "r_exp", "r_turn", "r_w", "r_hid", "r_relu", "r_sq", "r_y")]
        c_link = sem("c_link")
        c_pool, c_pool16 = sem("c_pool"), sem("c_pool16")
        (c_wts, c_vecs, c_xs, c_out, c_wt, c_wt_sb, c_blk, c_lt, c_lt_sb, c_stat, c_rstd, c_z, c_zt, c_zt_sb,
         c_qkv, c_q_sb, c_kv_sb, c_klin, c_klin_read, c_kn, c_knt, c_kmask, c_qlin, c_lin, c_diff, c_var, c_rstd16,
         c_qn, c_qnt, c_qnt_sb, c_logit, c_scaled, c_lg, c_pr, c_prt, c_prt_sb, c_pv, c_outs, c_outt, c_dsum,
         c_att, c_att_t, c_att_t_sb, c_proj, c_hid, c_relu, c_sq, c_ffn, c_final) = [sem(f"c_{n}") for n in (
             "wts", "vecs", "xs", "out", "wt", "wt_sb", "blk", "lt", "lt_sb", "stat", "rstd", "z", "zt", "zt_sb",
             "qkv", "q_sb", "kv_sb", "klin", "klin_read", "kn", "knt", "kmask", "qlin", "lin", "diff", "var", "rstd16",
             "qn", "qnt", "qnt_sb", "logit", "scaled", "lg", "pr", "prt", "prt_sb", "pv", "outs", "outt", "dsum",
             "att", "att_t", "att_t_sb", "proj", "hid", "relu", "sq", "ffn", "final")]
        c_out_zero = sem("c_out_zero")
        c_turn = sem("c_turn")

        waits_passed = {"sp": sem("sp_waits_passed"), "act": sem("act_waits_passed"),
                        "dve": sem("dve_waits_passed"), "pool": sem("pool_waits_passed"), "pe": sem("pe_waits_passed")}

        def ge_apart(eng, name, sem_, value):
            ge(eng, sem_, value)
            if not isinstance(value, int):
                eng.sem_inc(waits_passed[name], 1)

        block = ctx.enter_context(nc.Block())

        def four(pair):
            return pair[:, :, :].rearrange("p b (t d) -> p (b t) d", d=D)

        def x_group(n):
            return x_all[:, bass.ds(n * T, T), :]

        def x_tile(n, t):
            return x_all[:, bass.ds(n * T + t, 1), :]

        def lagged(g, b, back):
            k = b - back
            gj, bj = g + k // B, k % B
            return gj * B + bj, bj * G + gj, bj

        def runs(j):
            return not isinstance(j, int) or 0 <= j < NG

        def iteration(g):
            return None if isinstance(g, int) and g < 2 else g - 2

        def routed_ordinal(g, b, second):
            i = g * B + b
            if not isinstance(i, int):
                return i * 2 - 4 + second
            f4, f2 = min(max(i - 3, 0), NG), min(max(i - 1, 0), NG)
            return f4 + f2 + (1 if second and 0 <= i - 3 < NG else 0)

        def per_head(ap, k, p=P):
            return ap.rearrange("p (a h o) -> p a h o", a=k, o=1).to_broadcast([p, k, HC, HD])

        @block.sync
        def _(sp):
            sp.dma_start(x_all[:, 0:T, :], x_dram[0]).then_inc(x_loaded[0], 16)
            for dst, w in ((wq_raw, Wq), (wk_raw, Wk)):
                sp.dma_start(dst, rows(w)).then_inc(w_loaded, 16)
            for i, v in enumerate((bq, bk)):
                sp.dma_start(bias_rows[0:3, i * D:(i + 1) * D], row(v).to_broadcast([3, D])).then_inc(bias_loaded, 16)
            sp.dma_start(wr[:, :, :], rows(Wr)).then_inc(wr_loaded, 16)
            for g in range(1, G):
                sp.dma_start(x_all[:, g * T:(g + 1) * T, :], x_dram[g]).then_inc(x_loaded[g], 16)
            for dst, w in ((wv[:, :, :], rows(Wv)), (wo[:, :, :], rows(Wo)),
                           (ws1[:, :, :], rows(Ws1)), (ws2[:, :], Ws2), (bv_rows[:, :], row(bv).to_broadcast([P, D])),
                           (bo_rows[:, :], row(bo).to_broadcast([P, D])), (ob_rows[:, :], row(ob).to_broadcast([P, D]))):
                sp.dma_start(dst, w).then_inc(w2_loaded, 16)
            with sp.Fori(1, B) as b:
                for g in range(G):
                    n = b * G + g
                    sp.wait_ge(stat1, T * (n - G + 1))
                    sp.dma_start(x_group(n), x_dram[bass.ds(n, 1)].rearrange("o p t d -> p (o t) d")).then_inc(x_loaded[g], 16)
            sp.wait_ge(flag_ready, 1)
            routed = sp.value_load(routed_flag[0:1, 0:1], min_val=0, max_val=1)

            def load_experts(k):
                with sp.If(routed > 0):
                    with sp.Fori(0, NE) as e:
                        sp.wait_ge(r_turn, k * (NE + 1) + e + 1)
                        sp.dma_start(w1e[:, :, :], W1[bass.ds(e, 1)].rearrange("o (c p) f -> p (o c) f", p=P)).then_inc(r_w, 16)
                        sp.dma_start(w2e[:, :], W2[bass.ds(e, 1)].rearrange("o f d -> f (o d)")).then_inc(r_w, 16)
                    ge_apart(sp, "sp", r_turn, (k + 1) * (NE + 1))

            def step(g, b):
                u, n, bu = lagged(g, b, 3)
                if runs(u):
                    load_experts(routed_ordinal(g, b, 0))
                    sp.wait_ge(f4_added, u + 1)
                    sp.dma_start(out_dram[bass.ds(n, 1)].rearrange("o p t d -> p (o t) d"),
                                 x_out).then_inc(stored, 16)
                if runs(lagged(g, b, 1)[0]):
                    load_experts(routed_ordinal(g, b, 1))

            sp.wait_ge(q_mm, NG)
            for dst, w in zip(raw4, (qw, kw, vw, ow)):
                sp.dma_start(dst, rows(w)).then_inc(c_wts, 16)
            for b in range(B):
                step(0, b)
            sp.wait_ge(q_copied, B)
            for dst, v in ((ob_b, ob), (lna_b, lna_w), (lnb_b, lnb_w)):
                sp.dma_start(dst, row(v).to_broadcast([SP, D])).then_inc(c_vecs, 16)
            for dst, w in zip(l_rows, (lqw, lkw, lvw)):
                for h in range(HC):
                    sp.dma_start(dst[h * HD:(h + 1) * HD, :], w).then_inc(c_vecs, 16)
            with nc.allow_non_contiguous_dma(reason="two short bias vectors, features on partitions"):
                for dst, v in ((qb_col, qb), (vb_col, vb)):
                    sp.dma_start(dst, v.rearrange("(c p) -> p c", p=P)).then_inc(c_vecs, 16)
            for dst, v in ((lqb_b, lqb), (lkb_b, lkb), (lvb_b, lvb), (lnc_b, lnc_w), (lnd_b, lnd_w)):
                sp.dma_start(dst, row(v).to_broadcast([SP, HD])).then_inc(c_vecs, 16)
            step(1, 0)
            sp.wait_ge(f2_added, B)
            for b in range(B):
                sp.dma_start(xs[b * SPT:(b + 1) * SPT, :], x_all[0:SPT, b * G * T, :]).then_inc(c_xs, 16)
            for b in range(1, B):
                step(1, b)
            with sp.Fori(2, G) as g:
                for b in range(B):
                    step(g, b)
            for b in range(3):
                step(G, b)

            load_experts(2 * NG)
            sp.wait_ge(stored, 16 * NG)
            sp.wait_ge(c_final, 1)
            for b in range(B):
                sp.dma_start(out[b, 0:SPT, :], x_s_out[b * SPT:(b + 1) * SPT, :]).then_inc(c_out, 16)
            sp.wait_ge(c_out, 16 * B)

        @block.gpsimd
        def _(pool):
            def mask(ap, pattern, lower, upper):
                for base, mult, pat in (lower, upper):
                    pool.wait_ge(pool_setup, mask.n)
                    nc.gpsimd.affine_select(out=ap, in_=ap, compare_op=ALU.is_ge, fill=0.0, base=base,
                                            pattern=[[pat, pattern]], channel_multiplier=mult).then_inc(pool_setup, 1)
                    mask.n += 1
            mask.n = 3
            nc.gpsimd.memset(ident[:, :], 1.0).then_inc(pool_setup, 1)
            nc.gpsimd.memset(head_mask[:, :], 1.0).then_inc(pool_setup, 1)
            nc.gpsimd.memset(minus_half[:, :], -0.5).then_inc(pool_setup, 1)
            mask(ident[:, :], P, (0, 1, -1), (0, -1, 1))
            mask(head_mask[:, :], HC, (0, 1, -HD), (HD - 1, -1, HD))
            nc.gpsimd.memset(ones_f[:, :], 1.0).then_inc(consts, 1)
            nc.gpsimd.memset(ones_row[:, :], 1.0).then_inc(consts, 1)
            for i in range(2):
                nc.gpsimd.memset(xn[i][:, :, D:D + 1], 1.0).then_inc(consts, 1)
            pool.wait_ge(pool_setup, mask.n)
            nc.gpsimd.tensor_copy(norm_inv[:, 0, 0:1], ident[:, 0:1]).then_inc(consts, 1)

            def rstd(slot, j, stat, powed, done, normed):
                mean, var = ln_mv[:, slot, :, 0], ln_mv[:, slot, :, 1]
                pool.wait_ge(stat, T * (j + 1))
                ge_apart(pool, "pool", normed, T * j)
                nc.gpsimd.tensor_scalar(ln_rstd[:, slot, :], var, LN_EPS, None, ALU.add).then_inc(powed, 1)
                pool.wait_ge(powed, 3 * j + 1)
                nc.gpsimd.tensor_tensor(ln_rstd[:, slot, :], ln_rstd[:, slot, :], minus_half[:, 0:T], ALU.pow).then_inc(powed, 1)
                pool.wait_ge(powed, 3 * j + 2)
                nc.gpsimd.tensor_tensor(ln_shift[:, slot, :], mean, ln_rstd[:, slot, :], ALU.mult).then_inc(powed, 1)
                ge_apart(pool, "pool", powed, 3 * j + 3)
                nc.gpsimd.tensor_scalar(ln_shift[:, slot, :], ln_shift[:, slot, :], -1.0, None, ALU.mult).then_inc(done, 1)

            def ln1(n):
                rstd(0, n, stat1, pow1, rstd1, norm1)

            def add_row(n, rows_, done):
                nc.gpsimd.tensor_tensor(x_group(n), x_group(n), rows_[:, :].rearrange("p (o d) -> p o d", o=1).to_broadcast([P, T, D]),
                                        ALU.add).then_inc(done, 1)

            def add_bo(n):
                ge_apart(pool, "pool", norm1, T * (n + 1))
                add_row(n, bo_rows, bo_added)

            ln1(0)
            pool.wait_ge(w2_loaded, 16 * 7)
            with pool.Fori(1, NG) as n:
                ln1(n)
                add_bo(n - 1)
            add_bo(NG - 1)

            pool.wait_ge(g_mm, NG)
            pool.wait_ge(q_done, NG)
            pool.wait_ge(norm1, T * NG)

            def copy_q(g, b, ahead):
                i, n, bi = lagged(g, b, -ahead)
                if runs(i):
                    ge(pool, o_mm, i - 1)
                    nc.gpsimd.tensor_copy(q_cur[bi % 2], q_all[:, bass.ds(n * C, C), :]).then_inc(q_copied, 1)

            def step(g, b):
                r, nr, _ = lagged(g, b, 1)
                if runs(r):
                    ge_apart(pool, "pool", norm2, T * (r + 1))
                    add_row(nr, ob_rows, ob_added)
                u = lagged(g, b, 2)[0]
                if runs(u):
                    rstd(1, u, stat3, pow3, rstd3, norm3)
                attention_b(g, b, "after rstd3")
                copy_q(g, b, 1)
                attention_b(g, b, "before rstd2")
                i = g * B + b
                if runs(i):
                    rstd(0, i, stat2, pow2, rstd2, norm2)
                attention_b(g, b, "end")

            def chain_rstd(k):
                pool.wait_ge(c_stat, k + 1)
                nc.gpsimd.tensor_scalar(s_rs[:, 0:1], s_mv[:, 1:2], LN_EPS, None, ALU.add).then_inc(c_pool, 1)
                pool.wait_ge(c_pool, k + 1)
                nc.gpsimd.tensor_tensor(s_rs[:, 1:2], s_rs[:, 0:1], minus_half[0:SP, 0:1], ALU.pow).then_inc(c_rstd, 1)

            def chain_rstd16(k):
                ge_apart(pool, "pool", c_var, k + 1)
                nc.gpsimd.tensor_scalar(st16[2], st16[2], 1.0 / HD, LN_EPS, ALU.mult, ALU.add).then_inc(c_pool16, 1)
                pool.wait_ge(c_pool16, k + 1)
                nc.gpsimd.tensor_tensor(st16[3], st16[2], minus_half[0:SP, :], ALU.pow).then_inc(c_rstd16, 1)

            def attention_b(g, b, place):
                it = iteration(g)
                if it is None:
                    if (g, b, place) == (1, 1, "after rstd3"):
                        chain_rstd(0)
                    elif (g, b, place) == (1, 1, "end"):
                        chain_rstd(1)
                    elif (g, b, place) == (1, 3, "before rstd2"):
                        chain_rstd16(0)
                elif (b, place) == (0, "end"):
                    chain_rstd16(it + 1)

            copy_q(0, 0, 0)
            for g in range(G + 1):
                for b in range(B):
                    step(g, b)
            chain_rstd(2)

        @block.scalar
        def _(act):
            def normalise(dst, n, slot, j, ready, done):
                ge_apart(act, "act", ready, j + 1)
                for t in range(T):
                    nc.scalar.activation(dst[:, t:t + 1, 0:D], x_tile(n, t), ACT.Identity, scale=ln_rstd[:, slot, t:t + 1],
                                         bias=ln_shift[:, slot, t:t + 1]).then_inc(done, 1)

            def ln1(n, g):
                ge_apart(act, "act", g_mm, n - 1)
                normalise(xn[g % 2], n, 0, n, rstd1, norm1)

            def t1(n, g):
                act.wait_ge(t1_mm, n + 1)
                ge(act, q_mm, n)
                nc.scalar.activation(xt_hi[:, :, :], PT[:, :, :], ACT.Copy).then_inc(t1_hi, 1)

            act.wait_ge(w_loaded, 32)
            for hi, raw in ((wq_hi, wq_raw), (wk_hi, wk_raw)):
                nc.scalar.activation(hi[:, :, :], raw, ACT.Copy).then_inc(w_split, 1)
            ln1(0, 0)
            t1(0, 0)

            def pass1(b, last):
                for g in range(G):
                    n = b * G + g
                    if not (last and g == G - 1):
                        ln1(n + 1, g + 1)
                    act.wait_ge(k_mm, n + 1)
                    ge(act, q_done, n)
                    nc.scalar.activation(exp_k, four(PB), ACT.Exp, bias=minus_one[:, 0:1]).then_inc(k_exp, 1)
                    if g == 0 and not (isinstance(b, int) and b == 0):
                        transposed_g(b - 1)
                    act.wait_ge(q_mm, n + 1)
                    act.wait_ge(k_done, n + 1)
                    nc.scalar.activation(exp_q, PA[:, :, :], ACT.Exp, bias=minus_one[:, 0:1]).then_inc(q_exp, 1)
                    if not (last and g == G - 1):
                        t1(n + 1, g + 1)

            def transposed_g(b):
                act.wait_ge(gt_mm, b + 1)
                ge(act, kv_mm, b)
                nc.scalar.activation(g_t[:, :, :], PG[:, :, 0:D], ACT.Copy).then_inc(gt_copied, 1)

            act.wait_ge(setup_dve, 1)
            pass1(0, False)
            with act.Fori(1, B - 1) as b:
                pass1(b, False)
            pass1(B - 1, True)
            transposed_g(B - 1)

            act.wait_ge(flag_ready, 1)
            routed = act.value_load(routed_flag[0:1, 0:1], min_val=0, max_val=1)

            act.wait_ge(g_mm, NG)
            act.wait_ge(q_done, NG)

            def run_experts(k, n_tok, relu):
                with act.If(routed > 0):
                    act.wait_ge(r_gap_ready, k + 1)
                    nc.scalar.activation(r_gap[:, 1, :], r_gap[:, 0, :], ACT.Exp).then_inc(r_exp, 1)
                    with act.Fori(0, NE) as e:
                        act.wait_ge(r_hid, k * NE + e + 1)
                        nc.scalar.activation(relu, PT[:, 1, 0:n_tok], ACT.Relu).then_inc(r_relu, 1)

            def step(g, b):
                i = g * B + b
                u3 = lagged(g, b, 3)[0]
                if runs(u3):
                    run_experts(routed_ordinal(g, b, 0), GT, h3)
                r = lagged(g, b, 1)[0]
                if runs(r):
                    act.wait_ge(t2_mm, r + 1)
                    ge(act, f1_mm, r)
                    for c in range(C):
                        nc.scalar.activation(x2t[:, c, :], PT[:, c, :], ACT.Copy).then_inc(t2_done, 1)
                if runs(i):
                    act.wait_ge(ot_mm, i + 1)
                    ge(act, w_mm, i)
                    nc.scalar.activation(o_t, PG[:, :, :], ACT.Copy).then_inc(ot_done, 1)
                u, nu, _ = lagged(g, b, 2)
                if runs(r):
                    act.wait_ge(f1_mm, r + 1)
                    ge(act, f2_mm, r)
                    nc.scalar.activation(h2, PA[:, 0, :], ACT.Relu).then_inc(f1_relu, 1)
                if runs(u):
                    ge(act, t3_mm, u)
                    normalise(y3, nu, 1, u, rstd3, norm3)
                    act.wait_ge(t3_mm, u + 1)
                    ge(act, f3_mm, u)
                    nc.scalar.activation(x3t, PT[:, :, :], ACT.Copy).then_inc(t3_done, 1)
                if iteration(g) is not None and b == 2:
                    it = iteration(g)
                    act.wait_ge(c_lg, it + 1)
                    nc.scalar.activation(pr, lg, ACT.Exp).then_inc(c_pr, 1)
                if runs(r):
                    run_experts(routed_ordinal(g, b, 1), GT, h2)
                if runs(u):
                    act.wait_ge(f3_mm, u + 1)
                    ge(act, f4_mm, u)
                    nc.scalar.activation(h3, PA[:, 1, :], ACT.Relu).then_inc(f3_relu, 1)
                if runs(i):
                    ge(act, t2_mm, i)
                    normalise(y2, lagged(g, b, 0)[1], 0, i, rstd2, norm2)
                if iteration(g) is not None and b == 2:
                    act.wait_ge(c_prt, it + 1)
                    nc.scalar.activation(pr_t.rearrange("p (b n) -> p b n", b=2), PG[0:SP, :, :], ACT.Copy).then_inc(c_prt_sb, 1)
                elif iteration(g) is None and g == 1 and b < 2:
                    act.wait_ge(c_wt, 2 * b + 2)
                    nc.scalar.activation(w4t[2 * b + 1], PG[:, 0, :].rearrange("p (c n) -> p c n", c=C), ACT.Copy).then_inc(c_wt_sb, 1)

            for g in range(2):
                for b in range(B):
                    step(g, b)
            with act.Fori(2, G) as g:
                for b in range(B):
                    step(g, b)
            for b in range(B):
                step(G, b)

            act.wait_ge(c_hid, 1)
            nc.scalar.activation(h_s, PA[:, 1, 0:SP], ACT.Relu).then_inc(c_relu, 1)
            run_experts(2 * NG, SP, h_s)

        @block.vector
        def _(dve):
            links = [0]

            def link(ins):
                ins.then_inc(c_link, 1)
                links[0] += 1
                dve.wait_ge(c_link, links[0])

            def stats(n, slot, j, bn, stat, used):
                ge_apart(dve, "dve", used, j)
                for t in range(T):
                    nc.vector.bn_stats(ln_bn[:, slot, t:t + 1, :], x_tile(n, t)).then_inc(bn, 1)
                for t in range(T):
                    ge_apart(dve, "dve", bn, T * j + t + 1)
                    nc.vector.bn_aggr(ln_mv[:, slot, t:t + 1, :], ln_bn[:, slot, t:t + 1, :]).then_inc(stat, 1)

            def ln1(n, g, b):
                dve.wait_ge(x_loaded[g % G], 16 * (b + g // G + 1))
                stats(n, 0, n, bn1, stat1, rstd1)

            def t1(n, g):
                dve.wait_ge(t1_hi, n + 1)
                ge(dve, q_mm, n)
                nc.vector.tensor_tensor(xt_lo[:, :, :], PT[:, :, :], xt_hi[:, :, :].bitcast(F32),
                                        ALU.subtract).then_inc(t1_lo, 1)

            nc.vector.memset(minus_one[:, :], -1.0).then_inc(setup_dve, 1)
            nc.vector.memset(bias3[:, :], 0.0).then_inc(setup_dve, 1)
            ln1(0, 0, 0)
            for i, (lo, hi, raw) in enumerate(((wq_lo, wq_hi, wq_raw), (wk_lo, wk_hi, wk_raw))):
                dve.wait_ge(w_split, i + 1)
                nc.vector.tensor_tensor(lo[:, :, :], raw, hi[:, :, :].bitcast(F32), ALU.subtract).then_inc(setup_dve, 1)
            dve.wait_ge(bias_loaded, 32)
            dve.wait_ge(consts, 5)
            link(nc.vector.tensor_scalar(bias_rows[0:3, 0:2 * D], bias_rows[0:3, 0:2 * D], 1.0, None, ALU.add))
            link(nc.vector.tensor_copy(bpart[0:3, 0, :], bias_rows[0:3, :]))
            link(nc.vector.tensor_tensor(bias_rows[0:3, :], bias_rows[0:3, :], bpart[0:3, 0, :], ALU.subtract))
            link(nc.vector.tensor_copy(bpart[0:3, 1, :], bias_rows[0:3, :]))
            link(nc.vector.tensor_tensor(bias_rows[0:3, :], bias_rows[0:3, :], bpart[0:3, 1, :], ALU.subtract))
            link(nc.vector.tensor_scalar(bias_rows[0:3, :], bias_rows[0:3, :], ident[0:3, 2:3], None, ALU.mult))
            link(nc.vector.scalar_tensor_tensor(bias_rows[0:3, :], bpart[0:3, 1, :], ident[0:3, 1:2], bias_rows[0:3, :], ALU.mult, ALU.add))
            nc.vector.scalar_tensor_tensor(bias3[0:3, :], bpart[0:3, 0, :], ident[0:3, 0:1], bias_rows[0:3, :],
                                           ALU.mult, ALU.add).then_inc(bias_ready, 1)
            dve.wait_ge(wr_loaded, 16)
            nc.vector.tensor_tensor(wr_tmp[:, :], wr[:, :, :].rearrange("p c e -> p (c e)"),
                                    wr[:, :, :].rearrange("p c e -> p (c e)"), ALU.mult).then_inc(wr_sq, 1)
            ln1(1, 1, 0)
            t1(0, 0)
            dve.wait_ge(wr_sum, 1)
            link(nc.vector.reduce_max(wr_max[0:1, 0:1], PG[0:1, 0, 0:NE], AX))
            link(nc.vector.tensor_scalar(wr_max[0:1, 1:2], wr_max[0:1, 0:1], WR_NORM2_BOUND, None, ALU.is_lt))
            nc.vector.tensor_scalar(routed_flag[0:1, 0:1], wr_max[0:1, 1:2], -1.0, 1.0, ALU.mult, ALU.add).then_inc(flag_ready, 1)

            def pass1(b, last):
                for g in range(G):
                    n = b * G + g
                    later_batch = not (isinstance(b, int) and b == 0)
                    if g == 0 and later_batch:
                        copy_g(b - 1)
                    dve.wait_ge(k_exp, n + 1)
                    ge(dve, g_mm, n)
                    nc.vector.scalar_tensor_tensor(k_tok, exp_k, 1.0, four(PB), ALU.min, ALU.max).then_inc(k_done, 1)
                    if not (last and g >= G - 2):
                        ln1(n + 2, g + 2, b)
                    if g == 0 and later_batch:
                        batch_kv(b - 1)
                    dve.wait_ge(q_exp, n + 1)
                    nc.vector.scalar_tensor_tensor(q_all[:, bass.ds(n * C, C), :], exp_q, 1.0, PA[:, :, :],
                                                   ALU.min, ALU.max).then_inc(q_done, 1)
                    if not (last and g == G - 1):
                        t1(n + 1, g + 1)

            def copy_g(b):
                dve.wait_ge(g_mm, (b + 1) * G)
                ge(dve, kv_done, 2 * C * b)
                ge(dve, gt_mm, b)
                nc.vector.tensor_copy(g_sb[:, :, :], PG[:, :, 0:D + 1]).then_inc(g_copied, 1)

            def batch_kv(b):
                dve.wait_ge(kv_mm, b + 1)
                for c in range(C):
                    nc.vector.scalar_tensor_tensor(kv_tmp[:, c, :], bv_rows[:, c * P:(c + 1) * P], g_sb[:, c, D:D + 1],
                                                   PG[:, c, D:D + P], ALU.mult, ALU.add).then_inc(kv_step, 1)
                for c in range(C):
                    dve.wait_ge(kv_step, C * b + c + 1)
                    dst = kv_all[:, bass.ds(b * C + c, 1), :]
                    nc.vector.tensor_tensor(dst[:, :, 0:P].rearrange("p o (h e) -> p (o h) e", e=HD),
                                            kv_tmp[:, c, :].rearrange("p (h e) -> p h e", e=HD),
                                            head_mask[:, :].rearrange("p (h o) -> p h o", o=1).to_broadcast([P, HC, HD]),
                                            ALU.mult).then_inc(kv_done, 1)
                    nc.vector.tensor_scalar(dst[:, :, P:KVW].rearrange("p o h -> p (o h)"), head_mask[:, :],
                                            g_sb[:, c, D:D + 1], None, ALU.mult).then_inc(kv_done, 1)

            pass1(0, False)
            with dve.Fori(1, B - 1) as b:
                pass1(b, False)
            pass1(B - 1, True)
            copy_g(B - 1)
            batch_kv(B - 1)

            dve.wait_ge(flag_ready, 1)
            routed = dve.value_load(routed_flag[0:1, 0:1], min_val=0, max_val=1)

            def run_experts(k, p, tiles, x_of, y, h):
                with dve.If(routed > 0):
                    dve.wait_ge(r_logits, k + 1)
                    nc.vector.tensor_copy(r_lg[0:p, 0:tiles, :], PT[0:p, 0, 0:tiles * NE].rearrange("p (t e) -> p t e", e=NE)).then_inc(r_step, 1)
                    ge_apart(dve, "dve", r_step, 4 * k + 1)
                    for t in range(tiles):
                        last = nc.vector.max(r_top[0:p, t, :], r_lg[0:p, t, :])
                    last.then_inc(r_step, 1)
                    dve.wait_ge(r_step, 4 * k + 2)
                    nc.vector.tensor_tensor(r_gap[0:p, 0, 0:tiles], r_top[0:p, 0:tiles, 1], r_top[0:p, 0:tiles, 0],
                                            ALU.subtract).then_inc(r_gap_ready, 1)
                    dve.wait_ge(r_exp, k + 1)
                    nc.vector.tensor_scalar(r_gap[0:p, 2, 0:tiles], r_gap[0:p, 1, 0:tiles], 1.0, None, ALU.add).then_inc(r_step, 1)
                    dve.wait_ge(r_step, 4 * k + 3)
                    nc.vector.tensor_scalar(r_gap[0:p, 3, 0:tiles], r_gap[0:p, 2, 0:tiles], 1.0, None, ALU.is_le).then_inc(r_step, 1)
                    dve.wait_ge(r_step, 4 * k + 4)
                    for t in range(tiles):
                        last = nc.vector.tensor_scalar(probs[0:p, :, t], r_lg[0:p, t, :], r_top[0:p, t, 0:1],
                                                       r_gap[0:p, 3, t:t + 1], ALU.is_ge, ALU.mult)
                    last.then_inc(r_turn, 1)
                    with dve.Fori(0, NE) as e:
                        dve.wait_ge(r_relu, k * NE + e + 1)
                        nc.vector.tensor_tensor(h, h, h, ALU.mult).then_inc(r_sq, 1)
                        dve.wait_ge(r_y, k * NE + e + 1)
                        dve.wait_ge(r_turn, k * (NE + 1) + e + 1)
                        for t in range(tiles):
                            x = x_of(t)
                            last = nc.vector.scalar_tensor_tensor(x, y[0:p, t:t + 1, :], probs[0:p, bass.ds(e, 1), t], x,
                                                                  ALU.mult, ALU.add)
                        last.then_inc(r_turn, 1)
                    ge_apart(dve, "dve", r_turn, (k + 1) * (NE + 1))

            dve.wait_ge(norm1, T * NG)
            dve.wait_ge(g_mm, NG)

            def step(g, b):
                i, n, _ = lagged(g, b, 0)
                r, nr, _ = lagged(g, b, 1)
                u, nu, _ = lagged(g, b, 2)
                v, nv, bv_ = lagged(g, b, 3)
                if runs(i):
                    regions = ((6, 2, PT[:, 0, 0:2 * KVW]), (0, 3, PA[:, 0, 0:3 * KVW]), (3, 3, PA[:, 1, 0:3 * KVW]))
                    dve.wait_ge(o_mm, i + 1)
                    for k0, nb, reg in regions:
                        last = nc.vector.tensor_scalar(norm_sb[:, k0:k0 + nb, :], reg.rearrange("p (k w) -> p k w", w=KVW)[:, :, P:KVW],
                                                       NORM_EPS, None, ALU.max)
                    last.then_inc(o_max, 1)
                    dve.wait_ge(o_max, i + 1)
                    nc.vector.reciprocal(norm_inv[:, :, :], norm_sb[:, :, :]).then_inc(o_inv, 1)
                    dve.wait_ge(o_inv, i + 1)
                    ge(dve, ot_mm, i)
                    for k0, nb, reg in regions:
                        nc.vector.tensor_tensor(o_tok[:, k0:k0 + nb, :].rearrange("p k (h e) -> p k h e", e=HD),
                                                reg.rearrange("p (k w) -> p k w", w=KVW)[:, :, 0:P].rearrange("p k (h e) -> p k h e", e=HD),
                                                norm_inv[:, k0:k0 + nb, :].unsqueeze(3).to_broadcast([P, nb, HC, HD]),
                                                ALU.mult).then_inc(o_done, 1)
                if runs(u):
                    stats(nu, 1, u, bn3, stat3, rstd3)
                if runs(v):
                    dve.wait_ge(f4_mm, v + 1)
                    ge(dve, stored, 16 * v)
                    nc.vector.tensor_tensor(x_out, four(PB), x_group(nv), ALU.add).then_inc(f4_added, 1)
                    ge_apart(dve, "dve", f4_added, v + 1)
                    run_experts(routed_ordinal(g, b, 0), P, T, lambda t: x_out[:, t:t + 1, :], four(PB), h3)
                attention_b(g, b, "before x")
                if runs(r):
                    dve.wait_ge(f1_relu, r + 1)
                    nc.vector.tensor_tensor(h2, h2, h2, ALU.mult).then_inc(f1_sq, 1)
                attention_b(g, b, "x")
                if runs(i):
                    dve.wait_ge(w_mm, i + 1)
                    dve.wait_ge(bo_added, NG)
                    nc.vector.tensor_tensor(x_group(n), four(PB), x_group(n), ALU.add).then_inc(w_added, 1)
                    dve.wait_ge(w_added, i + 1)
                    stats(n, 0, i, bn2, stat2, rstd2)
                if runs(r):
                    dve.wait_ge(f2_mm, r + 1)
                    dve.wait_ge(ob_added, r + 1)
                    nc.vector.tensor_tensor(x_group(nr), four(PG), x_group(nr), ALU.add).then_inc(f2_added, 1)
                    ge_apart(dve, "dve", f2_added, r + 1)
                    run_experts(routed_ordinal(g, b, 1), P, T, lambda t: x_tile(nr, t), four(PG), h2)
                if runs(u):
                    dve.wait_ge(f3_relu, u + 1)
                    nc.vector.tensor_tensor(h3, h3, h3, ALU.mult).then_inc(f3_sq, 1)
                attention_b(g, b, "y")

            def heads(ap):
                return ap.rearrange("p (h e) -> p h e", e=HD)

            def over_heads(ap):
                return ap.rearrange("p (o e) -> p o e", o=1).to_broadcast([SP, H, HD])

            def over_feats(ap):
                return ap.rearrange("p (h o) -> p h o", o=1).to_broadcast([SP, H, HD])

            def over_keys(ap):
                return ap.rearrange("p (h o) -> p h o", o=1).to_broadcast([SP, H, SP])

            def mean_var(src):
                link(nc.vector.bn_stats(s_bn, src))
                nc.vector.bn_aggr(s_mv, s_bn).then_inc(c_stat, 1)

            def scale_shift(dst, src, k):
                dve.wait_ge(c_stat, k + 1)
                dve.wait_ge(c_rstd, k + 1)
                link(nc.vector.tensor_scalar(dst, src, s_mv[:, 0:1], s_rs[:, 1:2], ALU.subtract, ALU.mult))

            def transposed_weight(i, bank):
                dve.wait_ge(c_wt, i + 1)
                nc.vector.tensor_copy(w4t[i], bank.rearrange("p (c n) -> p c n", c=C)).then_inc(c_wt_sb, 1)

            def turn(it, k, ins):
                ins.then_inc(c_turn, 1)
                dve.wait_ge(c_turn, it * TURNS + k)

            TURNS = 10

            def center16(step_):
                step_(1, nc.vector.reduce_sum(st16[0], heads(lin), AX))
                step_(2, nc.vector.tensor_scalar(st16[1], st16[0], 1.0 / HD, None, ALU.mult))
                step_(3, nc.vector.tensor_tensor(heads(cen), heads(lin), over_feats(st16[1]), ALU.subtract))
                step_(4, nc.vector.tensor_tensor(sq16, cen, cen, ALU.mult))
                nc.vector.reduce_sum(st16[2], heads(sq16), AX).then_inc(c_var, 1)

            def prepare(b, place):
                if place == "x" and b in (0, 1):
                    transposed_weight(2 * b, PA[:, 1, :])
                if (b, place) == (0, "y"):
                    dve.wait_ge(c_vecs, 16 * (10 + 3 * HC))
                    for rows16, blk in zip(l_rows, l_blk):
                        nc.vector.tensor_tensor(blk.rearrange("p (h e) -> p h e", e=HD),
                                                rows16.rearrange("p (o e) -> p o e", o=1).to_broadcast([P, HC, HD]),
                                                head_mask[:, :].rearrange("p (h o) -> p h o", o=1).to_broadcast([P, HC, HD]),
                                                ALU.mult).then_inc(c_blk, 1)
                elif (b, place) == (1, "before x"):
                    dve.wait_ge(c_xs, 16 * B)
                    link(nc.vector.tensor_tensor(xs, xs, ob_b, ALU.subtract))
                    mean_var(xs)
                elif (b, place) == (1, "x"):
                    scale_shift(zs, xs, 0)
                    mean_var(zs)
                elif (b, place) == (1, "y"):
                    dve.wait_ge(c_lt, 1)
                    nc.vector.tensor_copy(l_bdt_all, PG[:, 1, 0:3 * P]).then_inc(c_lt_sb, 1)
                elif (b, place) == (2, "before x"):
                    scale_shift(zz, zs, 1)
                    nc.vector.tensor_tensor(za, zz, lna_b, ALU.mult).then_inc(c_z, 1)
                    nc.vector.tensor_tensor(zb, zz, lnb_b, ALU.mult).then_inc(c_z, 1)
                elif (b, place) == (2, "x"):
                    dve.wait_ge(c_zt, 1)
                    nc.vector.tensor_copy(za_t, chunked(PA[:, 1, 0:C * SP])).then_inc(c_zt_sb, 1)
                    nc.vector.tensor_copy(zb_t, chunked(PA[:, 1, C * SP:2 * C * SP])).then_inc(c_zt_sb, 1)
                    dve.wait_ge(c_wt, 4)
                    link(nc.vector.tensor_scalar(neg_mask.rearrange("p (b s) -> p b s", s=SPT),
                                                 head_mask[0:SP, 0:B].rearrange("p (b o) -> p b o", o=1).to_broadcast([SP, B, SPT]),
                                                 1.0, 1e30, ALU.subtract, ALU.mult))
                elif (b, place) == (2, "y"):
                    dve.wait_ge(c_qkv, 1)
                    for c in range(C):
                        nc.vector.tensor_copy(k_t[:, c, :], PG[:, 0, (C + c) * SP:(C + c + 1) * SP]).then_inc(c_kv_sb, 1)
                        nc.vector.tensor_scalar(v_t[:, c, :], PG[:, 0, (2 * C + c) * SP:(2 * C + c + 1) * SP], vb_col[:, c:c + 1],
                                                None, ALU.add).then_inc(c_kv_sb, 1)
                        last = nc.vector.tensor_scalar(qcur_t[:, c, :], PG[:, 0, c * SP:(c + 1) * SP], qb_col[:, c:c + 1], None, ALU.add)
                    last.then_inc(c_q_sb, 1)
                elif (b, place) == (3, "x"):
                    dve.wait_ge(c_klin, 1)
                    link(nc.vector.tensor_tensor(heads(vi), heads(PA[0:SP, 1, D:2 * D]), over_heads(lvb_b), ALU.add))
                    nc.vector.tensor_tensor(heads(lin), heads(PA[0:SP, 1, 0:D]), over_heads(lkb_b), ALU.add).then_inc(c_klin_read, 1)
                    dve.wait_ge(c_klin_read, 1)
                    center16(lambda k, ins: link(ins))
                    nc.vector.memset(out_cur, 0.0).then_inc(c_out_zero, 1)
                elif (b, place) == (3, "y"):
                    dve.wait_ge(c_rstd16, 1)
                    link(nc.vector.tensor_tensor(heads(cen), heads(cen), over_feats(st16[3]), ALU.mult))
                    nc.vector.tensor_tensor(heads(kn), heads(cen), over_heads(lnd_b), ALU.mult).then_inc(c_kn, 1)
                    dve.wait_ge(c_knt, 1)
                    for c in range(C):
                        nc.vector.tensor_tensor(kn_mask[c].rearrange("p (h s) -> p h s", s=SP),
                                                PG[:, 0, c * SP:(c + 1) * SP].rearrange("p (o s) -> p o s", o=1).to_broadcast([P, HC, SP]),
                                                head_mask[:, :].rearrange("p (h o) -> p h o", o=1).to_broadcast([P, HC, SP]),
                                                ALU.mult).then_inc(c_kmask, 1)

            def attention_b(g, b, place):
                it = iteration(g)
                last_one = isinstance(g, int)
                if it is None:
                    if g == 1:
                        prepare(b, place)
                    return
                lgh = lg.rearrange("p (h s) -> p h s", s=SP)
                prh = pr.rearrange("p (h s) -> p h s", s=SP)
                if (b, place) == (0, "x"):
                    if last_one:
                        stop_after_second()
                    dve.wait_ge(c_qlin, it + 1)
                    nc.vector.tensor_tensor(heads(lin), heads(PA[0:SP, 1, 0:D]), over_heads(lqb_b), ALU.add).then_inc(c_lin, 1)
                    dve.wait_ge(c_lin, it + 1)
                    center16(lambda k, ins: turn(it, k, ins))
                elif (b, place) == (1, "before x"):
                    dve.wait_ge(c_rstd16, it + 2)
                    turn(it, 5, nc.vector.tensor_tensor(heads(cen), heads(cen), over_feats(st16[3]), ALU.mult))
                    nc.vector.tensor_tensor(heads(qn), heads(cen), over_heads(lnc_b), ALU.mult).then_inc(c_qn, 1)
                elif (b, place) == (1, "x"):
                    dve.wait_ge(c_qnt, it + 1)
                    nc.vector.tensor_copy(qn_t, chunked(PA[:, 1, 0:C * SP])).then_inc(c_qnt_sb, 1)
                elif (b, place) == (1, "y"):
                    dve.wait_ge(c_logit, it + 1)
                    nc.vector.scalar_tensor_tensor(lgh, PG[0:SP, :, :].rearrange("p b (h s) -> p (b h) s", s=SP), HD ** -0.5,
                                                   neg_mask.rearrange("p (o s) -> p o s", o=1).to_broadcast([SP, H, SP]),
                                                   ALU.mult, ALU.add).then_inc(c_scaled, 1)
                elif (b, place) == (2, "before x"):
                    dve.wait_ge(c_scaled, it + 1)
                    turn(it, 6, nc.vector.reduce_max(mx16, lgh, AX))
                    nc.vector.tensor_tensor(lgh, lgh, over_keys(mx16), ALU.subtract).then_inc(c_lg, 1)
                elif (b, place) == (3, "before x"):
                    dve.wait_ge(c_pr, it + 1)
                    turn(it, 7, nc.vector.reduce_sum(sum16, prh, AX))
                    turn(it, 8, nc.vector.reciprocal(inv16, sum16))
                    dve.wait_ge(c_out_zero, 1)
                    turn(it, 9, nc.vector.tensor_copy(out_prev, out_cur))
                elif (b, place) == (3, "x"):
                    dve.wait_ge(c_pv, it + 1)
                    nc.vector.tensor_tensor(heads(out_cur), heads(PA[0:SP, 1, 0:D]), over_feats(inv16), ALU.mult).then_inc(c_outs, 1)
                    dve.wait_ge(c_outs, it + 1)
                    if not last_one:
                        turn(it, 10, nc.vector.tensor_tensor(dif, out_cur, out_prev, ALU.subtract))
                        nc.vector.tensor_reduce(dsum[0:SP, 0:1], dif, AX, ALU.add, apply_absolute_value=True).then_inc(c_dsum, 1)
                elif (b, place) == (3, "y") and not last_one:
                    dve.wait_ge(c_outt, it + 1)
                    nc.vector.tensor_tensor(qcur_t, chunked(PG[:, 0, 0:C * SP]), qcur_t, ALU.add).then_inc(c_q_sb, 1)

            def stop_after_second():
                dve.wait_ge(c_diff, 1)
                link(nc.vector.tensor_scalar(dsum[0:SP, 1:2], PA[0:SP, 1, D:D + 1], 1.0 / (B * S * D), None, ALU.mult))
                link(nc.vector.tensor_scalar(dsum[0:SP, 2:3], dsum[0:SP, 1:2], FACTOR, THRESH, ALU.mult, ALU.add))
                link(nc.vector.tensor_tensor(dsum[0:SP, 3:4], dsum[0:SP, 1:2], dsum[0:SP, 2:3], ALU.is_lt))
                link(nc.vector.tensor_scalar(dsum[0:SP, 4:5], dsum[0:SP, 3:4], -1.0, 1.0, ALU.mult, ALU.add))

            for g in range(2):
                for b in range(B):
                    step(g, b)
            with dve.Fori(2, G) as g:
                for b in range(B):
                    step(g, b)
            for b in range(B):
                step(G, b)

            link(nc.vector.tensor_scalar(tmpd, out_prev, dsum[0:SP, 3:4], None, ALU.mult))
            nc.vector.scalar_tensor_tensor(att, out_cur, dsum[0:SP, 4:5], tmpd, ALU.mult, ALU.add).then_inc(c_att, 1)
            dve.wait_ge(c_att_t, 1)
            nc.vector.tensor_copy(att_t, PT[:, 1, 0:C * SP].rearrange("p (c n) -> p c n", c=C)).then_inc(c_att_t_sb, 1)
            dve.wait_ge(c_proj, 1)
            link(nc.vector.tensor_tensor(tmpd, PB[0:SP, 0, 0:D], ob_b, ALU.add))
            link(nc.vector.tensor_tensor(xs, xs, tmpd, ALU.add))
            mean_var(xs)
            dve.wait_ge(c_stat, 3)
            dve.wait_ge(c_rstd, 3)
            nc.vector.tensor_scalar(zs, xs, s_mv[:, 0:1], s_rs[:, 1:2], ALU.subtract, ALU.mult).then_inc(c_z, 1)
            dve.wait_ge(c_zt, 2)
            nc.vector.tensor_copy(xs_t, PT[:, 0, 0:C * SP].rearrange("p (c n) -> p c n", c=C)).then_inc(c_zt_sb, 1)
            dve.wait_ge(c_relu, 1)
            nc.vector.tensor_tensor(h_s, h_s, h_s, ALU.mult).then_inc(c_sq, 1)
            dve.wait_ge(c_ffn, 1)
            link(nc.vector.tensor_tensor(x_s_out, PB[0:SP, 1, 0:D], xs, ALU.add))
            run_experts(2 * NG, SP, 1, lambda t: x_s_out.rearrange("p (t d) -> p t d", t=1), four(PB)[:, 2:3, :], h_s)
            nc.vector.tensor_copy(dsum[0:SP, 7:8], x_s_out[:, 0:1]).then_inc(c_final, 1)

        @block.tensor
        def _(pe):
            mm = nc.tensor.matmul

            def t1(n, g):
                pe.wait_ge(norm1, T * (n + 1))
                ge(pe, t1_lo, n)
                for c in range(C):
                    for t in range(T):
                        last = nc.tensor.transpose(PT[:, c, t * P:(t + 1) * P], xn[g % 2][:, t, c * P:(c + 1) * P], ident[:, :])
                last.then_inc(t1_mm, 1)

            def column_norms():
                pe.wait_ge(wr_sq, 1)
                for c in range(C):
                    last = mm(PG[0:P, 0, 0:NE], ones_f[:, :], wr_tmp[:, c * NE:(c + 1) * NE], start=(c == 0), stop=(c == C - 1))
                last.then_inc(wr_sum, 1)

            pe.wait_ge(consts, 5)
            t1(0, 0)
            column_norms()
            pe.wait_ge(setup_dve, 4)
            pe.wait_ge(bias_ready, 1)

            def k_product(n, g):
                pe.wait_ge(t1_lo, n + 1)
                ge(pe, k_done, n)
                for t in range(T):
                    dst = four(PB)[:, t, :]
                    mm(dst, ones_row[:, 0:P], bias3[:, D:2 * D], start=True, stop=False)
                    for c in range(C):
                        hi, lo = (x[:, c, t * P:(t + 1) * P] for x in (xt_hi, xt_lo))
                        mm(dst, hi, wk_hi[:, c, :], start=False, stop=False)
                        mm(dst, hi, wk_lo[:, c, :], start=False, stop=False)
                        last = mm(dst, lo, wk_hi[:, c, :], start=False, stop=(c == C - 1))
                last.then_inc(k_mm, 1)

            def q_product(n, g):
                ge(pe, q_done, n)
                for o in range(C):
                    dst, cols = PA[:, o, :], slice(o * P, (o + 1) * P)
                    mm(dst, bias3[:, cols], ones_row[:, :], start=True, stop=False)
                    for c in range(C):
                        hi, lo = xt_hi[:, c, :], xt_lo[:, c, :]
                        mm(dst, wq_hi[:, c, cols], hi, start=False, stop=False)
                        mm(dst, wq_hi[:, c, cols], lo, start=False, stop=False)
                        last = mm(dst, wq_lo[:, c, cols], hi, start=False, stop=(c == C - 1))
                last.then_inc(q_mm, 1)

            def g_product(n, g):
                pe.wait_ge(k_done, n + 1)
                for t in range(T):
                    for c in range(C):
                        last = mm(PG[:, c, 0:D + 1], k_tok[:, t, c * P:(c + 1) * P], xn[g % 2][:, t, :],
                                  start=(g == 0 and t == 0), stop=(g == G - 1 and t == T - 1))
                last.then_inc(g_mm, 1)

            def g_transposes(b):
                pe.wait_ge(g_copied, b + 1)
                for i in range(C):
                    for c in range(C):
                        last = nc.tensor.transpose(PG[:, i, c * P:(c + 1) * P], g_sb[:, c, i * P:(i + 1) * P], ident[:, :])
                last.then_inc(gt_mm, 1)

            def kv_product(b):
                pe.wait_ge(gt_copied, b + 1)
                for c in range(C):
                    for i in range(C):
                        last = mm(PG[:, c, D:D + P], g_t[:, i, c * P:(c + 1) * P], wv[:, i, c * P:(c + 1) * P],
                                  start=(i == 0), stop=(i == C - 1))
                last.then_inc(kv_mm, 1)

            def pass1(b, last):
                for g in range(G):
                    n = b * G + g
                    later_batch = g == 0 and not (isinstance(b, int) and b == 0)
                    k_product(n, g)
                    if later_batch:
                        g_transposes(b - 1)
                    q_product(n, g)
                    if later_batch:
                        kv_product(b - 1)
                    if not (last and g == G - 1):
                        t1(n + 1, g + 1)
                    if g == 0 and later_batch:
                        pe.wait_ge(kv_done, 2 * C * b)
                    elif g == 0:
                        pe.wait_ge(flag_ready, 1)
                    g_product(n, g)

            pass1(0, False)
            with pe.Fori(1, B - 1) as b:
                pass1(b, False)
            pass1(B - 1, True)
            g_transposes(B - 1)
            kv_product(B - 1)

            pe.wait_ge(flag_ready, 1)
            routed = pe.value_load(routed_flag[0:1, 0:1], min_val=0, max_val=1)

            def run_experts(k, p, tiles, xt, y, h, free):
                with pe.If(routed > 0):
                    for s, v in free:
                        ge(pe, s, v)
                    for t in range(tiles):
                        for c in range(C):
                            last = mm(PT[0:p, 0, t * NE:(t + 1) * NE], xt[:, c, t * P:t * P + p], wr[:, c, :],
                                      start=(c == 0), stop=(c == C - 1))
                    last.then_inc(r_logits, 1)
                    with pe.Fori(0, NE) as e:
                        pe.wait_ge(r_w, 32 * (k * NE + e + 1))
                        for c in range(C):
                            last = mm(PT[:, 1, 0:tiles * p], w1e[:, c, :], xt[:, c, :], start=(c == 0), stop=(c == C - 1))
                        last.then_inc(r_hid, 1)
                        pe.wait_ge(r_sq, k * NE + e + 1)
                        for t in range(tiles):
                            last = mm(y[0:p, t, :], h[:, t * P:t * P + p], w2e[:, :], start=True, stop=True)
                        last.then_inc(r_y, 1)
                    pe.wait_ge(r_turn, (k + 1) * (NE + 1))

            pe.wait_ge(kv_done, 2 * C * B)
            pe.wait_ge(q_done, NG)
            pe.wait_ge(k_done, NG)

            def transposes(dst, src, done):
                for c in range(C):
                    for t in range(T):
                        last = nc.tensor.transpose(dst[:, c, t * P:(t + 1) * P], src[:, t, c * P:(c + 1) * P], ident[:, :])
                last.then_inc(done, 1)

            def hidden(dst, xt, done, copied, before, each):
                for c in range(C):
                    if c == 0 or each:
                        pe.wait_ge(copied, before + c + 1)
                    last = mm(dst, ws1[:, c, :], xt[:, c, :], start=(c == 0), stop=(c == C - 1))
                last.then_inc(done, 1)

            def down(pair, h, done):
                for t in range(T):
                    last = mm(four(pair)[:, t, :], h[:, t * P:(t + 1) * P], ws2[:, :], start=True, stop=True)
                last.then_inc(done, 1)

            def step(g, b):
                i, r, u, v = (lagged(g, b, back)[0] for back in range(4))
                if runs(i):
                    pe.wait_ge(q_copied, i + 1)
                    ge(pe, f1_relu, i - 1)
                    ge(pe, t3_done, i - 2)
                    for k in (0, 1, 2, 6, 7, 3, 4, 5):
                        t, c = k // C, k % C
                        if k == 3:
                            ge(pe, f3_relu, i - 2)
                        dst = PA[:, k // 3, (k % 3) * KVW:(k % 3 + 1) * KVW] if k < 6 else PT[:, 0, (k - 6) * KVW:(k - 5) * KVW]
                        last = mm(dst, q_cur[b % 2][:, c, t * P:(t + 1) * P], kv_all[:, b * C + c, :], start=True, stop=True)
                    last.then_inc(o_mm, 1)
                if runs(v):
                    pe.wait_ge(f3_sq, v + 1)
                    ge(pe, w_added, min(i, NG) if isinstance(i, int) else i)
                    down(PB, h3, f4_mm)
                    run_experts(routed_ordinal(g, b, 0), P, T, x3t, four(PB), h3,
                                [(f4_added, v + 1), (t3_done, v + 1)] + ([(o_done, 3 * (i + 1))] if runs(i) else []))
                if runs(r):
                    pe.wait_ge(norm2, T * (r + 1))
                    ge(pe, t3_done, i - 2)
                    if runs(i):
                        pe.wait_ge(o_done, 3 * i + 1)
                    transposes(PT, y2, t2_mm)
                if runs(i):
                    pe.wait_ge(o_done, 3 * (i + 1))
                    ge(pe, f2_added, i - 1)
                    attention_b_has_read(g, b, "y")
                    for c in range(C):
                        for t in range(T):
                            last = nc.tensor.transpose(PG[:, c, t * P:(t + 1) * P], o_tok[:, t * C + c, :], ident[:, :])
                    last.then_inc(ot_mm, 1)
                if runs(r):
                    hidden(PA[:, 0, :], x2t, f1_mm, t2_done, C * r, 1)
                attention_b(g, b, "x")
                if runs(i):
                    pe.wait_ge(ot_done, i + 1)
                    ge(pe, f4_added, i - 2)
                    for t in range(T):
                        dst = four(PB)[:, t, :]
                        for c in range(C):
                            last = mm(dst, o_t[:, c, t * P:(t + 1) * P], wo[:, c, :], start=(c == 0), stop=(c == C - 1))
                    last.then_inc(w_mm, 1)
                if runs(u):
                    pe.wait_ge(norm3, T * (u + 1))
                    if runs(r):
                        pe.wait_ge(t2_done, C * (r + 1))
                    transposes(PT, y3, t3_mm)
                if runs(r):
                    pe.wait_ge(f1_sq, r + 1)
                    if runs(i):
                        pe.wait_ge(ot_done, i + 1)
                    ge(pe, f2_added, r)
                    down(PG, h2, f2_mm)
                    run_experts(routed_ordinal(g, b, 1), P, T, x2t, four(PG), h2,
                                [(f2_added, r + 1)] + ([(t3_done, u + 1)] if runs(u) else [(t2_done, C * (r + 1))]))
                if runs(u):
                    attention_b_has_read(g, b, "x")
                    hidden(PA[:, 1, :], x3t, f3_mm, t3_done, u, 0)
                attention_b(g, b, "y")

            def special_transposes(dst, src):
                for c in range(C):
                    last = nc.tensor.transpose(dst[:, c * SP:(c + 1) * SP], src[:, c * P:(c + 1) * P], ident[0:SP, 0:SP])
                return last

            def weight_transposes(w, bank):
                pe.wait_ge(c_wts, 16 * 4)
                for i in range(C):
                    for o in range(C):
                        last = nc.tensor.transpose(bank[:, i * D + o * P:i * D + (o + 1) * P], raw4[w][:, o, i * P:(i + 1) * P], ident[:, :])
                last.then_inc(c_wt, 1)

            def prepare(b, place):
                if place == "x" and b < 2:
                    weight_transposes(2 * b, PA[:, 1, :])
                elif place == "y" and b < 2:
                    weight_transposes(2 * b + 1, PG[:, 0, :])
                    if b == 1:
                        pe.wait_ge(c_blk, 3)
                        for i in range(3):
                            last = nc.tensor.transpose(PG[:, 1, i * P:(i + 1) * P], l_blk[i], ident[:, :])
                        last.then_inc(c_lt, 1)
                elif (b, place) == (2, "x"):
                    pe.wait_ge(c_z, 2)
                    special_transposes(PA[:, 1, 0:C * SP], za)
                    special_transposes(PA[:, 1, C * SP:2 * C * SP], zb).then_inc(c_zt, 1)
                elif (b, place) == (2, "y"):
                    pe.wait_ge(c_wt_sb, 4)
                    pe.wait_ge(c_zt_sb, 2)
                    for w, zt in enumerate((za_t, zb_t, zb_t)):
                        for o in range(C):
                            for i in range(C):
                                last = mm(PG[:, 0, (w * C + o) * SP:(w * C + o + 1) * SP], w4t[w][:, i, o * P:(o + 1) * P], zt[:, i, :],
                                          start=(i == 0), stop=(i == C - 1))
                    last.then_inc(c_qkv, 1)
                elif (b, place) == (3, "x"):
                    pe.wait_ge(c_lt_sb, 1)
                    pe.wait_ge(c_kv_sb, 2 * C)
                    for k, src, bd in ((0, k_t, l_bdt[1]), (1, v_t, l_bdt[2])):
                        for c in range(C):
                            last = mm(PA[0:SP, 1, k * D + c * P:k * D + (c + 1) * P], src[:, c, :], bd, start=True, stop=True)
                    last.then_inc(c_klin, 1)
                elif (b, place) == (3, "y"):
                    pe.wait_ge(c_kn, 1)
                    special_transposes(PG[:, 0, 0:C * SP], kn).then_inc(c_knt, 1)
                    pe.wait_ge(c_kmask, C)

            def attention_b(g, b, place):
                def wait(s, v):
                    ge_apart(pe, "pe", s, v)

                it = iteration(g)
                last_one = isinstance(g, int)
                i = g * B + b
                if it is None and g == 0:
                    return
                if place == "x":
                    wait(f3_relu, min(i - 2, NG) if isinstance(i, int) else i - 2)
                else:
                    wait(f2_added, min(i, NG) if isinstance(i, int) else i)
                if it is None:
                    prepare(b, place)
                elif (b, place) == (0, "x"):
                    wait(c_q_sb, it + 1)
                    for c in range(C):
                        last = mm(PA[0:SP, 1, c * P:(c + 1) * P], qcur_t[:, c, :], l_bdt[0], start=True, stop=True)
                    last.then_inc(c_qlin, 1)
                    if last_one:
                        pe.wait_ge(c_dsum, ITERS - 1)
                        mm(PA[0:SP, 1, D:D + 1], ones_f[0:SP, 0:SP], dsum[0:SP, 0:1], start=True, stop=True).then_inc(c_diff, 1)
                elif (b, place) == (1, "x"):
                    wait(c_qn, it + 1)
                    special_transposes(PA[:, 1, 0:C * SP], qn).then_inc(c_qnt, 1)
                elif (b, place) == (1, "y"):
                    wait(c_qnt_sb, it + 1)
                    for c in range(C):
                        last = mm(PG[0:SP, c, :], qn_t[:, c, :], kn_mask[c], start=True, stop=True)
                    last.then_inc(c_logit, 1)
                elif (b, place) == (2, "y"):
                    wait(c_pr, it + 1)
                    for h in range(H):
                        last = nc.tensor.transpose(PG[0:SP, h // HC, (h % HC) * SP:(h % HC + 1) * SP], pr[:, h * SP:(h + 1) * SP],
                                                   ident[0:SP, 0:SP])
                    last.then_inc(c_prt, 1)
                elif (b, place) == (3, "x"):
                    wait(c_prt_sb, it + 1)
                    for h in range(H):
                        last = mm(PA[0:SP, 1, h * HD:(h + 1) * HD], pr_t[:, h * SP:(h + 1) * SP], vi[:, h * HD:(h + 1) * HD],
                                  start=True, stop=True)
                    last.then_inc(c_pv, 1)
                elif (b, place) == (3, "y") and not last_one:
                    wait(c_outs, it + 1)
                    special_transposes(PG[:, 0, 0:C * SP], out_cur).then_inc(c_outt, 1)

            def attention_b_has_read(g, b, place):
                it = iteration(g)
                if it is None and g == 0:
                    return
                if place == "x":
                    if it is None:
                        s, v = ((c_wt_sb, 1), (c_wt_sb, 3), (c_zt_sb, 2), (c_klin_read, 1))[b]
                    else:
                        s, v = ((c_lin, it + 1), (c_qnt_sb, it + 1), (c_qnt_sb, it + 1), (c_outs, it + 1))[b]
                elif it is None:
                    if b == 0:
                        return
                    s, v = (None, (c_wt_sb, 2), (c_wt_sb, 4), (c_q_sb, 1))[b]
                    if b == 2:
                        pe.wait_ge(c_lt_sb, 1)
                else:
                    s, v = ((c_q_sb, it + 1), (c_q_sb, it + 1), (c_scaled, it + 1), (c_prt_sb, it + 1))[b]
                pe.wait_ge(s, v)

            for g in range(2):
                for b in range(B):
                    step(g, b)
            with pe.Fori(2, G) as g:
                for b in range(B):
                    step(g, b)
            for b in range(B):
                step(G, b)

            pe.wait_ge(f4_added, NG)
            pe.wait_ge(c_att, 1)
            special_transposes(PT[:, 1, 0:C * SP], att).then_inc(c_att_t, 1)
            pe.wait_ge(c_att_t_sb, 1)
            for i in range(C):
                last = mm(PB[0:SP, 0, 0:D], att_t[:, i, :], w4t[3][:, i, :], start=(i == 0), stop=(i == C - 1))
            last.then_inc(c_proj, 1)
            pe.wait_ge(c_z, 3)
            special_transposes(PT[:, 0, 0:C * SP], zs).then_inc(c_zt, 1)
            pe.wait_ge(c_zt_sb, 3)
            for c in range(C):
                last = mm(PA[:, 1, 0:SP], ws1[:, c, :], xs_t[:, c, :], start=(c == 0), stop=(c == C - 1))
            last.then_inc(c_hid, 1)
            pe.wait_ge(c_sq, 1)
            mm(PB[0:SP, 1, 0:D], h_s, ws2[:, :], start=True, stop=True).then_inc(c_ffn, 1)
            run_experts(2 * NG, SP, 1, xs_t, four(PB)[:, 2:3, :], h_s, [])


_NAMES = ["inputs_q", "Wq", "bq", "Wk", "bk", "Wv", "bv", "Wo", "bo"]
_NAMES_B = ["qw", "qb", "kw", "vw", "vb", "ow", "ob", "lna_w", "lnb_w", "lnc_w", "lnd_w", "lqw", "lqb", "lkw", "lkb", "lvw", "lvb"]
_NAMES_F = ["Ws1", "Ws2", "W1", "W2", "Wr"]
_INS = [f"L0_attn_a_{n}" for n in _NAMES] + [f"L0_attn_b_{n}" for n in _NAMES_B] + [f"L0_ffn_{n}" for n in _NAMES_F]


def kernel(**inputs):
    import numpy as _np
    import concourse.bacc as _bacc
    from concourse import mybir as _mybir
    from concourse.bass_utils import run_bass_kernel_spmd as _run

    nc = _bacc.Bacc("TRN2", target_bir_lowering=False, num_devices=1)
    arrays, args = {}, []
    for name in _INS:
        a = _np.ascontiguousarray(inputs[name])
        arrays[f"in_{name}_dram"] = a
        args.append(nc.dram_tensor(f"in_{name}_dram", a.shape, _mybir.dt.from_np(a.dtype), kind="ExternalInput").ap())
    args.append(nc.dram_tensor("out_0_dram", (B, S, D), _mybir.dt.float32, kind="ExternalOutput").ap())
    hybrid_kernel(nc, *args)
    r = _run(nc, [arrays], core_ids=[0])
    return r.results[0]["out_0_dram"]
```

```python
from contextlib import ExitStack

import concourse.bass as bass
from concourse import mybir

F32 = mybir.dt.float32
F32R = mybir.dt.float32r
BF16 = mybir.dt.bfloat16
I32 = mybir.dt.int32
ALU = mybir.AluOpType
ACT = mybir.ActivationFunctionType
AX = mybir.AxisListType.X

P = 128
B, S, D = 4, 2048, 256
C = D // P
H, HD = 16, 16
HC = H // C
T = 4
GT = T * P
G = S // GT
NG = B * G
F = 128
NE = 8
KVW = P + HC
LN_EPS = 1e-5
NORM_EPS = 1e-6
SPT = 16
SP = B * SPT
ITERS = 3
THRESH, FACTOR = 0.01, 0.1
WR_NORM2_BOUND = (16.0 / (2.0 * D ** 0.5)) ** 2


def ge(eng, sem, value):
    if isinstance(value, int) and value <= 0:
        return
    eng.wait_ge(sem, value)


def hybrid_kernel(nc, x_in, Wq, bq, Wk, bk, Wv, bv, Wo, bo, qw, qb, kw, vw, vb, ow, ob,
                  lna_w, lnb_w, lnc_w, lnd_w, lqw, lqb, lkw, lkb, lvw, lvb,
                  Ws1, Ws2, W1, W2, Wr, out):
    x_dram = x_in.rearrange("b (g t p) d -> (b g) p t d", t=T, p=P)
    out_dram = out.rearrange("b (g t p) d -> (b g) p t d", t=T, p=P)

    def rows(w):
        return w.rearrange("(c p) n -> p c n", p=P)

    def row(v):
        return v.rearrange("(o n) -> o n", o=1)

    with ExitStack() as ctx:
        def sb(name, shape, dt=F32):
            return ctx.enter_context(nc.sbuf_tensor(name, shape, dt))

        def ps(name):
            return ctx.enter_context(nc.psum_tensor(name, [P, 2, 512], F32))

        def sem(name):
            return ctx.enter_context(nc.semaphore(name))

        x_all = sb("x_all", [P, NG * T, D])
        q_all = sb("q_all", [P, NG * C, GT])
        kv_all = sb("kv_all", [P, B * C, KVW])
        ident = sb("ident", [P, P])
        head_mask = sb("head_mask", [P, HC])
        ones_row = sb("ones_row", [P, P], BF16)
        bias3 = sb("bias3", [P, D], BF16)
        bq_col = sb("bq_col", [P, C])
        ob_rows = sb("ob_rows", [P, D])
        wo_hi, wo_lo = sb("wo_hi", [P, C, D], F32R), sb("wo_lo", [P, C, D], F32R)
        o_hi, o_lo = sb("o_hi", [P, C, GT], F32R), sb("o_lo", [P, C, GT], F32R)
        ws1 = sb("ws1", [P, C, F])
        ws2 = sb("ws2", [P, D])
        wr = sb("wr", [P, C, NE])
        routed_flag = sb("routed_flag", [1, 1], I32)
        wr_tmp = sb("wr_tmp", [P, C * NE])
        wr_max = sb("wr_max", [1, 4])
        ones_f = sb("ones_f", [P, P])
        minus_half = sb("minus_half", [P, H])
        minus_one = sb("minus_one", [P, 1])
        ln_bn = sb("ln_bn", [P, 2, T, 6])
        ln_mv = sb("ln_mv", [P, 2, T, 2])
        ln_rstd = sb("ln_rstd", [P, 2, T])
        ln_shift = sb("ln_shift", [P, 2, T])
        norm_sb = sb("norm_sb", [P, T * C, HC])
        norm_inv = sb("norm_inv", [P, T * C, HC])
        g_t = sb("g_t", [P, C, D])
        probs = sb("probs", [P, NE, T])
        r_lg = sb("r_lg", [P, T, NE])
        r_top = sb("r_top", [P, T, 8])
        r_gap = sb("r_gap", [P, 4, T])

        SCR = 9 * 1024 + 8
        scratch = sb("scratch", [P, SCR])
        used = [0]

        def part(n):
            a = scratch[:, used[0]:used[0] + n]
            used[0] += n
            assert used[0] <= SCR
            return a

        xn = [part(T * (D + 1)).rearrange("p (t d) -> p t d", t=T) for _ in range(2)]
        k_tok = part(T * D).rearrange("p (t d) -> p t d", t=T)
        exp_kq = part(T * D)
        exp_k = exp_kq.rearrange("p (t d) -> p t d", t=T)
        exp_q = exp_kq.rearrange("p (c n) -> p c n", c=C)
        setup_start = used[0]
        wq_raw = part(C * D).rearrange("p (c n) -> p c n", c=C)
        wk_raw = part(C * D).rearrange("p (c n) -> p c n", c=C)
        bias_rows = part(D)
        bpart = part(D).bitcast(BF16).rearrange("p (k n) -> p k n", k=2)
        used[0] = setup_start + 2 * C * GT
        wv, wo_raw = [part(C * D).rearrange("p (c n) -> p c n", c=C) for _ in range(2)]
        bv_rows, bo_rows = part(D), part(D)
        kv_tmp = part(C * P).rearrange("p (c n) -> p c n", c=C)
        g_sb = part(C * (D + 1)).rearrange("p (c n) -> p c n", c=C)
        used[0] = 0
        o_tok = part(T * D).rearrange("p (k n) -> p k n", k=T * C)
        y2 = part(T * D).rearrange("p (t d) -> p t d", t=T)
        y3 = part(T * D).rearrange("p (t d) -> p t d", t=T)
        x2t = part(C * GT).rearrange("p (c n) -> p c n", c=C)
        used[0] = setup_start
        q_cur = [part(C * GT).rearrange("p (c n) -> p c n", c=C) for _ in range(2)]
        x3t = part(C * GT).rearrange("p (c n) -> p c n", c=C)
        h2, h3 = part(GT), part(GT)
        x_out = part(T * D).rearrange("p (t d) -> p t d", t=T)

        with ExitStack() as pass1_memory:
            def sb1(name, shape):
                return pass1_memory.enter_context(nc.sbuf_tensor(name, shape, F32R))

            wq_hi, wq_lo = sb1("wq_hi", [P, C, D]), sb1("wq_lo", [P, C, D])
            wk_hi, wk_lo = sb1("wk_hi", [P, C, D]), sb1("wk_lo", [P, C, D])
            xt_hi, xt_lo = sb1("xt_hi", [P, C, GT]), sb1("xt_lo", [P, C, GT])
        b_weights = sb("b_weights", [P, 2, 4, C * D])

        PT, PA, PB, PG = ps("PT"), ps("PA"), ps("PB"), ps("PG")

        w1e, w2e = g_t[:, 0, :].rearrange("p (c f) -> p c f", c=C), g_t[:, 1, :]

        raw4 = [b_weights[:, 0, i, :].rearrange("p (c n) -> p c n", c=C) for i in range(4)]
        w4t = [b_weights[:, 1, i, :].rearrange("p (c n) -> p c n", c=C) for i in range(4)]

        def carve(piece):
            at = [0]

            def take(n, p=P):
                a = piece[0:p, at[0]:at[0] + n]
                at[0] += n
                assert at[0] <= piece.shape[1]
                return a
            return take

        def chunked(ap):
            return ap.rearrange("p (c n) -> p c n", c=C)

        used_q = [carve(q_all[:, b * G * C:(b * G + 1) * C, :].rearrange("p k n -> p (k n)")) for b in range(B)]
        l_rows = [used_q[0](HD) for _ in range(3)]
        l_blk = [used_q[0](P) for _ in range(3)]
        l_bdt_all = used_q[0](3 * P)
        l_bdt = [l_bdt_all[:, i * P:(i + 1) * P] for i in range(3)]
        qb_col, vb_col = used_q[0](C), used_q[0](C)
        lqb_b, lkb_b, lvb_b, lnc_b, lnd_b = [used_q[0](HD, SP) for _ in range(5)]
        s_bn, s_mv, s_rs = used_q[0](6, SP), used_q[0](2, SP), used_q[0](4, SP)
        xs, zs, zz, za = [used_q[1](D, SP) for _ in range(4)]
        zb, ob_b, lna_b, lnb_b = [used_q[2](D, SP) for _ in range(4)]
        za_t, zb_t, qcur_t, k_t, v_t, qn_t, att_t, xs_t = [chunked(used_q[3](C * SP)) for _ in range(8)]
        after_raw = carve(b_weights[:, 0, :, :].rearrange("p i n -> p (i n)"))
        vi, lin, cen, sq16, kn, qn = [after_raw(D, SP) for _ in range(6)]
        neg_mask = after_raw(SP, SP)
        st16 = [after_raw(H, SP) for _ in range(4)]
        mx16, sum16, inv16 = [after_raw(H, SP) for _ in range(3)]
        dsum = after_raw(8)
        out_cur = after_raw(D, SP)
        later_q = [q_all[:, (b * G + 1) * C:(b * G + 2) * C, :].rearrange("p k n -> p (k n)") for b in range(B)]
        kn_mask = [later_q[0][:, c * HC * SP:(c + 1) * HC * SP] for c in range(C)]
        lg, pr, pr_t = [piece[0:SP, :] for piece in later_q[1:]]
        last_q = [carve(q_all[:, (b * G + 2) * C:(b * G + 3) * C, :].rearrange("p k n -> p (k n)")) for b in range(2)]
        out_prev, dif, att = [last_q[0](D, SP) for _ in range(3)]
        tmpd, x_s_out = [last_q[1](D, SP) for _ in range(2)]
        h_s = last_q[1](SP)

        w_loaded = sem("w_loaded")
        w2_loaded = sem("w2_loaded")
        wr_loaded = sem("wr_loaded")
        bias_loaded, bq_loaded = sem("bias_loaded"), sem("bq_loaded")
        consts = sem("consts")
        pool_setup = sem("pool_setup")
        setup_dve = sem("setup_dve")
        w_split = sem("w_split")
        bias_ready = sem("bias_ready")
        wr_sq, wr_sum, flag_ready = sem("wr_sq"), sem("wr_sum"), sem("flag_ready")
        x_loaded = [sem(f"x_loaded{g}") for g in range(G)]
        bn1, stat1, pow1, rstd1, norm1 = [sem(n) for n in ("bn1", "stat1", "pow1", "rstd1", "norm1")]
        bn2, stat2, pow2, rstd2, norm2 = [sem(n) for n in ("bn2", "stat2", "pow2", "rstd2", "norm2")]
        bn3, stat3, pow3, rstd3, norm3 = [sem(n) for n in ("bn3", "stat3", "pow3", "rstd3", "norm3")]
        t1_mm, t1_hi, t1_lo = sem("t1_mm"), sem("t1_hi"), sem("t1_lo")
        k_mm, k_exp, k_done = sem("k_mm"), sem("k_exp"), sem("k_done")
        q_mm, q_exp, q_relu, q_done = sem("q_mm"), sem("q_exp"), sem("q_relu"), sem("q_done")
        g_mm, g_copied, gt_mm, gt_copied, kv_mm, kv_step, kv_done = [
            sem(n) for n in ("g_mm", "g_copied", "gt_mm", "gt_copied", "kv_mm", "kv_step", "kv_done")]
        q_copied, o_mm, o_max, o_inv, o_done = [sem(n) for n in ("q_copied", "o_mm", "o_max", "o_inv", "o_done")]
        ot_mm, o_hi_done, o_lo_done, w_mm, w_added = [sem(n) for n in ("ot_mm", "o_hi_done", "o_lo_done", "w_mm", "w_added")]
        t2_mm, t2_done, f1_mm, f1_relu, f1_sq, f2_mm, f2_added = [
            sem(n) for n in ("t2_mm", "t2_done", "f1_mm", "f1_relu", "f1_sq", "f2_mm", "f2_added")]
        t3_mm, t3_done, f3_mm, f3_relu, f3_sq, f4_mm, f4_added = [
            sem(n) for n in ("t3_mm", "t3_done", "f3_mm", "f3_relu", "f3_sq", "f4_mm", "f4_added")]
        stored = sem("stored")
        bo_added, ob_added = sem("bo_added"), sem("ob_added")
        r_logits, r_step, r_gap_ready, r_exp, r_turn, r_w, r_hid, r_relu, r_sq, r_y = [
            sem(n) for n in ("r_logits", "r_step", "r_gap_ready", "r_exp", "r_turn", "r_w", "r_hid", "r_relu", "r_sq", "r_y")]
        c_link = sem("c_link")
        c_pool, c_pool16 = sem("c_pool"), sem("c_pool16")
        (c_wts, c_vecs, c_xs, c_out, c_wt, c_wt_sb, c_blk, c_lt, c_lt_sb, c_stat, c_rstd, c_z, c_zt, c_zt_sb,
         c_qkv, c_q_sb, c_kv_sb, c_klin, c_klin_read, c_kn, c_knt, c_kmask, c_qlin, c_lin, c_diff, c_var,
         c_rstd16, c_qn, c_qnt, c_qnt_sb, c_logit, c_scaled, c_lg, c_pr, c_prt, c_prt_sb, c_pv, c_outs, c_outt,
         c_dsum, c_att, c_att_t, c_att_t_sb, c_proj, c_hid, c_relu, c_sq, c_ffn, c_final) = [sem(f"c_{n}") for n in (
             "wts", "vecs", "xs", "out", "wt", "wt_sb", "blk", "lt", "lt_sb", "stat", "rstd", "z", "zt",
             "zt_sb", "qkv", "q_sb", "kv_sb", "klin", "klin_read", "kn", "knt", "kmask", "qlin", "lin", "diff",
             "var", "rstd16", "qn", "qnt", "qnt_sb", "logit", "scaled", "lg", "pr", "prt", "prt_sb", "pv",
             "outs", "outt", "dsum", "att", "att_t", "att_t_sb", "proj", "hid", "relu", "sq", "ffn", "final")]
        c_out_zero, c_added = sem("c_out_zero"), sem("c_added")
        c_turn = sem("c_turn")

        waits_passed = {"sp": sem("sp_waits_passed"), "act": sem("act_waits_passed"),
                        "dve": sem("dve_waits_passed"), "pool": sem("pool_waits_passed"), "pe": sem("pe_waits_passed")}

        def ge_apart(eng, name, sem_, value):
            ge(eng, sem_, value)
            if not isinstance(value, int):
                eng.sem_inc(waits_passed[name], 1)

        block = ctx.enter_context(nc.Block())

        def four(pair):
            return pair[:, :, :].rearrange("p b (t d) -> p (b t) d", d=D)

        def turned_o(i):
            return PT if isinstance(i, int) and i == 0 else PG

        def x_group(n):
            return x_all[:, bass.ds(n * T, T), :]

        def x_tile(n, t):
            return x_all[:, bass.ds(n * T + t, 1), :]

        def lagged(g, b, back):
            k = b - back
            gj, bj = g + k // B, k % B
            return gj * B + bj, bj * G + gj, bj

        def runs(j):
            return not isinstance(j, int) or 0 <= j < NG

        def iteration(g):
            return None if isinstance(g, int) and g < 2 else g - 2

        PLACES = {(0, "x"): ("q",), (0, "y"): ("norm", "keys"), (1, "x"): ("turn q",), (1, "y"): ("logits",), (2, "before x"): ("max",),
                  (2, "y"): ("probs",), (3, "before x"): ("sum",), (3, "x"): ("out",), (3, "y"): ("next q",)}
        LAST_PLACES = {(0, "x"): ("q",), (0, "y"): ("norm",), (1, "x"): ("turn q", "logits", "max"), (1, "y"): ("probs", "sum"),
                       (2, "x"): ("out",)}

        def parts(g, b, place):
            return (LAST_PLACES if isinstance(g, int) else PLACES).get((b, place), ())

        def routed_ordinal(g, b, second):
            i = g * B + b
            if not isinstance(i, int):
                return i * 2 - 4 + second
            f4, f2 = min(max(i - 3, 0), NG), min(max(i - 1, 0), NG)
            return f4 + f2 + (1 if second and 0 <= i - 3 < NG else 0)

        def per_head(ap, k, p=P):
            return ap.rearrange("p (a h o) -> p a h o", a=k, o=1).to_broadcast([p, k, HC, HD])

        @block.sync
        def _(sp):
            sp.dma_start(x_all[:, 0:T, :], x_dram[0]).then_inc(x_loaded[0], 16)
            for dst, w in ((wq_raw, Wq), (wk_raw, Wk)):
                sp.dma_start(dst, rows(w)).then_inc(w_loaded, 16)
            sp.dma_start(bias_rows[0:3, :], row(bk).to_broadcast([3, D])).then_inc(bias_loaded, 16)
            with nc.allow_non_contiguous_dma(reason="a short bias vector, features on partitions"):
                sp.dma_start(bq_col[:, :], bq.rearrange("(c p) -> p c", p=P)).then_inc(bq_loaded, 16)
            sp.dma_start(wr[:, :, :], rows(Wr)).then_inc(wr_loaded, 16)
            for g in range(1, G):
                sp.dma_start(x_all[:, g * T:(g + 1) * T, :], x_dram[g]).then_inc(x_loaded[g], 16)
            for dst, w in ((wv, rows(Wv)), (wo_raw, rows(Wo)),
                           (ws1[:, :, :], rows(Ws1)), (ws2[:, :], Ws2), (bv_rows[:, :], row(bv).to_broadcast([P, D])),
                           (bo_rows[:, :], row(bo).to_broadcast([P, D])), (ob_rows[:, :], row(ob).to_broadcast([P, D]))):
                sp.dma_start(dst, w).then_inc(w2_loaded, 16)
            with sp.Fori(1, B) as b:
                for g in range(G):
                    n = b * G + g
                    sp.wait_ge(stat1, T * (n - G + 1))
                    sp.dma_start(x_group(n), x_dram[bass.ds(n, 1)].rearrange("o p t d -> p (o t) d")).then_inc(x_loaded[g], 16)
            sp.wait_ge(flag_ready, 1)
            routed = sp.value_load(routed_flag[0:1, 0:1], min_val=0, max_val=1)

            def load_experts(k):
                with sp.If(routed > 0):
                    with sp.Fori(0, NE) as e:
                        sp.wait_ge(r_turn, k * (NE + 1) + e + 1)
                        sp.dma_start(w1e[:, :, :], W1[bass.ds(e, 1)].rearrange("o (c p) f -> p (o c) f", p=P)).then_inc(r_w, 16)
                        sp.dma_start(w2e[:, :], W2[bass.ds(e, 1)].rearrange("o f d -> f (o d)")).then_inc(r_w, 16)
                    ge_apart(sp, "sp", r_turn, (k + 1) * (NE + 1))

            def step(g, b):
                u, n, bu = lagged(g, b, 3)
                if runs(u):
                    load_experts(routed_ordinal(g, b, 0))
                    sp.wait_ge(f4_added, u + 1)
                    sp.dma_start(out_dram[bass.ds(n, 1)].rearrange("o p t d -> p (o t) d"),
                                 x_out).then_inc(stored, 16)
                if runs(lagged(g, b, 1)[0]):
                    load_experts(routed_ordinal(g, b, 1))

            sp.wait_ge(q_mm, C * NG)
            for dst, w in zip(raw4, (qw, kw, vw, ow)):
                sp.dma_start(dst, rows(w)).then_inc(c_wts, 16)
            for b in range(B):
                step(0, b)
            sp.wait_ge(q_copied, B)
            for dst, v in ((ob_b, ob), (lna_b, lna_w), (lnb_b, lnb_w)):
                sp.dma_start(dst, row(v).to_broadcast([SP, D])).then_inc(c_vecs, 16)
            for dst, w in zip(l_rows, (lqw, lkw, lvw)):
                for h in range(HC):
                    sp.dma_start(dst[h * HD:(h + 1) * HD, :], w).then_inc(c_vecs, 16)
            with nc.allow_non_contiguous_dma(reason="two short bias vectors, features on partitions"):
                for dst, v in ((qb_col, qb), (vb_col, vb)):
                    sp.dma_start(dst, v.rearrange("(c p) -> p c", p=P)).then_inc(c_vecs, 16)
            for dst, v in ((lqb_b, lqb), (lkb_b, lkb), (lvb_b, lvb), (lnc_b, lnc_w), (lnd_b, lnd_w)):
                sp.dma_start(dst, row(v).to_broadcast([SP, HD])).then_inc(c_vecs, 16)
            step(1, 0)
            sp.wait_ge(f2_added, B)
            for b in range(B):
                sp.dma_start(xs[b * SPT:(b + 1) * SPT, :], x_all[0:SPT, b * G * T, :]).then_inc(c_xs, 16)
            for b in range(1, B):
                step(1, b)
            with sp.Fori(2, G) as g:
                for b in range(B):
                    step(g, b)
            for b in range(3):
                step(G, b)

            load_experts(2 * NG)
            sp.wait_ge(stored, 16 * NG)
            sp.wait_ge(c_final, 1)
            for b in range(B):
                sp.dma_start(out[b, 0:SPT, :], x_s_out[b * SPT:(b + 1) * SPT, :]).then_inc(c_out, 16)
            sp.wait_ge(c_out, 16 * B)

        @block.gpsimd
        def _(pool):
            def mask(ap, pattern, lower, upper):
                for base, mult, pat in (lower, upper):
                    pool.wait_ge(pool_setup, mask.n)
                    nc.gpsimd.affine_select(out=ap, in_=ap, compare_op=ALU.is_ge, fill=0.0, base=base,
                                            pattern=[[pat, pattern]], channel_multiplier=mult).then_inc(pool_setup, 1)
                    mask.n += 1
            mask.n = 3
            nc.gpsimd.memset(ident[:, :], 1.0).then_inc(pool_setup, 1)
            nc.gpsimd.memset(head_mask[:, :], 1.0).then_inc(pool_setup, 1)
            nc.gpsimd.memset(minus_half[:, :], -0.5).then_inc(pool_setup, 1)
            mask(ident[:, :], P, (0, 1, -1), (0, -1, 1))
            mask(head_mask[:, :], HC, (0, 1, -HD), (HD - 1, -1, HD))
            nc.gpsimd.memset(ones_f[:, :], 1.0).then_inc(consts, 1)
            nc.gpsimd.memset(ones_row[:, :], 1.0).then_inc(consts, 1)
            for i in range(2):
                nc.gpsimd.memset(xn[i][:, :, D:D + 1], 1.0).then_inc(consts, 1)
            pool.wait_ge(pool_setup, mask.n)
            nc.gpsimd.tensor_copy(norm_inv[:, 0, 0:1], ident[:, 0:1]).then_inc(consts, 1)

            def rstd(slot, j, stat, powed, done, normed):
                mean, var = ln_mv[:, slot, :, 0], ln_mv[:, slot, :, 1]
                pool.wait_ge(stat, T * (j + 1))
                ge_apart(pool, "pool", normed, T * j)
                nc.gpsimd.tensor_scalar(ln_rstd[:, slot, :], var, LN_EPS, None, ALU.add).then_inc(powed, 1)
                pool.wait_ge(powed, 3 * j + 1)
                nc.gpsimd.tensor_tensor(ln_rstd[:, slot, :], ln_rstd[:, slot, :], minus_half[:, 0:T], ALU.pow).then_inc(powed, 1)
                pool.wait_ge(powed, 3 * j + 2)
                nc.gpsimd.tensor_tensor(ln_shift[:, slot, :], mean, ln_rstd[:, slot, :], ALU.mult).then_inc(powed, 1)
                ge_apart(pool, "pool", powed, 3 * j + 3)
                nc.gpsimd.tensor_scalar(ln_shift[:, slot, :], ln_shift[:, slot, :], -1.0, None, ALU.mult).then_inc(done, 1)

            def ln1(n):
                rstd(0, n, stat1, pow1, rstd1, norm1)

            def add_row(n, rows_, done):
                nc.gpsimd.tensor_tensor(x_group(n), x_group(n), rows_[:, :].rearrange("p (o d) -> p o d", o=1).to_broadcast([P, T, D]),
                                        ALU.add).then_inc(done, 1)

            def add_bo(n):
                ge_apart(pool, "pool", norm1, T * (n + 1))
                add_row(n, bo_rows, bo_added)

            ln1(0)
            pool.wait_ge(w2_loaded, 16 * 7)
            with pool.Fori(1, NG) as n:
                ln1(n)
                add_bo(n - 1)
            add_bo(NG - 1)

            def copy_q(g, b, ahead):
                i, n, bi = lagged(g, b, -ahead)
                if runs(i):
                    ge(pool, o_mm, i - 1)
                    nc.gpsimd.tensor_copy(q_cur[bi % 2], q_all[:, bass.ds(n * C, C), :]).then_inc(q_copied, 1)

            def step(g, b):
                r, nr, _ = lagged(g, b, 1)
                if runs(r):
                    ge_apart(pool, "pool", norm2, T * (r + 1))
                    add_row(nr, ob_rows, ob_added)
                u = lagged(g, b, 2)[0]
                if runs(u):
                    rstd(1, u, stat3, pow3, rstd3, norm3)
                attention_b(g, b, "after rstd3")
                copy_q(g, b, 1)
                attention_b(g, b, "before rstd2")
                i = g * B + b
                if runs(i):
                    rstd(0, i, stat2, pow2, rstd2, norm2)

            def chain_rstd(k):
                pool.wait_ge(c_stat, k + 1)
                nc.gpsimd.tensor_scalar(s_rs[:, 0:1], s_mv[:, 1:2], LN_EPS, None, ALU.add).then_inc(c_pool, 1)
                pool.wait_ge(c_pool, k + 1)
                nc.gpsimd.tensor_tensor(s_rs[:, 1:2], s_rs[:, 0:1], minus_half[0:SP, 0:1], ALU.pow).then_inc(c_rstd, 1)

            def chain_rstd16(k):
                ge_apart(pool, "pool", c_var, k + 1)
                nc.gpsimd.tensor_scalar(st16[2], st16[2], 1.0 / HD, LN_EPS, ALU.mult, ALU.add).then_inc(c_pool16, 1)
                pool.wait_ge(c_pool16, k + 1)
                nc.gpsimd.tensor_tensor(st16[3], st16[2], minus_half[0:SP, :], ALU.pow).then_inc(c_rstd16, 1)

            def attention_b(g, b, place):
                it = iteration(g)
                if it is None:
                    if (g, b, place) == (1, 1, "after rstd3"):
                        chain_rstd(0)
                    elif (g, b, place) == (1, 1, "before rstd2"):
                        chain_rstd(1)
                    elif (g, b, place) == (1, 3, "after rstd3"):
                        chain_rstd16(0)
                elif (b, place) == (0, "before rstd2"):
                    chain_rstd16(it + 1)

            copy_q(0, 0, 0)
            for g in range(G + 1):
                for b in range(B):
                    step(g, b)
            chain_rstd(2)

        @block.scalar
        def _(act):
            def normalise(dst, n, slot, j, ready, done):
                ge_apart(act, "act", ready, j + 1)
                for t in range(T):
                    nc.scalar.activation(dst[:, t:t + 1, 0:D], x_tile(n, t), ACT.Identity, scale=ln_rstd[:, slot, t:t + 1],
                                         bias=ln_shift[:, slot, t:t + 1]).then_inc(done, 1)

            def ln1(n, g):
                ge_apart(act, "act", g_mm, n - 1)
                normalise(xn[g % 2], n, 0, n, rstd1, norm1)

            def t1(n, g):
                ge(act, q_mm, C * n)
                for c in range(C):
                    ge_apart(act, "act", t1_mm, C * n + c + 1)
                    nc.scalar.activation(xt_hi[:, c, :], PT[:, c, :], ACT.Copy).then_inc(t1_hi, 1)

            act.wait_ge(w_loaded, 32)
            for hi, raw in ((wq_hi, wq_raw), (wk_hi, wk_raw)):
                nc.scalar.activation(hi[:, :, :], raw, ACT.Copy).then_inc(w_split, 1)
            ln1(0, 0)
            t1(0, 0)

            def pass1(b, last):
                for g in range(G):
                    n = b * G + g
                    if not (last and g == G - 1):
                        ln1(n + 1, g + 1)
                    act.wait_ge(k_mm, n + 1)
                    ge(act, q_done, n)
                    nc.scalar.activation(exp_k, four(PB), ACT.Exp, bias=minus_one[:, 0:1]).then_inc(k_exp, 1)
                    if g == 0 and not (isinstance(b, int) and b == 0):
                        transposed_g(b - 1)
                    act.wait_ge(k_done, n + 1)
                    for c in range(C):
                        ge_apart(act, "act", q_mm, C * n + c + 1)
                        nc.scalar.activation(exp_q[:, c, :], PA[:, c, :], ACT.Exp, bias=bq_col[:, c:c + 1]).then_inc(q_exp, 1)
                        nc.scalar.activation(q_all[:, bass.ds(n * C + c, 1), :], PA[:, c:c + 1, :], ACT.Relu,
                                             bias=bq_col[:, c:c + 1]).then_inc(q_relu, 1)
                    if not (last and g == G - 1):
                        t1(n + 1, g + 1)

            def transposed_g(b):
                act.wait_ge(gt_mm, b + 1)
                ge(act, kv_mm, b)
                nc.scalar.activation(g_t[:, :, :], PG[:, :, 0:D], ACT.Copy).then_inc(gt_copied, 1)

            act.wait_ge(setup_dve, 1)
            act.wait_ge(bq_loaded, 16)
            pass1(0, False)
            act.wait_ge(w2_loaded, 16 * 7)
            nc.scalar.activation(wo_hi[:, :, :], wo_raw, ACT.Copy).then_inc(w_split, 1)
            with act.Fori(1, B - 1) as b:
                pass1(b, False)
            pass1(B - 1, True)
            transposed_g(B - 1)

            act.wait_ge(flag_ready, 1)
            routed = act.value_load(routed_flag[0:1, 0:1], min_val=0, max_val=1)

            act.wait_ge(g_mm, NG)
            act.wait_ge(q_done, NG)

            def run_experts(k, n_tok, relu):
                with act.If(routed > 0):
                    act.wait_ge(r_gap_ready, k + 1)
                    nc.scalar.activation(r_gap[:, 1, :], r_gap[:, 0, :], ACT.Exp).then_inc(r_exp, 1)
                    with act.Fori(0, NE) as e:
                        act.wait_ge(r_hid, k * NE + e + 1)
                        nc.scalar.activation(relu, PT[:, 1, 0:n_tok], ACT.Relu).then_inc(r_relu, 1)

            def step(g, b):
                i = g * B + b
                u3 = lagged(g, b, 3)[0]
                if runs(u3):
                    run_experts(routed_ordinal(g, b, 0), GT, h3)
                r = lagged(g, b, 1)[0]
                if runs(r):
                    ge(act, f1_mm, r)
                    for c in range(C):
                        act.wait_ge(t2_mm, C * r + c + 1)
                        nc.scalar.activation(x2t[:, c, :], PT[:, c, :], ACT.Copy).then_inc(t2_done, 1)
                if runs(i):
                    ge(act, w_mm, i)
                    for c in range(C):
                        act.wait_ge(ot_mm, C * i + c + 1)
                        nc.scalar.activation(o_hi[:, c, :], turned_o(i)[:, c, :], ACT.Copy).then_inc(o_hi_done, 1)
                u, nu, _ = lagged(g, b, 2)
                if runs(u):
                    ge(act, t3_mm, C * u)
                    normalise(y3, nu, 1, u, rstd3, norm3)
                if runs(r):
                    act.wait_ge(f1_mm, r + 1)
                    ge(act, f2_mm, r)
                    nc.scalar.activation(h2, PA[:, 0, :], ACT.Relu).then_inc(f1_relu, 1)
                    act.wait_ge(f1_relu, r + 1)
                    nc.scalar.activation(h2, h2, ACT.Square).then_inc(f1_sq, 1)
                if runs(u):
                    act.wait_ge(t3_mm, C * (u + 1))
                    ge(act, f3_mm, u)
                    nc.scalar.activation(x3t, PT[:, :, :], ACT.Copy).then_inc(t3_done, 1)
                it = iteration(g)
                softmax_here = it is not None and b == (1 if isinstance(g, int) else 2)
                if softmax_here:
                    act.wait_ge(c_lg, it + 1)
                    nc.scalar.activation(pr, lg, ACT.Exp).then_inc(c_pr, 1)
                if runs(r):
                    run_experts(routed_ordinal(g, b, 1), GT, h2)
                if runs(u):
                    act.wait_ge(f3_mm, u + 1)
                    ge(act, f4_mm, u)
                    nc.scalar.activation(h3, PA[:, 1, :], ACT.Relu).then_inc(f3_relu, 1)
                    act.wait_ge(f3_relu, u + 1)
                    nc.scalar.activation(h3, h3, ACT.Square).then_inc(f3_sq, 1)
                if isinstance(i, int) and i == 0:
                    for k, pair in enumerate((PT, PG)):
                        act.wait_ge(c_wt, k + 1)
                        nc.scalar.activation(b_weights[:, 1, 2 * k:2 * k + 2, :], pair[:, :, :], ACT.Copy).then_inc(c_wt_sb, 1)
                if runs(i):
                    ge(act, t2_mm, C * i)
                    normalise(y2, lagged(g, b, 0)[1], 0, i, rstd2, norm2)
                if softmax_here:
                    act.wait_ge(c_prt, it + 1)
                    nc.scalar.activation(pr_t.rearrange("p (b n) -> p b n", b=2), PG[0:SP, :, :], ACT.Copy).then_inc(c_prt_sb, 1)

            for g in range(2):
                for b in range(B):
                    step(g, b)
            with act.Fori(2, G) as g:
                for b in range(B):
                    step(g, b)
            for b in range(3):
                step(G, b)

            act.wait_ge(c_hid, 1)
            nc.scalar.activation(h_s, PA[:, 1, 0:SP], ACT.Relu).then_inc(c_relu, 1)
            run_experts(2 * NG, SP, h_s)

        @block.vector
        def _(dve):
            links = [0]

            def link(ins):
                ins.then_inc(c_link, 1)
                links[0] += 1
                dve.wait_ge(c_link, links[0])

            def stats(n, slot, j, bn, stat, used):
                ge_apart(dve, "dve", used, j)
                for t in range(T):
                    nc.vector.bn_stats(ln_bn[:, slot, t:t + 1, :], x_tile(n, t)).then_inc(bn, 1)
                for t in range(T):
                    ge_apart(dve, "dve", bn, T * j + t + 1)
                    nc.vector.bn_aggr(ln_mv[:, slot, t:t + 1, :], ln_bn[:, slot, t:t + 1, :]).then_inc(stat, 1)

            def ln1(n, g, b):
                dve.wait_ge(x_loaded[g % G], 16 * (b + g // G + 1))
                stats(n, 0, n, bn1, stat1, rstd1)

            def t1(n, g):
                ge(dve, q_mm, C * n)
                for c in range(C):
                    dve.wait_ge(t1_hi, C * n + c + 1)
                    nc.vector.tensor_tensor(xt_lo[:, c, :], PT[:, c, :], xt_hi[:, c, :].bitcast(F32), ALU.subtract).then_inc(t1_lo, 1)

            nc.vector.memset(minus_one[:, :], -1.0).then_inc(setup_dve, 1)
            nc.vector.memset(bias3[:, :], 0.0).then_inc(setup_dve, 1)
            ln1(0, 0, 0)
            for i, (lo, hi, raw) in enumerate(((wq_lo, wq_hi, wq_raw), (wk_lo, wk_hi, wk_raw))):
                dve.wait_ge(w_split, i + 1)
                nc.vector.tensor_tensor(lo[:, :, :], raw, hi[:, :, :].bitcast(F32), ALU.subtract).then_inc(setup_dve, 1)
            dve.wait_ge(bias_loaded, 16)
            dve.wait_ge(consts, 5)
            link(nc.vector.tensor_scalar(bias_rows[0:3, :], bias_rows[0:3, :], 1.0, None, ALU.add))
            link(nc.vector.tensor_copy(bpart[0:3, 0, :], bias_rows[0:3, :]))
            link(nc.vector.tensor_tensor(bias_rows[0:3, :], bias_rows[0:3, :], bpart[0:3, 0, :], ALU.subtract))
            link(nc.vector.tensor_copy(bpart[0:3, 1, :], bias_rows[0:3, :]))
            link(nc.vector.tensor_tensor(bias_rows[0:3, :], bias_rows[0:3, :], bpart[0:3, 1, :], ALU.subtract))
            link(nc.vector.tensor_scalar(bias_rows[0:3, :], bias_rows[0:3, :], ident[0:3, 2:3], None, ALU.mult))
            link(nc.vector.scalar_tensor_tensor(bias_rows[0:3, :], bpart[0:3, 1, :], ident[0:3, 1:2], bias_rows[0:3, :], ALU.mult, ALU.add))
            nc.vector.scalar_tensor_tensor(bias3[0:3, :], bpart[0:3, 0, :], ident[0:3, 0:1], bias_rows[0:3, :],
                                           ALU.mult, ALU.add).then_inc(bias_ready, 1)
            dve.wait_ge(wr_loaded, 16)
            nc.vector.tensor_tensor(wr_tmp[:, :], wr[:, :, :].rearrange("p c e -> p (c e)"),
                                    wr[:, :, :].rearrange("p c e -> p (c e)"), ALU.mult).then_inc(wr_sq, 1)
            t1(0, 0)
            ln1(1, 1, 0)
            dve.wait_ge(wr_sum, 1)
            link(nc.vector.reduce_max(wr_max[0:1, 0:1], PG[0:1, 0, 0:NE], AX))
            link(nc.vector.tensor_scalar(wr_max[0:1, 1:2], wr_max[0:1, 0:1], WR_NORM2_BOUND, None, ALU.is_lt))
            nc.vector.tensor_scalar(routed_flag[0:1, 0:1], wr_max[0:1, 1:2], -1.0, 1.0, ALU.mult, ALU.add).then_inc(flag_ready, 1)

            def pass1(b, last):
                for g in range(G):
                    n = b * G + g
                    later_batch = not (isinstance(b, int) and b == 0)
                    if g == 0 and later_batch:
                        copy_g(b - 1)
                    dve.wait_ge(k_exp, n + 1)
                    ge(dve, g_mm, n)
                    nc.vector.scalar_tensor_tensor(k_tok, exp_k, 1.0, four(PB), ALU.min, ALU.max).then_inc(k_done, 1)
                    if not (last and g >= G - 2):
                        ln1(n + 2, g + 2, b)
                    if g == 0 and later_batch:
                        batch_kv(b - 1)
                    if not (last and g == G - 1):
                        t1(n + 1, g + 1)
                    ge_apart(dve, "dve", q_relu, C * (n + 1))
                    q = q_all[:, bass.ds(n * C, C), :]
                    nc.vector.scalar_tensor_tensor(q, exp_q, 1.0, q, ALU.min, ALU.add).then_inc(q_done, 1)

            def copy_g(b):
                dve.wait_ge(g_mm, (b + 1) * G)
                ge(dve, kv_done, 2 * C * b)
                ge(dve, gt_mm, b)
                nc.vector.tensor_copy(g_sb[:, :, :], PG[:, :, 0:D + 1]).then_inc(g_copied, 1)

            def batch_kv(b):
                dve.wait_ge(kv_mm, b + 1)
                for c in range(C):
                    nc.vector.scalar_tensor_tensor(kv_tmp[:, c, :], bv_rows[:, c * P:(c + 1) * P], g_sb[:, c, D:D + 1],
                                                   PG[:, c, D:D + P], ALU.mult, ALU.add).then_inc(kv_step, 1)
                for c in range(C):
                    dve.wait_ge(kv_step, C * b + c + 1)
                    dst = kv_all[:, bass.ds(b * C + c, 1), :]
                    nc.vector.tensor_tensor(dst[:, :, 0:P].rearrange("p o (h e) -> p (o h) e", e=HD),
                                            kv_tmp[:, c, :].rearrange("p (h e) -> p h e", e=HD),
                                            head_mask[:, :].rearrange("p (h o) -> p h o", o=1).to_broadcast([P, HC, HD]),
                                            ALU.mult).then_inc(kv_done, 1)
                    nc.vector.tensor_scalar(dst[:, :, P:KVW].rearrange("p o h -> p (o h)"), head_mask[:, :],
                                            g_sb[:, c, D:D + 1], None, ALU.mult).then_inc(kv_done, 1)

            pass1(0, False)
            dve.wait_ge(w_split, 3)
            nc.vector.tensor_tensor(wo_lo[:, :, :], wo_raw, wo_hi[:, :, :].bitcast(F32), ALU.subtract).then_inc(setup_dve, 1)
            with dve.Fori(1, B - 1) as b:
                pass1(b, False)
            pass1(B - 1, True)
            copy_g(B - 1)

            dve.wait_ge(flag_ready, 1)
            routed = dve.value_load(routed_flag[0:1, 0:1], min_val=0, max_val=1)

            def run_experts(k, added, count, p, tiles, x_of, y, h):
                with dve.If(routed > 0):
                    ge_apart(dve, "dve", added, count)
                    dve.wait_ge(r_logits, k + 1)
                    nc.vector.tensor_copy(r_lg[0:p, 0:tiles, :], PT[0:p, 0, 0:tiles * NE].rearrange("p (t e) -> p t e", e=NE)).then_inc(r_step, 1)
                    ge_apart(dve, "dve", r_step, 4 * k + 1)
                    for t in range(tiles):
                        last = nc.vector.max(r_top[0:p, t, :], r_lg[0:p, t, :])
                    last.then_inc(r_step, 1)
                    dve.wait_ge(r_step, 4 * k + 2)
                    nc.vector.tensor_tensor(r_gap[0:p, 0, 0:tiles], r_top[0:p, 0:tiles, 1], r_top[0:p, 0:tiles, 0],
                                            ALU.subtract).then_inc(r_gap_ready, 1)
                    dve.wait_ge(r_exp, k + 1)
                    nc.vector.tensor_scalar(r_gap[0:p, 2, 0:tiles], r_gap[0:p, 1, 0:tiles], 1.0, None, ALU.add).then_inc(r_step, 1)
                    dve.wait_ge(r_step, 4 * k + 3)
                    nc.vector.tensor_scalar(r_gap[0:p, 3, 0:tiles], r_gap[0:p, 2, 0:tiles], 1.0, None, ALU.is_le).then_inc(r_step, 1)
                    dve.wait_ge(r_step, 4 * k + 4)
                    for t in range(tiles):
                        last = nc.vector.tensor_scalar(probs[0:p, :, t], r_lg[0:p, t, :], r_top[0:p, t, 0:1],
                                                       r_gap[0:p, 3, t:t + 1], ALU.is_ge, ALU.mult)
                    last.then_inc(r_turn, 1)
                    with dve.Fori(0, NE) as e:
                        dve.wait_ge(r_relu, k * NE + e + 1)
                        nc.vector.tensor_tensor(h, h, h, ALU.mult).then_inc(r_sq, 1)
                        dve.wait_ge(r_y, k * NE + e + 1)
                        dve.wait_ge(r_turn, k * (NE + 1) + e + 1)
                        for t in range(tiles):
                            x = x_of(t)
                            last = nc.vector.scalar_tensor_tensor(x, y[0:p, t:t + 1, :], probs[0:p, bass.ds(e, 1), t], x,
                                                                  ALU.mult, ALU.add)
                        last.then_inc(r_turn, 1)
                    ge_apart(dve, "dve", r_turn, (k + 1) * (NE + 1))

            dve.wait_ge(norm1, T * NG)
            dve.wait_ge(g_mm, NG)

            def step(g, b):
                i, n, _ = lagged(g, b, 0)
                r, nr, _ = lagged(g, b, 1)
                u, nu, _ = lagged(g, b, 2)
                v, nv, bv_ = lagged(g, b, 3)
                if runs(i):
                    regions = ((6, 2, PT[:, 0, 0:2 * KVW]), (0, 3, PA[:, 0, 0:3 * KVW]), (3, 3, PA[:, 1, 0:3 * KVW]))
                    dve.wait_ge(o_mm, i + 1)
                    for k0, nb, reg in regions:
                        last = nc.vector.tensor_scalar(norm_sb[:, k0:k0 + nb, :], reg.rearrange("p (k w) -> p k w", w=KVW)[:, :, P:KVW],
                                                       NORM_EPS, None, ALU.max)
                    last.then_inc(o_max, 1)
                    dve.wait_ge(o_max, i + 1)
                    nc.vector.reciprocal(norm_inv[:, :, :], norm_sb[:, :, :]).then_inc(o_inv, 1)
                    dve.wait_ge(o_inv, i + 1)
                    ge(dve, ot_mm, C * i)
                    for k0, nb, reg in regions:
                        nc.vector.tensor_tensor(o_tok[:, k0:k0 + nb, :].rearrange("p k (h e) -> p k h e", e=HD),
                                                reg.rearrange("p (k w) -> p k w", w=KVW)[:, :, 0:P].rearrange("p k (h e) -> p k h e", e=HD),
                                                norm_inv[:, k0:k0 + nb, :].unsqueeze(3).to_broadcast([P, nb, HC, HD]),
                                                ALU.mult).then_inc(o_done, 1)
                if isinstance(i, int) and i == 0:
                    batch_kv(B - 1)
                if runs(u):
                    ge_apart(dve, "dve", f2_added, u + 1)
                    stats(nu, 1, u, bn3, stat3, rstd3)
                if runs(v):
                    dve.wait_ge(f4_mm, v + 1)
                    ge(dve, stored, 16 * v)
                    nc.vector.tensor_tensor(x_out, four(PB), x_group(nv), ALU.add).then_inc(f4_added, 1)
                    run_experts(routed_ordinal(g, b, 0), f4_added, v + 1, P, T, lambda t: x_out[:, t:t + 1, :], four(PB), h3)
                if runs(i):
                    for c in range(C):
                        dve.wait_ge(o_hi_done, C * i + c + 1)
                        ge(dve, w_mm, i)
                        nc.vector.tensor_tensor(o_lo[:, c, :], turned_o(i)[:, c, :], o_hi[:, c, :].bitcast(F32),
                                                ALU.subtract).then_inc(o_lo_done, 1)
                attention_b(g, b, "before x")
                attention_b(g, b, "x")
                if runs(i):
                    dve.wait_ge(w_mm, i + 1)
                    dve.wait_ge(bo_added, NG)
                    nc.vector.tensor_tensor(x_group(n), four(PB), x_group(n), ALU.add).then_inc(w_added, 1)
                    dve.wait_ge(w_added, i + 1)
                    stats(n, 0, i, bn2, stat2, rstd2)
                if runs(r):
                    dve.wait_ge(f2_mm, r + 1)
                    dve.wait_ge(ob_added, r + 1)
                    nc.vector.tensor_tensor(x_group(nr), four(PG), x_group(nr), ALU.add).then_inc(f2_added, 1)
                    run_experts(routed_ordinal(g, b, 1), f2_added, r + 1, P, T, lambda t: x_tile(nr, t), four(PG), h2)
                attention_b(g, b, "y")

            def heads(ap):
                return ap.rearrange("p (h e) -> p h e", e=HD)

            def over_heads(ap):
                return ap.rearrange("p (o e) -> p o e", o=1).to_broadcast([SP, H, HD])

            def over_feats(ap):
                return ap.rearrange("p (h o) -> p h o", o=1).to_broadcast([SP, H, HD])

            def over_keys(ap):
                return ap.rearrange("p (h o) -> p h o", o=1).to_broadcast([SP, H, SP])

            def mean_var(src):
                link(nc.vector.bn_stats(s_bn, src))
                nc.vector.bn_aggr(s_mv, s_bn).then_inc(c_stat, 1)

            def scale_shift(dst, src, k):
                dve.wait_ge(c_stat, k + 1)
                dve.wait_ge(c_rstd, k + 1)
                link(nc.vector.tensor_scalar(dst, src, s_mv[:, 0:1], s_rs[:, 1:2], ALU.subtract, ALU.mult))

            def turn(it, k, ins):
                ins.then_inc(c_turn, 1)
                dve.wait_ge(c_turn, it * TURNS + k)

            TURNS = 10

            def center16(step_):
                step_(1, nc.vector.reduce_sum(st16[0], heads(lin), AX))
                step_(2, nc.vector.tensor_scalar(st16[1], st16[0], 1.0 / HD, None, ALU.mult))
                step_(3, nc.vector.tensor_tensor(heads(cen), heads(lin), over_feats(st16[1]), ALU.subtract))
                step_(4, nc.vector.tensor_tensor(sq16, cen, cen, ALU.mult))
                nc.vector.reduce_sum(st16[2], heads(sq16), AX).then_inc(c_var, 1)

            def prepare(i, place):
                if (i, place) == (4, "y"):
                    dve.wait_ge(c_vecs, 16 * (10 + 3 * HC))
                    for rows16, blk in zip(l_rows, l_blk):
                        nc.vector.tensor_tensor(blk.rearrange("p (h e) -> p h e", e=HD),
                                                rows16.rearrange("p (o e) -> p o e", o=1).to_broadcast([P, HC, HD]),
                                                head_mask[:, :].rearrange("p (h o) -> p h o", o=1).to_broadcast([P, HC, HD]),
                                                ALU.mult).then_inc(c_blk, 1)
                elif (i, place) == (5, "before x"):
                    dve.wait_ge(c_xs, 16 * B)
                    link(nc.vector.tensor_tensor(xs, xs, ob_b, ALU.subtract))
                    mean_var(xs)
                elif (i, place) == (5, "x"):
                    scale_shift(zs, xs, 0)
                    mean_var(zs)
                elif (i, place) == (5, "y"):
                    scale_shift(zz, zs, 1)
                    nc.vector.tensor_tensor(za, zz, lna_b, ALU.mult).then_inc(c_z, 1)
                    nc.vector.tensor_tensor(zb, zz, lnb_b, ALU.mult).then_inc(c_z, 1)
                    dve.wait_ge(c_lt, 1)
                    nc.vector.tensor_copy(l_bdt_all, PG[:, 1, 0:3 * P]).then_inc(c_lt_sb, 1)
                    dve.wait_ge(c_zt, 1)
                    nc.vector.tensor_copy(za_t, chunked(PG[:, 0, 0:C * SP])).then_inc(c_zt_sb, 1)
                    nc.vector.tensor_copy(zb_t, chunked(PG[:, 0, C * SP:2 * C * SP])).then_inc(c_zt_sb, 1)
                elif (i, place) == (6, "x"):
                    dve.wait_ge(c_qkv, 1)
                    for c in range(C):
                        nc.vector.tensor_copy(k_t[:, c, :], PA[:, 1, (C + c) * SP:(C + c + 1) * SP]).then_inc(c_kv_sb, 1)
                        nc.vector.tensor_scalar(v_t[:, c, :], PA[:, 1, (2 * C + c) * SP:(2 * C + c + 1) * SP], vb_col[:, c:c + 1],
                                                None, ALU.add).then_inc(c_kv_sb, 1)
                        last = nc.vector.tensor_scalar(qcur_t[:, c, :], PA[:, 1, c * SP:(c + 1) * SP], qb_col[:, c:c + 1], None, ALU.add)
                    last.then_inc(c_q_sb, 1)
                    link(nc.vector.tensor_scalar(neg_mask.rearrange("p (b s) -> p b s", s=SPT),
                                                 head_mask[0:SP, 0:B].rearrange("p (b o) -> p b o", o=1).to_broadcast([SP, B, SPT]),
                                                 1.0, 1e30, ALU.subtract, ALU.mult))
                elif (i, place) == (6, "y"):
                    dve.wait_ge(c_klin, 1)
                    nc.vector.tensor_tensor(heads(vi), heads(PG[0:SP, 1, 0:D]), over_heads(lvb_b), ALU.add).then_inc(c_klin_read, 1)
                    nc.vector.tensor_tensor(heads(lin), heads(PG[0:SP, 0, 0:D]), over_heads(lkb_b), ALU.add).then_inc(c_klin_read, 1)
                    dve.wait_ge(c_klin_read, 2)
                    center16(lambda k, ins: link(ins))
                    nc.vector.memset(out_cur, 0.0).then_inc(c_out_zero, 1)
                elif (i, place) == (7, "x"):
                    dve.wait_ge(c_rstd16, 1)
                    link(nc.vector.tensor_tensor(heads(cen), heads(cen), over_feats(st16[3]), ALU.mult))
                    nc.vector.tensor_tensor(heads(kn), heads(cen), over_heads(lnd_b), ALU.mult).then_inc(c_kn, 1)

            def attention_b(g, b, place):
                it = iteration(g)
                last_one = isinstance(g, int)
                if it is None:
                    prepare(g * B + b, place)
                    return
                for name in parts(g, b, place):
                    iterate(name, it, last_one)

            def iterate(name, it, last_one):
                lgh = lg.rearrange("p (h s) -> p h s", s=SP)
                prh = pr.rearrange("p (h s) -> p h s", s=SP)
                if name == "q":
                    if last_one:
                        stop_after_second()
                    dve.wait_ge(c_qlin, it + 1)
                    nc.vector.tensor_tensor(heads(lin), heads(PA[0:SP, 1, 0:D]), over_heads(lqb_b), ALU.add).then_inc(c_lin, 1)
                    dve.wait_ge(c_lin, it + 1)
                    center16(lambda k, ins: turn(it, k, ins))
                elif name == "norm":
                    dve.wait_ge(c_rstd16, it + 2)
                    turn(it, 5, nc.vector.tensor_tensor(heads(cen), heads(cen), over_feats(st16[3]), ALU.mult))
                    nc.vector.tensor_tensor(heads(qn), heads(cen), over_heads(lnc_b), ALU.mult).then_inc(c_qn, 1)
                elif name == "keys":
                    dve.wait_ge(c_knt, it + 1)
                    for c in range(C):
                        nc.vector.tensor_tensor(kn_mask[c].rearrange("p (h s) -> p h s", s=SP),
                                                PG[:, 0, c * SP:(c + 1) * SP].rearrange("p (o s) -> p o s", o=1).to_broadcast([P, HC, SP]),
                                                head_mask[:, :].rearrange("p (h o) -> p h o", o=1).to_broadcast([P, HC, SP]),
                                                ALU.mult).then_inc(c_kmask, 1)
                elif name == "turn q":
                    dve.wait_ge(c_qnt, it + 1)
                    nc.vector.tensor_copy(qn_t, chunked(PA[:, 1, 0:C * SP])).then_inc(c_qnt_sb, 1)
                elif name == "logits":
                    dve.wait_ge(c_logit, it + 1)
                    nc.vector.scalar_tensor_tensor(lgh, PG[0:SP, :, :].rearrange("p b (h s) -> p (b h) s", s=SP), HD ** -0.5,
                                                   neg_mask.rearrange("p (o s) -> p o s", o=1).to_broadcast([SP, H, SP]),
                                                   ALU.mult, ALU.add).then_inc(c_scaled, 1)
                elif name == "max":
                    dve.wait_ge(c_scaled, it + 1)
                    turn(it, 6, nc.vector.reduce_max(mx16, lgh, AX))
                    nc.vector.tensor_tensor(lgh, lgh, over_keys(mx16), ALU.subtract).then_inc(c_lg, 1)
                elif name == "sum":
                    dve.wait_ge(c_pr, it + 1)
                    turn(it, 7, nc.vector.reduce_sum(sum16, prh, AX))
                    turn(it, 8, nc.vector.reciprocal(inv16, sum16))
                    dve.wait_ge(c_out_zero, 1)
                    turn(it, 9, nc.vector.tensor_copy(out_prev, out_cur))
                elif name == "out":
                    dve.wait_ge(c_pv, it + 1)
                    nc.vector.tensor_tensor(heads(out_cur), heads(PA[0:SP, 1, 0:D]), over_feats(inv16), ALU.mult).then_inc(c_outs, 1)
                    dve.wait_ge(c_outs, it + 1)
                    if not last_one:
                        turn(it, 10, nc.vector.tensor_tensor(dif, out_cur, out_prev, ALU.subtract))
                        nc.vector.tensor_reduce(dsum[0:SP, 0:1], dif, AX, ALU.add, apply_absolute_value=True).then_inc(c_dsum, 1)
                elif name == "next q":
                    dve.wait_ge(c_outt, it + 1)
                    nc.vector.tensor_tensor(qcur_t, chunked(PG[:, 0, 0:C * SP]), qcur_t, ALU.add).then_inc(c_q_sb, 1)

            def stop_after_second():
                dve.wait_ge(c_diff, 1)
                link(nc.vector.tensor_scalar(dsum[0:SP, 1:2], PA[0:SP, 1, D:D + 1], 1.0 / (B * S * D), None, ALU.mult))
                link(nc.vector.tensor_scalar(dsum[0:SP, 2:3], dsum[0:SP, 1:2], FACTOR, THRESH, ALU.mult, ALU.add))
                link(nc.vector.tensor_tensor(dsum[0:SP, 3:4], dsum[0:SP, 1:2], dsum[0:SP, 2:3], ALU.is_lt))
                link(nc.vector.tensor_scalar(dsum[0:SP, 4:5], dsum[0:SP, 3:4], -1.0, 1.0, ALU.mult, ALU.add))

            for g in range(2):
                for b in range(B):
                    step(g, b)
            with dve.Fori(2, G) as g:
                for b in range(B):
                    step(g, b)
            for b in range(3):
                step(G, b)

            link(nc.vector.tensor_scalar(tmpd, out_prev, dsum[0:SP, 3:4], None, ALU.mult))
            nc.vector.scalar_tensor_tensor(att, out_cur, dsum[0:SP, 4:5], tmpd, ALU.mult, ALU.add).then_inc(c_att, 1)
            dve.wait_ge(c_att_t, 1)
            nc.vector.tensor_copy(att_t, PT[:, 1, 0:C * SP].rearrange("p (c n) -> p c n", c=C)).then_inc(c_att_t_sb, 1)
            dve.wait_ge(c_proj, 1)
            link(nc.vector.tensor_tensor(tmpd, PB[0:SP, 0, 0:D], ob_b, ALU.add))
            link(nc.vector.tensor_tensor(xs, xs, tmpd, ALU.add))
            mean_var(xs)
            dve.wait_ge(c_stat, 3)
            dve.wait_ge(c_rstd, 3)
            nc.vector.tensor_scalar(zs, xs, s_mv[:, 0:1], s_rs[:, 1:2], ALU.subtract, ALU.mult).then_inc(c_z, 1)
            dve.wait_ge(c_zt, 2)
            nc.vector.tensor_copy(xs_t, PT[:, 0, 0:C * SP].rearrange("p (c n) -> p c n", c=C)).then_inc(c_zt_sb, 1)
            dve.wait_ge(c_relu, 1)
            nc.vector.tensor_tensor(h_s, h_s, h_s, ALU.mult).then_inc(c_sq, 1)
            dve.wait_ge(c_ffn, 1)
            nc.vector.tensor_tensor(x_s_out, PB[0:SP, 1, 0:D], xs, ALU.add).then_inc(c_added, 1)
            dve.wait_ge(c_added, 1)
            run_experts(2 * NG, c_added, 1, SP, 1, lambda t: x_s_out.rearrange("p (t d) -> p t d", t=1), four(PB)[:, 2:3, :], h_s)
            nc.vector.tensor_copy(dsum[0:SP, 7:8], x_s_out[:, 0:1]).then_inc(c_final, 1)

        @block.tensor
        def _(pe):
            mm = nc.tensor.matmul

            def t1(n, g):
                pe.wait_ge(norm1, T * (n + 1))
                ge(pe, t1_lo, C * n)
                for c in range(C):
                    for t in range(T):
                        last = nc.tensor.transpose(PT[:, c, t * P:(t + 1) * P], xn[g % 2][:, t, c * P:(c + 1) * P], ident[:, :])
                    last.then_inc(t1_mm, 1)

            def column_norms():
                pe.wait_ge(wr_sq, 1)
                for c in range(C):
                    last = mm(PG[0:P, 0, 0:NE], ones_f[:, :], wr_tmp[:, c * NE:(c + 1) * NE], start=(c == 0), stop=(c == C - 1))
                last.then_inc(wr_sum, 1)

            pe.wait_ge(consts, 5)
            t1(0, 0)
            column_norms()
            pe.wait_ge(setup_dve, 4)
            pe.wait_ge(bias_ready, 1)

            def k_product(n, g):
                pe.wait_ge(t1_lo, C * (n + 1))
                ge(pe, k_done, n)
                for t in range(T):
                    dst = four(PB)[:, t, :]
                    mm(dst, ones_row[:, :], bias3[:, :], start=True, stop=False)
                    for c in range(C):
                        hi, lo = (x[:, c, t * P:(t + 1) * P] for x in (xt_hi, xt_lo))
                        mm(dst, hi, wk_hi[:, c, :], start=False, stop=False)
                        mm(dst, hi, wk_lo[:, c, :], start=False, stop=False)
                        last = mm(dst, lo, wk_hi[:, c, :], start=False, stop=(c == C - 1))
                last.then_inc(k_mm, 1)

            def q_product(n, g, batch):
                ge(pe, q_relu, C * n)
                for o in range(C):
                    if batch is not None and o == C - 1:
                        kv_product(batch)
                    dst, cols = PA[:, o, :], slice(o * P, (o + 1) * P)
                    for c in range(C):
                        hi, lo = xt_hi[:, c, :], xt_lo[:, c, :]
                        mm(dst, wq_hi[:, c, cols], hi, start=(c == 0), stop=False)
                        mm(dst, wq_hi[:, c, cols], lo, start=False, stop=False)
                        last = mm(dst, wq_lo[:, c, cols], hi, start=False, stop=(c == C - 1))
                    last.then_inc(q_mm, 1)

            def g_product(n, g):
                pe.wait_ge(k_done, n + 1)
                for t in range(T):
                    for c in range(C):
                        last = mm(PG[:, c, 0:D + 1], k_tok[:, t, c * P:(c + 1) * P], xn[g % 2][:, t, :],
                                  start=(g == 0 and t == 0), stop=(g == G - 1 and t == T - 1))
                last.then_inc(g_mm, 1)

            def g_transposes(b):
                pe.wait_ge(g_copied, b + 1)
                for i in range(C):
                    for c in range(C):
                        last = nc.tensor.transpose(PG[:, i, c * P:(c + 1) * P], g_sb[:, c, i * P:(i + 1) * P], ident[:, :])
                last.then_inc(gt_mm, 1)

            def kv_product(b):
                pe.wait_ge(gt_copied, b + 1)
                for c in range(C):
                    for i in range(C):
                        last = mm(PG[:, c, D:D + P], g_t[:, i, c * P:(c + 1) * P], wv[:, i, c * P:(c + 1) * P],
                                  start=(i == 0), stop=(i == C - 1))
                last.then_inc(kv_mm, 1)

            def pass1(b, last):
                for g in range(G):
                    n = b * G + g
                    later_batch = g == 0 and not (isinstance(b, int) and b == 0)
                    k_product(n, g)
                    if later_batch:
                        g_transposes(b - 1)
                    q_product(n, g, b - 1 if later_batch else None)
                    if not (last and g == G - 1):
                        t1(n + 1, g + 1)
                    if g == 0 and later_batch:
                        pe.wait_ge(kv_done, 2 * C * b)
                    elif g == 0:
                        pe.wait_ge(flag_ready, 1)
                    g_product(n, g)

            pass1(0, False)
            with pe.Fori(1, B - 1) as b:
                pass1(b, False)
            pass1(B - 1, True)

            pe.wait_ge(flag_ready, 1)
            routed = pe.value_load(routed_flag[0:1, 0:1], min_val=0, max_val=1)

            def run_experts(k, p, tiles, xt, y, h, free):
                with pe.If(routed > 0):
                    for s, v in free:
                        ge(pe, s, v)
                    for t in range(tiles):
                        for c in range(C):
                            last = mm(PT[0:p, 0, t * NE:(t + 1) * NE], xt[:, c, t * P:t * P + p], wr[:, c, :],
                                      start=(c == 0), stop=(c == C - 1))
                    last.then_inc(r_logits, 1)
                    with pe.Fori(0, NE) as e:
                        pe.wait_ge(r_w, 32 * (k * NE + e + 1))
                        for c in range(C):
                            last = mm(PT[:, 1, 0:tiles * p], w1e[:, c, :], xt[:, c, :], start=(c == 0), stop=(c == C - 1))
                        last.then_inc(r_hid, 1)
                        pe.wait_ge(r_sq, k * NE + e + 1)
                        for t in range(tiles):
                            last = mm(y[0:p, t, :], h[:, t * P:t * P + p], w2e[:, :], start=True, stop=True)
                        last.then_inc(r_y, 1)
                    pe.wait_ge(r_turn, (k + 1) * (NE + 1))

            pe.wait_ge(setup_dve, 5)
            pe.wait_ge(q_relu, C * NG)
            pe.wait_ge(k_done, NG)

            def transposes(dst, src, done):
                for c in range(C):
                    for t in range(T):
                        last = nc.tensor.transpose(dst[:, c, t * P:(t + 1) * P], src[:, t, c * P:(c + 1) * P], ident[:, :])
                    last.then_inc(done, 1)

            def hidden(dst, xt, done, copied, before, each):
                for c in range(C):
                    if c == 0 or each:
                        pe.wait_ge(copied, before + c + 1)
                    last = mm(dst, ws1[:, c, :], xt[:, c, :], start=(c == 0), stop=(c == C - 1))
                last.then_inc(done, 1)

            def down(pair, h, done):
                for t in range(T):
                    last = mm(four(pair)[:, t, :], h[:, t * P:(t + 1) * P], ws2[:, :], start=True, stop=True)
                last.then_inc(done, 1)

            def step(g, b):
                i, r, u, v = (lagged(g, b, back)[0] for back in range(4))
                if runs(i):
                    pe.wait_ge(q_copied, i + 1)
                    ge(pe, f1_relu, i - 1)
                    ge(pe, t3_done, i - 2)
                    for k in (0, 1, 2, 6, 7, 3, 4, 5):
                        t, c = k // C, k % C
                        if k == 3:
                            ge(pe, f3_relu, i - 2)
                        dst = PA[:, k // 3, (k % 3) * KVW:(k % 3 + 1) * KVW] if k < 6 else PT[:, 0, (k - 6) * KVW:(k - 5) * KVW]
                        last = mm(dst, q_cur[b % 2][:, c, t * P:(t + 1) * P], kv_all[:, b * C + c, :], start=True, stop=True)
                    last.then_inc(o_mm, 1)
                if isinstance(i, int) and i == 0:
                    g_transposes(B - 1)
                    kv_product(B - 1)
                if runs(v):
                    pe.wait_ge(f3_sq, v + 1)
                    ge(pe, w_added, min(i, NG) if isinstance(i, int) else i)
                    down(PB, h3, f4_mm)
                    run_experts(routed_ordinal(g, b, 0), P, T, x3t, four(PB), h3,
                                [(f4_added, v + 1), (t3_done, v + 1)] + ([(o_done, 3 * (i + 1))] if runs(i) else []))
                if runs(r):
                    pe.wait_ge(norm2, T * (r + 1))
                    ge(pe, t3_done, i - 2)
                    if runs(i):
                        pe.wait_ge(o_done, 3 * i + 1)
                    transposes(PT, y2, t2_mm)
                if runs(i):
                    pe.wait_ge(o_done, 3 * (i + 1))
                    ge(pe, f2_added, i - 1)
                    attention_b_has_read(g, b, "y")
                    for c in range(C):
                        for t in range(T):
                            last = nc.tensor.transpose(turned_o(i)[:, c, t * P:(t + 1) * P], o_tok[:, t * C + c, :], ident[:, :])
                        last.then_inc(ot_mm, 1)
                if runs(r):
                    hidden(PA[:, 0, :], x2t, f1_mm, t2_done, C * r, 1)
                attention_b(g, b, "x")
                if runs(i):
                    pe.wait_ge(o_hi_done, C * (i + 1))
                    ge(pe, f4_added, i - 2)
                    for tiles in ((0, 2), (1, 3)):
                        for t in tiles:
                            for c in range(C):
                                hi = o_hi[:, c, t * P:(t + 1) * P]
                                mm(four(PB)[:, t, :], hi, wo_hi[:, c, :], start=(c == 0), stop=False)
                                mm(four(PB)[:, t, :], hi, wo_lo[:, c, :], start=False, stop=False)
                        for c in range(C):
                            if 0 in tiles:
                                pe.wait_ge(o_lo_done, C * i + c + 1)
                            for t in tiles:
                                last = mm(four(PB)[:, t, :], o_lo[:, c, t * P:(t + 1) * P], wo_hi[:, c, :], start=False, stop=(c == C - 1))
                    last.then_inc(w_mm, 1)
                if runs(u):
                    pe.wait_ge(norm3, T * (u + 1))
                    if runs(r):
                        pe.wait_ge(t2_done, C * (r + 1))
                    transposes(PT, y3, t3_mm)
                if runs(r):
                    pe.wait_ge(f1_sq, r + 1)
                    ge(pe, f2_added, r)
                    down(PG, h2, f2_mm)
                    run_experts(routed_ordinal(g, b, 1), P, T, x2t, four(PG), h2,
                                [(f2_added, r + 1)] + ([(t3_done, u + 1)] if runs(u) else [(t2_done, C * (r + 1))]))
                if runs(u):
                    attention_b_has_read(g, b, "x")
                    hidden(PA[:, 1, :], x3t, f3_mm, t3_done, u, 0)
                attention_b(g, b, "y")

            def special_transposes(dst, src):
                for c in range(C):
                    last = nc.tensor.transpose(dst[:, c * SP:(c + 1) * SP], src[:, c * P:(c + 1) * P], ident[0:SP, 0:SP])
                return last

            def weight_transposes(pair, first):
                pe.wait_ge(c_wts, 16 * 4)
                for w in range(2):
                    for c in range(C):
                        for o in range(C):
                            last = nc.tensor.transpose(pair[:, w, c * D + o * P:c * D + (o + 1) * P],
                                                       raw4[first + w][:, o, c * P:(c + 1) * P], ident[:, :])
                last.then_inc(c_wt, 1)

            def prepare(i, place):
                if (i, place) == (0, "y"):
                    pe.wait_ge(o_lo_done, C)
                    weight_transposes(PT, 0)
                    pe.wait_ge(kv_done, 2 * C * B)
                    weight_transposes(PG, 2)
                    pe.wait_ge(c_wt_sb, 1)
                elif (i, place) == (5, "y"):
                    pe.wait_ge(c_blk, 3)
                    for k in range(3):
                        last = nc.tensor.transpose(PG[:, 1, k * P:(k + 1) * P], l_blk[k], ident[:, :])
                    last.then_inc(c_lt, 1)
                    pe.wait_ge(c_z, 2)
                    special_transposes(PG[:, 0, 0:C * SP], za)
                    special_transposes(PG[:, 0, C * SP:2 * C * SP], zb).then_inc(c_zt, 1)
                elif (i, place) == (6, "x"):
                    pe.wait_ge(c_wt_sb, 2)
                    pe.wait_ge(c_zt_sb, 2)
                    for w, zt in enumerate((za_t, zb_t, zb_t)):
                        for o in range(C):
                            for c in range(C):
                                last = mm(PA[:, 1, (w * C + o) * SP:(w * C + o + 1) * SP], w4t[w][:, c, o * P:(o + 1) * P], zt[:, c, :],
                                          start=(c == 0), stop=(c == C - 1))
                    last.then_inc(c_qkv, 1)
                elif (i, place) == (6, "y"):
                    pe.wait_ge(c_lt_sb, 1)
                    pe.wait_ge(c_kv_sb, 2 * C)
                    for k, src, bd in ((0, k_t, l_bdt[1]), (1, v_t, l_bdt[2])):
                        for c in range(C):
                            last = mm(PG[0:SP, k, c * P:(c + 1) * P], src[:, c, :], bd, start=True, stop=True)
                    last.then_inc(c_klin, 1)

            def wait(s, v):
                ge_apart(pe, "pe", s, v)

            def attention_b(g, b, place):
                it = iteration(g)
                last_one = isinstance(g, int)
                i = g * B + b
                if it is None and i in (1, 2, 3, 4):
                    return
                if place == "before x":
                    return
                if place == "x":
                    wait(f3_relu, min(i - 2, NG) if isinstance(i, int) else i - 2)
                else:
                    wait(f2_added, min(i, NG) if isinstance(i, int) else i)
                if it is None:
                    prepare(i, place)
                    return
                for name in parts(g, b, place):
                    iterate(name, it, last_one)

            def iterate(name, it, last_one):
                if name == "q":
                    wait(c_q_sb, it + 1)
                    for c in range(C):
                        last = mm(PA[0:SP, 1, c * P:(c + 1) * P], qcur_t[:, c, :], l_bdt[0], start=True, stop=True)
                    last.then_inc(c_qlin, 1)
                    if last_one:
                        pe.wait_ge(c_dsum, ITERS - 1)
                        mm(PA[0:SP, 1, D:D + 1], ones_f[0:SP, 0:SP], dsum[0:SP, 0:1], start=True, stop=True).then_inc(c_diff, 1)
                elif name == "keys":
                    pe.wait_ge(c_kn, 1)
                    special_transposes(PG[:, 0, 0:C * SP], kn).then_inc(c_knt, 1)
                elif name == "turn q":
                    wait(c_qn, it + 1)
                    special_transposes(PA[:, 1, 0:C * SP], qn).then_inc(c_qnt, 1)
                elif name == "logits":
                    wait(c_qnt_sb, it + 1)
                    if last_one:
                        pe.wait_ge(f2_added, NG)
                    for c in range(C):
                        last = mm(PG[0:SP, c, :], qn_t[:, c, :], kn_mask[c], start=True, stop=True)
                    last.then_inc(c_logit, 1)
                elif name == "probs":
                    wait(c_pr, it + 1)
                    for h in range(H):
                        last = nc.tensor.transpose(PG[0:SP, h // HC, (h % HC) * SP:(h % HC + 1) * SP], pr[:, h * SP:(h + 1) * SP],
                                                   ident[0:SP, 0:SP])
                    last.then_inc(c_prt, 1)
                elif name == "out":
                    wait(c_prt_sb, it + 1)
                    for h in range(H):
                        last = mm(PA[0:SP, 1, h * HD:(h + 1) * HD], pr_t[:, h * SP:(h + 1) * SP], vi[:, h * HD:(h + 1) * HD],
                                  start=True, stop=True)
                    last.then_inc(c_pv, 1)
                elif name == "next q":
                    wait(c_outs, it + 1)
                    special_transposes(PG[:, 0, 0:C * SP], out_cur).then_inc(c_outt, 1)

            def attention_b_has_read(g, b, place):
                it = iteration(g)
                if it is None:
                    read = {(1, "y"): (c_wt_sb, 2), (6, "y"): (c_zt_sb, 2), (6, "x"): (c_q_sb, 1), (7, "y"): (c_klin_read, 2)}
                    if (g * B + b, place) not in read:
                        return
                    s, v = read[g * B + b, place]
                elif place == "x":
                    s, v = ((c_lin, it + 1), (c_qnt_sb, it + 1), (c_qnt_sb, it + 1), (c_outs, it + 1))[b]
                else:
                    s, v = ((c_q_sb, it + 1), (c_kmask, C * (it + 1)), (c_scaled, it + 1), (c_prt_sb, it + 1))[b]
                pe.wait_ge(s, v)

            for g in range(2):
                for b in range(B):
                    step(g, b)
            with pe.Fori(2, G) as g:
                for b in range(B):
                    step(g, b)
            for b in range(3):
                step(G, b)

            pe.wait_ge(f4_added, NG)
            pe.wait_ge(c_att, 1)
            special_transposes(PT[:, 1, 0:C * SP], att).then_inc(c_att_t, 1)
            pe.wait_ge(c_att_t_sb, 1)
            for i in range(C):
                last = mm(PB[0:SP, 0, 0:D], att_t[:, i, :], w4t[3][:, i, :], start=(i == 0), stop=(i == C - 1))
            last.then_inc(c_proj, 1)
            pe.wait_ge(c_z, 3)
            special_transposes(PT[:, 0, 0:C * SP], zs).then_inc(c_zt, 1)
            pe.wait_ge(c_zt_sb, 3)
            for c in range(C):
                last = mm(PA[:, 1, 0:SP], ws1[:, c, :], xs_t[:, c, :], start=(c == 0), stop=(c == C - 1))
            last.then_inc(c_hid, 1)
            pe.wait_ge(c_sq, 1)
            mm(PB[0:SP, 1, 0:D], h_s, ws2[:, :], start=True, stop=True).then_inc(c_ffn, 1)
            run_experts(2 * NG, SP, 1, xs_t, four(PB)[:, 2:3, :], h_s, [])


_NAMES = ["inputs_q", "Wq", "bq", "Wk", "bk", "Wv", "bv", "Wo", "bo"]
_NAMES_B = ["qw", "qb", "kw", "vw", "vb", "ow", "ob", "lna_w", "lnb_w", "lnc_w", "lnd_w", "lqw", "lqb", "lkw", "lkb", "lvw", "lvb"]
_NAMES_F = ["Ws1", "Ws2", "W1", "W2", "Wr"]
_INS = [f"L0_attn_a_{n}" for n in _NAMES] + [f"L0_attn_b_{n}" for n in _NAMES_B] + [f"L0_ffn_{n}" for n in _NAMES_F]


def kernel(**inputs):
    import numpy as _np
    import concourse.bacc as _bacc
    from concourse import mybir as _mybir
    from concourse.bass_utils import run_bass_kernel_spmd as _run

    nc = _bacc.Bacc("TRN2", target_bir_lowering=False, num_devices=1)
    arrays, args = {}, []
    for name in _INS:
        a = _np.ascontiguousarray(inputs[name])
        arrays[f"in_{name}_dram"] = a
        args.append(nc.dram_tensor(f"in_{name}_dram", a.shape, _mybir.dt.from_np(a.dtype), kind="ExternalInput").ap())
    args.append(nc.dram_tensor("out_0_dram", (B, S, D), _mybir.dt.float32, kind="ExternalOutput").ap())
    hybrid_kernel(nc, *args)
    r = _run(nc, [arrays], core_ids=[0])
    return r.results[0]["out_0_dram"]
```
